# Optimizing a Trainium2 kernel written in Bass

```python
import numpy as np
import jax
import jax.numpy as jnp

def _softmax(x, axis=-1):
    return jax.nn.softmax(x, axis=axis)

def _gelu(x):
    return jax.nn.gelu(x, approximate=True)

def _silu(x):
    return jax.nn.silu(x)

def _sigmoid(x):
    return jax.nn.sigmoid(x)

def _layernorm(x, axis=-1, eps=1e-05):
    m = jnp.mean(x, axis=axis, keepdims=True)
    v = jnp.var(x, axis=axis, keepdims=True)
    return (x - m) / jnp.sqrt(v + eps)

def _scatter_add(tgt, idx, src, axis=0):
    return tgt.at[idx].add(src)

def _segment_sum(src, seg, n):
    return jax.ops.segment_sum(src, seg, n)
kernel_name = 'mk_vit_tower_cls_d1_tok_img768_r4_c7cd54'

def setup_inputs(seed: int=0):
    np.random.seed(seed)
    _w = jnp.asarray

    def _rec_inputs():
        import jax
        import jax.numpy as jnp
        _rk = jax.random.key(seed)
        x = -0.00016672 + 0.999947 * jax.random.normal(jax.random.fold_in(_rk, 1), (64, 3, 96, 96), jnp.float32)
        cls_tok = 0.02 * jax.random.normal(jax.random.fold_in(_rk, 5), (1, 1, 192), jnp.float32)
        return (x, cls_tok)
    x, cls_tok = _rec_inputs()

    def _L0_tok_setup():
        import jax, jax.numpy as jnp
        import numpy as np
        PATCH = 16

        def _patchify(x):
            B, C, H, Wd = x.shape
            p = PATCH
            Hp, Wp = (H // p, Wd // p)
            x = x.reshape(B, C, Hp, p, Wp, p)
            x = x.transpose(0, 2, 4, 1, 3, 5)
            return x.reshape(B, Hp * Wp, C * p * p)
        key = jax.random.key(seed)
        k1, k2, k3, k4 = jax.random.split(key, 4)
        B, C, H, W_ = (64, 3, 96, 96)
        embed_dim = 192
        patch_dim = C * PATCH * PATCH
        num_patches = H // PATCH * (W_ // PATCH)
        x = jax.random.normal(k1, (B, C, H, W_), dtype=jnp.float32)
        W = jax.random.normal(k2, (embed_dim, patch_dim), dtype=jnp.float32) * (1.0 / np.sqrt(patch_dim))
        b = jax.random.normal(k3, (embed_dim,), dtype=jnp.float32) * 0.01
        pos_embed = jax.random.normal(k4, (1, num_patches, embed_dim), dtype=jnp.float32)
        return {'x': x, 'W': W, 'b': b, 'pos_embed': pos_embed}
    _L0_tok_all = _L0_tok_setup()
    _L0_tok_in = {k: v for k, v in _L0_tok_all.items() if k in ('W', 'b', 'pos_embed')}
    del _L0_tok_all

    def _L0_attn_setup():
        import jax, jax.numpy as jnp
        import numpy as np
        MAX_DIST = 100

        def _pos_bias(rel_emb, length):
            emb_sum = rel_emb[..., 0].sum(axis=-1)
            pos = jnp.arange(length)
            rel = pos[None, :] - pos[:, None]
            idx = jnp.clip(rel, -(MAX_DIST - 1), MAX_DIST - 1) + MAX_DIST - 1
            return emb_sum[:, idx]
        key = jax.random.key(seed)
        ks = jax.random.split(key, 6)
        b, s, e, h, d = (4, 512, 192, 8, 96)
        return {'x': jax.random.normal(ks[0], (b, s, e), dtype=jnp.float32), 'w_q': jax.random.normal(ks[1], (h, e, d), dtype=jnp.float32) * 0.02, 'w_k': jax.random.normal(ks[2], (h, e, d), dtype=jnp.float32) * 0.02, 'w_v': jax.random.normal(ks[3], (h, e, d), dtype=jnp.float32) * 0.02, 'w_o': jax.random.normal(ks[4], (h, d, e), dtype=jnp.float32) * 0.02, 'rel_emb': jax.random.normal(ks[5], (h, 2 * MAX_DIST - 1, d, 1), dtype=jnp.float32) * 0.02}
    _L0_attn_all = _L0_attn_setup()
    _L0_attn_in = {k: v for k, v in _L0_attn_all.items() if k in ('w_q', 'w_k', 'w_v', 'w_o', 'rel_emb')}
    del _L0_attn_all

    def _L0_ffn_setup():
        import jax, jax.numpy as jnp
        import numpy as np
        B, L, D, H, F = (4, 512, 192, 12, 768)
        ROUTE_FRAC = 0.15
        LN_EPS = 1e-05

        def _ln(x, g, b):
            m = jnp.mean(x, axis=-1, keepdims=True)
            v = jnp.mean((x - m) ** 2, axis=-1, keepdims=True)
            return (x - m) * jax.lax.rsqrt(v + LN_EPS) * g + b
        key = jax.random.key(seed)
        ks = jax.random.split(key, 20)
        s = 0.02
        return {'hidden_states': jax.random.normal(ks[0], (B, L, D), dtype=jnp.float32), 'g1': jnp.ones((D,), jnp.float32), 'b1': jnp.zeros((D,), jnp.float32), 'g2': jnp.ones((D,), jnp.float32), 'b2': jnp.zeros((D,), jnp.float32), 'Wr': jax.random.normal(ks[1], (D,), jnp.float32) * s, 'br': jnp.zeros((), jnp.float32), 'Wq': jax.random.normal(ks[2], (D, D), jnp.float32) * s, 'bq': jnp.zeros((D,), jnp.float32), 'Wk': jax.random.normal(ks[3], (D, D), jnp.float32) * s, 'bk': jnp.zeros((D,), jnp.float32), 'Wv': jax.random.normal(ks[4], (D, D), jnp.float32) * s, 'bv': jnp.zeros((D,), jnp.float32), 'Wo': jax.random.normal(ks[5], (D, D), jnp.float32) * s, 'bo': jnp.zeros((D,), jnp.float32), 'Wm': jax.random.normal(ks[6], (D, D), jnp.float32) * s, 'bm': jnp.zeros((D,), jnp.float32), 'W1': jax.random.normal(ks[7], (D, F), jnp.float32) * s, 'bf1': jnp.zeros((F,), jnp.float32), 'W2': jax.random.normal(ks[8], (F, D), jnp.float32) * s, 'bf2': jnp.zeros((D,), jnp.float32)}
    _L0_ffn_all = _L0_ffn_setup()
    _L0_ffn_in = {k: v for k, v in _L0_ffn_all.items() if k in ('g1', 'b1', 'g2', 'b2', 'Wr', 'br', 'Wq', 'bq', 'Wk', 'bk', 'Wv', 'bv', 'Wo', 'bo', 'Wm', 'bm', 'W1', 'bf1', 'W2', 'bf2')}
    del _L0_ffn_all
    return {'x': x, 'cls_tok': cls_tok, 'L0_tok_W': _L0_tok_in['W'], 'L0_tok_b': _L0_tok_in['b'], 'L0_tok_pos_embed': _L0_tok_in['pos_embed'], 'L0_attn_w_q': _L0_attn_in['w_q'], 'L0_attn_w_k': _L0_attn_in['w_k'], 'L0_attn_w_v': _L0_attn_in['w_v'], 'L0_attn_w_o': _L0_attn_in['w_o'], 'L0_attn_rel_emb': _L0_attn_in['rel_emb'], 'L0_ffn_g1': _L0_ffn_in['g1'], 'L0_ffn_b1': _L0_ffn_in['b1'], 'L0_ffn_g2': _L0_ffn_in['g2'], 'L0_ffn_b2': _L0_ffn_in['b2'], 'L0_ffn_Wr': _L0_ffn_in['Wr'], 'L0_ffn_br': _L0_ffn_in['br'], 'L0_ffn_Wq': _L0_ffn_in['Wq'], 'L0_ffn_bq': _L0_ffn_in['bq'], 'L0_ffn_Wk': _L0_ffn_in['Wk'], 'L0_ffn_bk': _L0_ffn_in['bk'], 'L0_ffn_Wv': _L0_ffn_in['Wv'], 'L0_ffn_bv': _L0_ffn_in['bv'], 'L0_ffn_Wo': _L0_ffn_in['Wo'], 'L0_ffn_bo': _L0_ffn_in['bo'], 'L0_ffn_Wm': _L0_ffn_in['Wm'], 'L0_ffn_bm': _L0_ffn_in['bm'], 'L0_ffn_W1': _L0_ffn_in['W1'], 'L0_ffn_bf1': _L0_ffn_in['bf1'], 'L0_ffn_W2': _L0_ffn_in['W2'], 'L0_ffn_bf2': _L0_ffn_in['bf2']}

def reference(x, cls_tok, L0_tok_W, L0_tok_b, L0_tok_pos_embed, L0_attn_w_q, L0_attn_w_k, L0_attn_w_v, L0_attn_w_o, L0_attn_rel_emb, L0_ffn_g1, L0_ffn_b1, L0_ffn_g2, L0_ffn_b2, L0_ffn_Wr, L0_ffn_br, L0_ffn_Wq, L0_ffn_bq, L0_ffn_Wk, L0_ffn_bk, L0_ffn_Wv, L0_ffn_bv, L0_ffn_Wo, L0_ffn_bo, L0_ffn_Wm, L0_ffn_bm, L0_ffn_W1, L0_ffn_bf1, L0_ffn_W2, L0_ffn_bf2):
    import jax
    import jax.numpy as jnp

    def _L0_tok_ref(x, W, b, pos_embed):
        import jax, jax.numpy as jnp
        import numpy as np
        PATCH = 16

        def _patchify(x):
            B, C, H, Wd = x.shape
            p = PATCH
            Hp, Wp = (H // p, Wd // p)
            x = x.reshape(B, C, Hp, p, Wp, p)
            x = x.transpose(0, 2, 4, 1, 3, 5)
            return x.reshape(B, Hp * Wp, C * p * p)
        patches = _patchify(x)
        tokens = jnp.einsum('bnd,ed->bne', patches, W) + b
        return tokens + pos_embed

    def _L0_attn_ref(x, w_q, w_k, w_v, w_o, rel_emb):
        import jax, jax.numpy as jnp
        import numpy as np
        MAX_DIST = 100

        def _pos_bias(rel_emb, length):
            emb_sum = rel_emb[..., 0].sum(axis=-1)
            pos = jnp.arange(length)
            rel = pos[None, :] - pos[:, None]
            idx = jnp.clip(rel, -(MAX_DIST - 1), MAX_DIST - 1) + MAX_DIST - 1
            return emb_sum[:, idx]
        b, s, e = x.shape
        d = w_q.shape[-1]
        q = jnp.einsum('bse,hed->bhsd', x, w_q)
        k = jnp.einsum('bse,hed->bhsd', x, w_k)
        v = jnp.einsum('bse,hed->bhsd', x, w_v)
        scale = d ** (-0.5)
        logits = jnp.einsum('bhqd,bhkd->bhqk', q, k) * scale
        logits = logits + _pos_bias(rel_emb, s)[None]
        attn = jax.nn.softmax(logits, axis=-1)
        ctx = jnp.einsum('bhqk,bhkd->bhqd', attn, v)
        return jnp.einsum('bhsd,hde->bse', ctx, w_o)

    def _L0_ffn_ref(hidden_states, g1, b1, g2, b2, Wr, br, Wq, bq, Wk, bk, Wv, bv, Wo, bo, Wm, bm, W1, bf1, W2, bf2):
        import jax, jax.numpy as jnp
        import numpy as np
        B, L, D, H, F = (4, 512, 192, 12, 768)
        ROUTE_FRAC = 0.15
        LN_EPS = 1e-05

        def _ln(x, g, b):
            m = jnp.mean(x, axis=-1, keepdims=True)
            v = jnp.mean((x - m) ** 2, axis=-1, keepdims=True)
            return (x - m) * jax.lax.rsqrt(v + LN_EPS) * g + b
        b, l, d = hidden_states.shape
        dh = d // H
        normed = _ln(hidden_states, g1, b1)
        scores = jax.nn.sigmoid(jnp.einsum('bld,d->bl', normed, Wr) + br)
        k = max(1, int(round(ROUTE_FRAC * l)))
        _, idx = jax.lax.top_k(-scores, k)
        attn_mask = jnp.zeros((b, l), bool).at[jnp.arange(b)[:, None], idx].set(True)
        q = (normed @ Wq + bq).reshape(b, l, H, dh)
        kk = (normed @ Wk + bk).reshape(b, l, H, dh)
        v = (normed @ Wv + bv).reshape(b, l, H, dh)
        logits = jnp.einsum('blhd,bmhd->bhlm', q, kk) / jnp.sqrt(jnp.float32(dh))
        probs = jax.nn.softmax(logits, axis=-1)
        ctx = jnp.einsum('bhlm,bmhd->blhd', probs, v).reshape(b, l, d)
        attn_out = ctx @ Wo + bo
        w = scores / (jnp.sum(scores, axis=1, keepdims=True) + 1e-06)
        pooled = jnp.einsum('bl,bld->bd', w, normed)
        mix_out = (normed + scores[..., None] * pooled[:, None, :]) @ Wm + bm
        merged = jnp.where(attn_mask[..., None], attn_out, mix_out)
        h = hidden_states + merged
        n2 = _ln(h, g2, b2)
        ffn = jax.nn.gelu(n2 @ W1 + bf1, approximate=False) @ W2 + bf2
        return h + ffn
    h = _L0_tok_ref(x, L0_tok_W, L0_tok_b, L0_tok_pos_embed)
    h = jnp.concatenate([jnp.broadcast_to(cls_tok, (h.shape[0], 1, h.shape[2])), h], axis=1)
    h = h + _L0_attn_ref(_layernorm(h, axis=-1), L0_attn_w_q, L0_attn_w_k, L0_attn_w_v, L0_attn_w_o, L0_attn_rel_emb)
    h = h + _L0_ffn_ref(_layernorm(h, axis=-1), L0_ffn_g1, L0_ffn_b1, L0_ffn_g2, L0_ffn_b2, L0_ffn_Wr, L0_ffn_br, L0_ffn_Wq, L0_ffn_bq, L0_ffn_Wk, L0_ffn_bk, L0_ffn_Wv, L0_ffn_bv, L0_ffn_Wo, L0_ffn_bo, L0_ffn_Wm, L0_ffn_bm, L0_ffn_W1, L0_ffn_bf1, L0_ffn_W2, L0_ffn_bf2)
    return h

_drawn_inputs = setup_inputs


def setup_inputs(seed=0):
    import zlib

    import numpy as np

    out = dict(_drawn_inputs(seed))
    spreads = {'L0_ffn_g1': (1.0, 0.2),
     'L0_ffn_b1': (0.0, 0.503),
     'L0_ffn_g2': (1.0, 0.6),
     'L0_ffn_b2': (0.0, 2.0),
     'L0_ffn_bq': (0.0, 0.8),
     'L0_ffn_bk': (0.0, 2.0),
     'L0_ffn_bv': (0.0, 0.8),
     'L0_ffn_bo': (0.0, 0.459),
     'L0_ffn_bm': (0.0, 0.294),
     'L0_ffn_bf1': (0.0, 0.612),
     'L0_ffn_bf2': (0.0, 0.1)}
    factors = {'L0_tok_b': 7.408,
     'L0_attn_w_q': 8.0,
     'L0_attn_w_k': 8.0,
     'L0_attn_rel_emb': 4.534,
     'L0_ffn_Wq': 8.0,
     'L0_ffn_Wk': 8.0,
     'L0_ffn_Wv': 8.0,
     'L0_ffn_Wo': 8.0}
    for name, (base, spread) in spreads.items():
        noise = np.random.default_rng([zlib.crc32(name.encode()), seed]).standard_normal(out[name].shape)
        drawn = base * np.exp(spread * noise) if base else spread * noise
        out[name] = jnp.asarray(drawn.astype(out[name].dtype))
    for name, factor in factors.items():
        out[name] = (out[name] * factor).astype(out[name].dtype)
    return out
```

```python
from contextlib import ExitStack

import concourse.bass as bass
from concourse import mybir

F32 = mybir.dt.float32
ALU = mybir.AluOpType
ACT = mybir.ActivationFunctionType
AX_X = mybir.AxisListType.X

BATCH, CHANNELS, SIDE, PATCH = 64, 3, 96, 16
HP = SIDE // PATCH
NP = HP * HP
TOK = NP + 1
E = 192
EC = E // 2
GB = 3
GT = GB * TOK
G = 2
RB = G * GB
RT = G * GT
RUNS = -(-BATCH // RB)
LAST_B = BATCH - (RUNS - 1) * RB
PD = CHANNELS * PATCH * PATCH
PC = PD // 128
H1, D1 = 8, 96
QUAD = 4
UNITS = (H1 // QUAD) * G
H2, D2 = 12, 16
HC = EC // D2
SEL = 6
GS = GB * SEL
RS = G * GS
FF = 768
FC = FF // 128
MAX_DIST = 100
REL = 2 * TOK - 1
EPS = 1e-5
NEG = -1e30
XP = CHANNELS * RB * HP
TW = HP // 2

CONST = {}
_at = 0
for _name, _n in (("ident", 128), ("same", GT), ("lower", GT), ("apart", GB), ("slot", GS),
                  ("headmask", HC), ("apart2", GT), ("shift", REL)):
    CONST[_name] = (_at, _at + _n)
    _at += _n
CONST_COLS = _at


class Signal:

    def __init__(self, sem, per_run, early):
        self.sem, self.per_run, self.early = sem, per_run, early

    def at(self, run, k=None):
        return (run + self.early) * self.per_run + (self.per_run if k is None else k)

    def before(self, run):
        assert self.early
        return run * self.per_run + self.per_run


def vit_block(nc, a):
    with ExitStack() as ctx:
        def sb(name, shape):
            return ctx.enter_context(nc.sbuf_tensor(name, shape, F32))

        def bank(name):
            return ctx.enter_context(nc.psum_tensor(name, [128, 512], F32))

        def sem(name):
            return ctx.enter_context(nc.semaphore(name))

        def signal(name, per_run=1, early=0):
            return Signal(sem(name), per_run, early)

        const = sb("const", [128, CONST_COLS])

        def cst(name, p=128):
            lo, hi = CONST[name]
            return const[0:p, lo:hi]

        ident = cst("ident")
        w_raw = sb("w_raw", [EC, 2, PD])
        w_tok = sb("w_tok", [128, PC, E])
        pos_tok = sb("pos_tok", [GT, E])
        b_tok = sb("b_tok", [GT, E])
        w_q = sb("w_q", [EC, 2, H1, D1])
        w_k = sb("w_k", [EC, 2, H1, D1])
        w_v = sb("w_v", [EC, 2, H1 * D1])
        w_o = sb("w_o", [128, FC, E])
        rel = sb("rel", [REL, H1, D1])
        place = sb("place", [REL, TOK, GT])
        rel_sum = sb("rel_sum", [REL, H1])
        pos_bias = sb("pos_bias", [GT, H1, GT])
        cols = sb("cols", [EC, 8, 2])
        g1, b1, g2, b2, bq, bk, bv, wr = (cols[:, n, :] for n in range(8))
        vec_rows = sb("vec_rows", [8, E])
        b_ff1_rows = sb("b_ff1_rows", [FC, 128])
        wr_all = sb("wr_all", [EC, 2, GT])
        br_neg = sb("br_neg", [GT, 1])
        b_ff1 = sb("b_ff1", [128, FC])
        b_ff2 = sb("b_ff2", [GT, E])
        w_q2 = sb("w_q2", [EC, 2, E])
        w_k2 = sb("w_k2", [EC, 2, E])
        w_v2 = sb("w_v2", [EC, 2, E])
        w_o2 = sb("w_o2", [EC + 1, 2, E])
        w_m = sb("w_m", [EC + 1, 2, E])
        w_ff1 = sb("w_ff1", [EC, 2, FF])
        w_ff2 = sb("w_ff2", [128, FC, E])
        power = sb("power", [GT, G])
        eps = sb("eps", [GT, G])

        x_rows = sb("x_rows", [XP, PATCH, HP, PATCH])
        x_split = sb("x_split", [XP, HP, PATCH * PATCH])
        x_t = sb("x_t", [128, PC, RT])
        h = sb("h", [GT, G, E])
        stats1 = sb("stats1", [GT, G, 6])
        mv1 = sb("mv1", [GT, G, 2])
        ve1 = sb("ve1", [GT, G])
        rstd1 = sb("rstd1", [GT, G])
        n1 = sb("n1", [GT, G, E])
        n1_t = sb("n1_t", [EC, 2, RT])
        qk = sb("qk", [D1, H1, 2, RT])
        v = sb("v", [GT, G, H1, D1 + 1])
        logits = sb("logits", [GT, 2, QUAD, GT])
        rowmax = sb("rowmax", [GT, 2, QUAD])
        shifted = sb("shifted", [GT, 2, QUAD, GT])
        probs = sb("probs", [GT, 2, QUAD, GT])
        probs_t = sb("probs_t", [GT, 2, QUAD, GT])
        den_inv = sb("den_inv", [GT, UNITS, QUAD])
        ctx1 = sb("ctx1", [GT, G, H1, D1])
        ctx1_t = sb("ctx1_t", [128, FC, RT])
        h2 = sb("h2", [GT, G, E])

        stats2 = sb("stats2", [GT, G, 6])
        mv2 = sb("mv2", [GT, G, 2])
        tmp2 = sb("tmp2", [GT, 3, G])
        rstd2 = sb("rstd2", [GT, G])
        rstd22 = sb("rstd22", [GT, G])
        n2 = sb("n2", [GT, G, E])
        nn2 = sb("nn2", [GT, G, E])
        n2_t = sb("n2_t", [EC, 2, RT])
        score_e = sb("score_e", [GT, RT])
        score_d = sb("score_d", [GT, RT])
        score = sb("score", [GT, RT])
        junk = sb("junk", [GT, 4, GT])
        score_col = sb("score_col", [GT, G])
        less = sb("less", [GT, G, GT])
        tied = sb("tied", [GT, G, GT])
        rank = sb("rank", [GT, G])
        sel = sb("sel", [GT, G, RS])
        sel_t = sb("sel_t", [RS, G, GT])
        unrouted = sb("unrouted", [GT, G])
        s_sum = sb("s_sum", [EC, RB])
        s_eps = sb("s_eps", [EC, RB])
        s_inv = sb("s_inv", [EC, RB])
        weighted = sb("weighted", [EC, 2, RT])
        pooled = sb("pooled", [EC, 2, RB])
        pooled_n = sb("pooled_n", [EC, 2, RB])
        spread = sb("spread", [EC, 2, RT])
        mix_t = sb("mix_t", [EC + 1, 2, RT])
        k2_t = sb("k2_t", [EC, 2, RT])
        v2 = sb("v2", [GT, G, E])
        nsel_t = sb("nsel_t", [EC, 2, RS])
        q2_t = sb("q2_t", [EC, 2, RS])
        q2_heads = sb("q2_heads", [EC, 2, G, HC, GS])
        logits2 = sb("logits2", [HC * GS, 4, GT])
        negmax2 = sb("negmax2", [HC * GS, 4])
        exp2 = sb("exp2", [HC * GS, 4, GT])
        den2 = sb("den2", [HC * GS, 4])
        den2_inv = sb("den2_inv", [HC * GS, 4])
        probs2 = sb("probs2", [HC * GS, 4, GT])
        probs2_t = sb("probs2_t", [GT, 4, HC * GS])
        own = sb("own", [EC, 4, HC, GS])
        ctx2 = sb("ctx2", [EC, 4, GS])
        ctx2_t = sb("ctx2_t", [EC + 1, 2, RS])
        attn2 = sb("attn2", [RS, E])
        mixed = sb("mixed", [GT, G, E])
        h3 = sb("h3", [GT, G, E])
        h2_b = sb("h2_b", [GT, G, E])
        h3_b = sb("h3_b", [GT, G, E])
        stats3 = sb("stats3", [GT, G, 6])
        mv3 = sb("mv3", [GT, G, 2])
        ve3 = sb("ve3", [GT, G])
        rstd3 = sb("rstd3", [GT, G])
        n3 = sb("n3", [GT, G, E])
        n3_t = sb("n3_t", [EC, 2, RT])
        ff_t = sb("ff_t", [128, FC, RT])
        y = sb("y", [GT, G, E])

        bank_proj = [bank("bank_proj0"), bank("bank_proj1")]
        bank_score = bank("bank_score")
        bank_turn = bank("bank_turn")
        bank_pv = bank("bank_pv")
        bank_front = bank("bank_front")
        bank_back = [bank("bank_back0"), bank("bank_back1")]

        ld_tok, ld_attn, ld_back = sem("ld_tok"), sem("ld_attn"), sem("ld_back")
        zeroed = sem("zeroed")
        wt_turned, wt_copied = sem("wt_turned"), sem("wt_copied")
        pos_ready = sem("pos_ready")
        rel_summed, rel_placed, bias_ready = sem("rel_summed"), sem("rel_placed"), sem("bias_ready")
        vector_passed, pool_passed = sem("vector_passed"), sem("pool_passed")
        place_ready = sem("place_ready")
        cols_turned, cols_ready = sem("cols_turned"), sem("cols_ready")
        wr_ready, power_ready = sem("wr_ready"), sem("power_ready")

        x_loaded = sem("x_loaded")
        x_split_done = signal("x_split_done")
        x_turned = signal("x_turned", 4)
        x_copied = signal("x_copied", 4 * CHANNELS)
        tok_done = signal("tok_done")
        h_ready = signal("h_ready")
        stats1_done, mv1_done = signal("stats1_done", 2), signal("mv1_done", 2)
        ve1_done, rstd1_done = signal("ve1_done"), signal("rstd1_done")
        n1_ready = signal("n1_ready", 2)
        n1_turned, n1_copied = signal("n1_turned"), signal("n1_copied")
        v_done, v_copied = signal("v_done", 4), signal("v_copied", 4)
        qk_done, qk_copied = signal("qk_done", H1), signal("qk_copied", H1, 1)
        score_done, logits_ready = signal("score_done", UNITS), signal("logits_ready", UNITS, 1)
        rowmax_done, shifted_done = signal("rowmax_done", UNITS), signal("shifted_done", UNITS)
        probs_ready = signal("probs_ready", UNITS)
        probs_turned, probs_copied = signal("probs_turned", UNITS), signal("probs_copied", UNITS)
        pv_done = signal("pv_done", UNITS)
        den_done, ctx1_ready = signal("den_done", UNITS), signal("ctx1_ready", UNITS, 1)
        ctx1_turned, ctx1_copied = signal("ctx1_turned", UNITS), signal("ctx1_copied", UNITS, 1)
        wo_done, h2_ready = signal("wo_done"), signal("h2_ready", 1, 1)

        stats2_done, mv2_done = signal("stats2_done", 2), signal("mv2_done", 2)
        pow2_step = signal("pow2_step", 6)
        n2_ready, nn2_ready = signal("n2_ready", 2), signal("nn2_ready", 2)
        n2_turned, n2t_ready = signal("n2_turned"), signal("n2t_ready", 2)
        z_done, score_exp, score_step = signal("z_done"), signal("score_exp"), signal("score_step", 2)
        col_done, cmp_done = signal("col_done", 2), signal("cmp_done", 4)
        rank_done, sel_ready, unrouted_ready = signal("rank_done", 2), signal("sel_ready", 2), signal("unrouted_ready", 2)
        sum_step = signal("sum_step", 3)
        weighted_done, pool_step, mix_step = signal("weighted_done"), signal("pool_step", 2), signal("mix_step", 2)
        k2_done, k2_copied = signal("k2_done"), signal("k2_copied", 2)
        v2_done, v2_copied = signal("v2_done"), signal("v2_copied")
        gather_done, nsel_ready, selt_copied = signal("gather_done"), signal("nsel_ready", 2), signal("selt_copied")
        q2_done, q2_copied, q2h_ready = signal("q2_done"), signal("q2_copied", 2), signal("q2h_ready", 2)
        s2_done, logits2_ready, max2_done = signal("s2_done"), signal("logits2_ready"), signal("max2_done")
        exp2_done, den2_done, probs2_ready = signal("exp2_done", 4), signal("den2_done"), signal("probs2_ready")
        p2_turned, p2_copied = signal("p2_turned"), signal("p2_copied")
        pv2_done, own_done, ctx2_done, ctx2_ready = signal("pv2_done"), signal("own_done"), signal("ctx2_done"), signal("ctx2_ready")
        ao_done, attn2_copied = signal("ao_done"), signal("attn2_copied")
        scat_done, mix_done = signal("scat_done"), signal("mix_done")
        mixed_done, h3_ready = signal("mixed_done", 2), signal("h3_ready")
        stats3_done, mv3_done = signal("stats3_done", 2), signal("mv3_done", 2)
        h2b_ready = signal("h2b_ready")
        ve3_done, rstd3_done, h3b_ready = signal("ve3_done"), signal("rstd3_done"), signal("h3b_ready")
        n3_ready, n3_turned, n3t_ready = signal("n3_ready", 2), signal("n3_turned"), signal("n3t_ready", 2)
        ff1_done, gelu_done = signal("ff1_done", 3), signal("gelu_done", 6)
        ff2_done, y_ready = signal("ff2_done"), signal("y_ready", 1, 1)
        y_stored = signal("y_stored", 16 * G, 1)

        def cols_of(g):
            return slice(g * GT, (g + 1) * GT)

        def half(k):
            return slice(k * EC, (k + 1) * EC)

        UNIT = [(quad, g) for quad in range(H1 // QUAD) for g in range(G)]

        block = ctx.enter_context(nc.Block())

        @block.sync
        def _(sp):
            sp.sem_inc(y_stored.sem, y_stored.per_run)

            def load_x(first, images):
                for c in range(CHANNELS):
                    sp.dma_start(
                        x_rows[c * RB * HP:c * RB * HP + images * HP].rearrange("p a w b -> p (a w b)"),
                        a["x"][bass.ds(first, images), c].rearrange("b (r q) w -> b r (q w)", q=PATCH),
                    ).then_inc(x_loaded, 16)

            def store(run, first, images):
                sp.wait_ge(y_ready.sem, y_ready.at(run))
                out = a["out"].rearrange("b t e -> (b t) e")
                for g in range(-(-images // GB)):
                    n = min(GB, images - g * GB) * TOK
                    sp.dma_start(out[bass.ds(first * TOK + g * GT, n)], y[0:n, g]).then_inc(y_stored.sem, 16)

            load_x(0, RB)
            sp.dma_start(const[:], a["consts"]).then_inc(ld_tok, 16)
            sp.dma_start(w_raw[:], a["L0_tok_W"].rearrange("(k e) d -> e k d", e=EC)).then_inc(ld_tok, 16)
            sp.wait_ge(zeroed, 2)
            for b in range(GB):
                rows = slice(b * TOK + 1, (b + 1) * TOK)
                sp.dma_start(pos_tok[rows], a["L0_tok_pos_embed"][0]).then_inc(ld_tok, 16)
                sp.dma_start(pos_tok[b * TOK:b * TOK + 1], a["cls_tok"][0]).then_inc(ld_tok, 16)
                sp.dma_start(b_tok[rows], a["L0_tok_b"].rearrange("(o e) -> o e", o=1).broadcast_to([NP, E])).then_inc(ld_tok, 16)
            for w, name in ((w_v, "w_v"), (w_q, "w_q"), (w_k, "w_k")):
                src = a["L0_attn_" + name].rearrange("h (k e) d -> k e h d", e=EC)
                for k in range(2):
                    dst = w[:, k] if len(w.shape) == 4 else w[:, k].rearrange("p (h d) -> p h d", h=H1)
                    sp.dma_start(dst, src[k]).then_inc(ld_attn, 16)
            for w, name in ((w_q2, "Wq"), (w_k2, "Wk"), (w_v2, "Wv"), (w_o2, "Wo"), (w_m, "Wm"), (w_ff1, "W1")):
                sp.dma_start(w[0:EC], a["L0_ffn_" + name].rearrange("(k e) d -> e k d", e=EC)).then_inc(ld_back, 16)
            sp.dma_start(w_ff2[:], a["L0_ffn_W2"].rearrange("(k e) d -> e k d", e=128)).then_inc(ld_back, 16)

            sp.wait_ge(x_split_done.sem, x_split_done.at(0))
            load_x(RB, RB)
            with sp.Fori(0, RUNS - 3) as i:
                sp.wait_ge(x_split_done.sem, x_split_done.at(i + 1))
                load_x(i * RB + 2 * RB, RB)
                store(i, i * RB, RB)
            sp.wait_ge(x_split_done.sem, x_split_done.at(RUNS - 2))
            load_x((RUNS - 1) * RB, LAST_B)
            store(RUNS - 3, (RUNS - 3) * RB, RB)
            sp.wait_ge(x_split_done.sem, x_split_done.at(RUNS - 1))
            sp.sem_inc(x_loaded, 16 * CHANNELS)
            store(RUNS - 2, (RUNS - 2) * RB, RB)
            store(RUNS - 1, (RUNS - 1) * RB, LAST_B)
            sp.wait_ge(y_stored.sem, y_stored.at(RUNS - 1))

        @block.gpsimd
        def _(pool):
            pool.memset(power[:], -0.5).then_inc(power_ready, 1)
            pool.memset(eps[:], EPS).then_inc(power_ready, 1)
            pool.wait_ge(power_ready, 2)

            def split_x(run):
                pool.wait_ge(x_loaded, (run + 1) * 16 * CHANNELS)
                if type(run) is not int or run > 0:
                    pool.wait_ge(x_turned.sem, x_turned.at(run - 1))
                pool.sem_inc(pool_passed, 1)
                pool.tensor_copy(x_split[:].rearrange("p w (a b) -> p w a b", b=PATCH),
                                 x_rows[:].rearrange("p a w b -> p w a b")).then_inc(x_split_done.sem, 1)

            def ln1(run):
                pool.wait_ge(mv1_done.sem, mv1_done.at(run))
                pool.tensor_tensor(ve1[:], mv1[:, :, 1], eps[:], ALU.add).then_inc(ve1_done.sem, 1)
                pool.wait_ge(ve1_done.sem, ve1_done.at(run))
                pool.tensor_tensor(rstd1[:], ve1[:], power[:], ALU.pow).then_inc(rstd1_done.sem, 1)

            def shift(run, u):
                pool.wait_ge(rowmax_done.sem, rowmax_done.at(run, u + 1))
                if u >= 2:
                    pool.wait_ge(probs_ready.sem, probs_ready.at(run, u - 1))
                pool.tensor_tensor(shifted[:, u % 2], logits[:, u % 2],
                                   rowmax[:, u % 2].unsqueeze(2).broadcast_to([GT, QUAD, GT]),
                                   ALU.subtract).then_inc(shifted_done.sem, 1)

            def ln2(run):
                pool.wait_ge(mv2_done.sem, mv2_done.at(run))
                s = pow2_step
                pool.tensor_tensor(tmp2[:, 0], mv2[:, :, 1], eps[:], ALU.add).then_inc(s.sem, 1)
                pool.wait_ge(s.sem, s.at(run, 1))
                pool.tensor_tensor(rstd2[:], tmp2[:, 0], power[:], ALU.pow).then_inc(s.sem, 1)
                pool.wait_ge(s.sem, s.at(run, 2))
                pool.tensor_tensor(tmp2[:, 1], rstd2[:], rstd2[:], ALU.mult).then_inc(s.sem, 1)
                pool.wait_ge(s.sem, s.at(run, 3))
                pool.tensor_tensor(tmp2[:, 2], tmp2[:, 1], mv2[:, :, 1], ALU.mult).then_inc(s.sem, 1)
                pool.wait_ge(s.sem, s.at(run, 4))
                pool.tensor_tensor(tmp2[:, 0], tmp2[:, 2], eps[:], ALU.add).then_inc(s.sem, 1)
                pool.wait_ge(s.sem, s.at(run, 5))
                pool.tensor_tensor(rstd22[:], tmp2[:, 0], power[:], ALU.pow).then_inc(s.sem, 1)

            def outer_residual(run):
                pool.tensor_tensor(h2_b[:], h2[:], b_ff2[:].unsqueeze(1).broadcast_to([GT, G, E]),
                                   ALU.add).then_inc(h2b_ready.sem, 1)

            def weigh(run):
                pool.wait_ge(n2t_ready.sem, n2t_ready.at(run))
                pool.wait_ge(score_step.sem, score_step.at(run))
                pool.tensor_tensor(weighted[:], n2_t[:],
                                   score[0:EC].unsqueeze(1).broadcast_to([EC, 2, RT]),
                                   ALU.mult).then_inc(weighted_done.sem, 1)

            def mix(run):
                pool.wait_ge(pool_step.sem, pool_step.at(run))
                pool.tensor_tensor(spread[:].rearrange("p k (b t) -> p k b t", t=TOK),
                                   pooled_n[:].unsqueeze(3).broadcast_to([EC, 2, RB, TOK]),
                                   score[0:EC].rearrange("p (b t) -> p b t", t=TOK).unsqueeze(1).broadcast_to([EC, 2, RB, TOK]),
                                   ALU.mult).then_inc(mix_step.sem, 1)
                pool.wait_ge(mix_step.sem, mix_step.at(run, 1))
                pool.tensor_tensor(mix_t[0:EC], spread[:], n2_t[:], ALU.add).then_inc(mix_step.sem, 1)

            def norm2(run):
                pool.wait_ge(den2_done.sem, den2_done.at(run))
                pool.wait_ge(exp2_done.sem, exp2_done.at(run))
                pool.tensor_tensor(probs2[:], exp2[:], den2_inv[:].unsqueeze(2).broadcast_to([HC * GS, 4, GT]),
                                   ALU.mult).then_inc(probs2_ready.sem, 1)

            def ln3(run):
                pool.wait_ge(mv3_done.sem, mv3_done.at(run))
                pool.tensor_tensor(ve3[:], mv3[:, :, 1], eps[:], ALU.add).then_inc(ve3_done.sem, 1)
                pool.wait_ge(ve3_done.sem, ve3_done.at(run))
                pool.tensor_tensor(rstd3[:], ve3[:], power[:], ALU.pow).then_inc(rstd3_done.sem, 1)
                pool.wait_ge(h3_ready.sem, h3_ready.at(run))
                pool.wait_ge(h2b_ready.sem, h2b_ready.at(run))
                pool.tensor_tensor(h3_b[:], h3[:], h2_b[:], ALU.add).then_inc(h3b_ready.sem, 1)

            def body(back, front):
                if back is not None:
                    ln2(back)
                if front is not None:
                    ln1(front)
                    split_x(front + 1)
                if back is not None:
                    outer_residual(back)
                    weigh(back)
                    mix(back)
                if front is not None:
                    shift(front, 0)
                if back is not None:
                    norm2(back)
                if front is not None:
                    shift(front, 1)
                if back is not None:
                    ln3(back)
                if front is not None:
                    shift(front, 2)
                    shift(front, 3)

            split_x(0)
            pool.wait_ge(ld_back, LD_BACK)
            body(None, 0)
            with pool.Fori(0, RUNS - 1) as i:
                body(i, i + 1)
            body(RUNS - 1, None)

        @block.scalar
        def _(act):
            act.sem_inc(qk_copied.sem, qk_copied.per_run)
            act.sem_inc(ctx1_copied.sem, ctx1_copied.per_run)
            act.dma_start(w_o[:], a["L0_attn_w_o"].rearrange("h d e -> (h d) e").rearrange("(k p) e -> p k e", p=128)).then_inc(ld_attn, 16)
            act.dma_start(rel[:], a["L0_attn_rel_emb"][:, MAX_DIST - TOK:MAX_DIST - TOK + REL].rearrange("h r d o -> r h (d o)")).then_inc(ld_attn, 16)
            for n, name in enumerate(("g1", "b1", "g2", "b2", "bq", "bk", "bv", "Wr")):
                act.dma_start(vec_rows[n:n + 1], a["L0_ffn_" + name].rearrange("(o e) -> o e", o=1)).then_inc(ld_back, 16)
            act.dma_start(br_neg[:], a["L0_ffn_br"].rearrange("(o e) -> o e", o=1).broadcast_to([GT, 1])).then_inc(ld_back, 16)
            act.dma_start(b_ff1_rows[:], a["L0_ffn_bf1"].rearrange("(m p) -> m p", p=128)).then_inc(ld_back, 16)
            act.dma_start(b_ff2[:], a["L0_ffn_bf2"].rearrange("(o e) -> o e", o=1).broadcast_to([GT, E])).then_inc(ld_back, 16)
            act.dma_start(w_o2[EC:EC + 1, 1], a["L0_ffn_bo"].rearrange("(o e) -> o e", o=1)).then_inc(ld_back, 16)
            act.dma_start(w_m[EC:EC + 1, 1], a["L0_ffn_bm"].rearrange("(o e) -> o e", o=1)).then_inc(ld_back, 16)

            def copy_x(run, j):
                hf, tri = j // 2, j % 2
                act.wait_ge(x_turned.sem, x_turned.at(run, j + 1))
                src = bank_front[:, 0:TW * XP].rearrange("p (w q) -> p w q", w=TW)
                for c in range(CHANNELS):
                    dst = x_t[:, 2 * c + hf].rearrange("p (b t) -> p b t", t=TOK)[:, :, 1:]
                    dst = dst.rearrange("p b (r w) -> p b r w", w=HP)[:, :, :, tri * TW:(tri + 1) * TW]
                    s = src[:, :, c * RB * HP:(c + 1) * RB * HP].rearrange("p w (b r) -> p b r w", r=HP)
                    act.copy(dst, s).then_inc(x_copied.sem, 1)

            def copy_n1(run):
                act.wait_ge(n1_turned.sem, n1_turned.at(run))
                act.copy(n1_t[:].rearrange("p k t -> p (k t)"), bank_front[0:EC, 0:2 * RT]).then_inc(n1_copied.sem, 1)

            def copy_qk(run, hd):
                act.wait_ge(qk_done.sem, qk_done.at(run, hd + 1))
                act.copy(qk[:, hd].rearrange("p a t -> p (a t)"), bank_proj[hd % 2][0:D1, 0:2 * RT]).then_inc(qk_copied.sem, 1)

            def exp1(run, u):
                act.wait_ge(shifted_done.sem, shifted_done.at(run, u + 1))
                act.activation(probs[:, u % 2], shifted[:, u % 2], ACT.Exp).then_inc(probs_ready.sem, 1)

            def copy_probs(run, u):
                act.wait_ge(probs_turned.sem, probs_turned.at(run, u + 1))
                act.copy(probs_t[:, u % 2].rearrange("p h t -> p (h t)"), bank_turn[0:GT, 0:QUAD * GT]).then_inc(probs_copied.sem, 1)

            def copy_ctx1(run, u):
                quad, g = UNIT[u]
                act.wait_ge(ctx1_turned.sem, ctx1_turned.at(run, u + 1))
                act.copy(ctx1_t[:, 3 * quad:3 * quad + 3, cols_of(g)],
                         bank_turn[:, 0:3 * GT].rearrange("p (k t) -> p k t", k=3)).then_inc(ctx1_copied.sem, 1)

            def exp_score(run):
                act.wait_ge(z_done.sem, z_done.at(run))
                act.activation(score_e[:], bank_back[1][0:GT, 0:RT], ACT.Exp, bias=br_neg[:], scale=-1.0).then_inc(score_exp.sem, 1)

            def copy_k2(run):
                act.wait_ge(k2_done.sem, k2_done.at(run))
                for k in range(2):
                    act.activation(k2_t[:, k], bank_back[0][0:EC, k * RT:(k + 1) * RT], ACT.Identity,
                                   bias=bk[:, k:k + 1]).then_inc(k2_copied.sem, 1)

            def copy_v2(run):
                act.wait_ge(v2_done.sem, v2_done.at(run))
                act.copy(v2[:].rearrange("p g e -> p (g e)"), bank_back[1][0:GT, 0:G * E]).then_inc(v2_copied.sem, 1)

            def copy_q2(run):
                act.wait_ge(q2_done.sem, q2_done.at(run))
                for k in range(2):
                    act.activation(q2_t[:, k], bank_back[1][0:EC, k * RS:(k + 1) * RS], ACT.Identity,
                                   bias=bq[:, k:k + 1]).then_inc(q2_copied.sem, 1)

            def exp_2(run):
                act.wait_ge(max2_done.sem, max2_done.at(run))
                for j in range(4):
                    act.activation(exp2[:, j], logits2[:, j], ACT.Exp, bias=negmax2[:, j:j + 1],
                                   accum_out=den2[:, j:j + 1]).then_inc(exp2_done.sem, 1)

            def copy_p2(run):
                act.wait_ge(p2_turned.sem, p2_turned.at(run))
                act.copy(probs2_t[:].rearrange("p j t -> p (j t)"), bank_back[1][0:GT, 0:4 * HC * GS]).then_inc(p2_copied.sem, 1)

            def copy_attn2(run):
                act.wait_ge(ao_done.sem, ao_done.at(run))
                act.copy(attn2[:], bank_back[1][0:RS, 0:E]).then_inc(attn2_copied.sem, 1)

            def gelu(run):
                for m in range(FC):
                    if m % 2 == 0:
                        act.wait_ge(ff1_done.sem, ff1_done.at(run, m // 2 + 1))
                    act.activation(ff_t[:, m], bank_back[(m // 2 + 1) % 2][:, (m % 2) * RT:(m % 2 + 1) * RT], ACT.Gelu,
                                   bias=b_ff1[:, m:m + 1]).then_inc(gelu_done.sem, 1)

            def body(back, front):
                b, f = back is not None, front is not None
                if f:
                    copy_n1(front)
                if b:
                    exp_score(back)
                    copy_k2(back)
                    copy_v2(back)
                if f:
                    copy_qk(front, 0)
                    copy_qk(front, 1)
                if b:
                    copy_q2(back)
                if f:
                    copy_qk(front, 2)
                    copy_qk(front, 3)
                    copy_qk(front, 4)
                if b:
                    exp_2(back)
                if f:
                    exp1(front, 0)
                    copy_qk(front, 5)
                if b:
                    copy_p2(back)
                if f:
                    exp1(front, 1)
                    copy_probs(front, 0)
                    copy_qk(front, 6)
                    copy_x(front + 1, 0)
                if b:
                    copy_attn2(back)
                if f:
                    copy_qk(front, 7)
                    copy_probs(front, 1)
                    copy_x(front + 1, 1)
                    copy_ctx1(front, 0)
                    copy_x(front + 1, 2)
                    exp1(front, 2)
                    copy_ctx1(front, 1)
                    exp1(front, 3)
                    copy_x(front + 1, 3)
                    copy_probs(front, 2)
                    copy_probs(front, 3)
                if b:
                    gelu(back)
                if f:
                    copy_ctx1(front, 2)
                    copy_ctx1(front, 3)

            act.wait_ge(zeroed, 6)
            for j in range(4):
                copy_x(0, j)
            body(None, 0)
            with act.Fori(0, RUNS - 1) as i:
                body(i, i + 1)
            body(RUNS - 1, None)

        @block.vector
        def _(dve):
            dve.memset(pos_tok[:], 0.0).then_inc(zeroed, 1)
            dve.memset(b_tok[:], 0.0).then_inc(zeroed, 1)
            dve.memset(x_t[:], 0.0).then_inc(zeroed, 1)
            dve.memset(sel[:], 0.0).then_inc(zeroed, 1)
            dve.memset(v[:, :, :, D1:D1 + 1], 1.0).then_inc(zeroed, 1)
            dve.memset(mix_t[EC:EC + 1], 1.0).then_inc(zeroed, 1)
            dve.memset(ctx2_t[EC:EC + 1], 1.0).then_inc(zeroed, 1)
            for s in (logits_ready, ctx1_ready, h2_ready, y_ready):
                dve.sem_inc(s.sem, s.per_run)
            for j in range(PC // 2):
                dve.wait_ge(wt_turned, j + 1)
                dve.tensor_copy(w_tok[:, 2 * j:2 * j + 2, :].rearrange("p c e -> p (c e)"),
                                bank_proj[j % 2][:, 0:2 * E]).then_inc(wt_copied, 1)
            dve.wait_ge(ld_tok, LD_TOK)
            dve.tensor_tensor(pos_tok[:], pos_tok[:], b_tok[:], ALU.add).then_inc(pos_ready, 1)
            shift_ap = cst("shift", REL)
            dve.tensor_copy(place[:].rearrange("p n (b q) -> p n b q", b=GB),
                            bass.AP(tensor=shift_ap.tensor, offset=shift_ap.offset,
                                    ap=[shift_ap.ap[0], [1, TOK], [0, GB], [1, TOK]])).then_inc(place_ready, 1)
            dve.wait_ge(ld_attn, LD_ATTN)
            dve.tensor_reduce(rel_sum[:], rel[:], AX_X, ALU.add).then_inc(rel_summed, 1)
            dve.wait_ge(rel_placed, 1)
            placed = bank_score[0:GT, 0:TOK * H1].rearrange("p (k h) -> p k h", h=H1)
            for b in range(GB):
                dve.tensor_tensor(
                    pos_bias[:, :, b * TOK:(b + 1) * TOK], placed.rearrange("p k h -> p h k"),
                    cst("apart", GT)[:, b:b + 1].unsqueeze(2).broadcast_to([GT, H1, TOK]),
                    ALU.add).then_inc(bias_ready, 1)
            dve.wait_ge(bias_ready, GB)
            dve.wait_ge(cols_turned, 1)
            dve.tensor_copy(cols[:].rearrange("p n k -> p k n"),
                            bank_turn[0:EC, 0:16].rearrange("p (k n) -> p k n", k=2)).then_inc(cols_ready, 1)
            dve.tensor_copy(b_ff1[:], bank_turn[:, 16:16 + FC]).then_inc(cols_ready, 1)
            dve.wait_ge(cols_ready, 2)
            dve.wait_ge(ld_back, LD_BACK)
            dve.tensor_copy(wr_all[:], wr.unsqueeze(2).broadcast_to([EC, 2, GT])).then_inc(wr_ready, 1)
            dve.tensor_scalar(br_neg[:], br_neg[:], -1.0, None, ALU.mult).then_inc(wr_ready, 1)
            dve.wait_ge(wr_ready, 2)

            def stats(run, src, st, mv, s_st, s_mv):
                for g in range(G):
                    dve.bn_stats(st[:, g], src[:, g]).then_inc(s_st.sem, 1)
                for g in range(G):
                    dve.wait_ge(s_st.sem, s_st.at(run, g + 1))
                    dve.sem_inc(vector_passed, 1)
                    dve.bn_aggr(mv[:, g], st[:, g]).then_inc(s_mv.sem, 1)

            def standardise(dst, src, mv, rstd, done):
                for g in range(G):
                    dve.tensor_scalar(dst[:, g], src[:, g], mv[:, g, 0:1], rstd[:, g:g + 1],
                                      ALU.subtract, ALU.mult).then_inc(done.sem, 1)

            def ln2_stats(run):
                dve.wait_ge(h2_ready.sem, h2_ready.at(run))
                stats(run, h2, stats2, mv2, stats2_done, mv2_done)

            def ln2_norm(run):
                dve.wait_ge(pow2_step.sem, pow2_step.at(run))
                standardise(n2, h2, mv2, rstd2, n2_ready)
                dve.wait_ge(n2_ready.sem, n2_ready.at(run))
                for g in range(G):
                    dve.tensor_scalar(nn2[:, g], n2[:, g], rstd22[:, g:g + 1], None, ALU.mult).then_inc(nn2_ready.sem, 1)

            def add_pos(run):
                dve.wait_ge(tok_done.sem, tok_done.at(run))
                dve.tensor_tensor(h[:], bank_front[0:GT, 0:G * E].rearrange("p (g e) -> p g e", g=G),
                                  pos_tok[:].unsqueeze(1).broadcast_to([GT, G, E]), ALU.add).then_inc(h_ready.sem, 1)
                dve.wait_ge(h_ready.sem, h_ready.at(run))
                stats(run, h, stats1, mv1, stats1_done, mv1_done)

            def ln1_norm(run):
                dve.wait_ge(rstd1_done.sem, rstd1_done.at(run))
                standardise(n1, h, mv1, rstd1, n1_ready)

            def gain(run, turned, src_bank, dst, gg, bb, done):
                dve.wait_ge(turned.sem, turned.at(run))
                for k in range(2):
                    dve.tensor_scalar(dst[:, k], src_bank[0:EC, k * RT:(k + 1) * RT], gg[:, k:k + 1], bb[:, k:k + 1],
                                      ALU.mult, ALU.add).then_inc(done.sem, 1)

            def route(run):
                dve.wait_ge(score_exp.sem, score_exp.at(run))
                dve.tensor_scalar(score_d[:], score_e[:], 1.0, None, ALU.add).then_inc(score_step.sem, 1)
                dve.wait_ge(score_step.sem, score_step.at(run, 1))
                dve.reciprocal(score[:], score_d[:]).then_inc(score_step.sem, 1)
                dve.wait_ge(score_step.sem, score_step.at(run, 2))
                for g in range(G):
                    dve.tensor_tensor_reduce(out=junk[:, g], in0=score[:, cols_of(g)], in1=ident[0:GT, 0:GT], scale=1.0,
                                             scalar=0.0, op0=ALU.mult, op1=ALU.add,
                                             accum_out=score_col[:, g:g + 1]).then_inc(col_done.sem, 1)
                dve.tensor_reduce(s_sum[:], score[0:EC].rearrange("p (b t) -> p b t", t=TOK), AX_X, ALU.add).then_inc(sum_step.sem, 1)
                for g in range(G):
                    dve.wait_ge(col_done.sem, col_done.at(run, g + 1))
                    dve.scalar_tensor_tensor(out=less[:, g], in0=score[:, cols_of(g)], scalar=score_col[:, g:g + 1],
                                             in1=cst("same", GT), op0=ALU.is_lt, op1=ALU.mult).then_inc(cmp_done.sem, 1)
                    dve.scalar_tensor_tensor(out=tied[:, g], in0=score[:, cols_of(g)], scalar=score_col[:, g:g + 1],
                                             in1=cst("lower", GT), op0=ALU.is_equal, op1=ALU.mult).then_inc(cmp_done.sem, 1)
                dve.wait_ge(sum_step.sem, sum_step.at(run, 1))
                dve.tensor_scalar(s_eps[:], s_sum[:], 1e-6, None, ALU.add).then_inc(sum_step.sem, 1)
                for g in range(G):
                    dve.wait_ge(cmp_done.sem, cmp_done.at(run, 2 * g + 2))
                    dve.sem_inc(vector_passed, 1)
                    dve.tensor_tensor_reduce(out=junk[:, 2 + g], in0=less[:, g], in1=tied[:, g], scale=1.0, scalar=0.0,
                                             op0=ALU.add, op1=ALU.add, accum_out=rank[:, g:g + 1]).then_inc(rank_done.sem, 1)
                dve.wait_ge(sum_step.sem, sum_step.at(run, 2))
                dve.reciprocal(s_inv[:], s_eps[:]).then_inc(sum_step.sem, 1)
                for g in range(G):
                    dve.wait_ge(rank_done.sem, rank_done.at(run, g + 1))
                    dve.tensor_scalar(sel[:, g, g * GS:(g + 1) * GS], cst("slot", GT), rank[:, g:g + 1], None,
                                      ALU.is_equal).then_inc(sel_ready.sem, 1)
                    dve.tensor_scalar(unrouted[:, g:g + 1], rank[:, g:g + 1], float(SEL), None,
                                      ALU.is_ge).then_inc(unrouted_ready.sem, 1)

            def pool_scores(run):
                dve.wait_ge(weighted_done.sem, weighted_done.at(run))
                dve.tensor_reduce(pooled[:].rearrange("p k b -> p (k b)"), weighted[:].rearrange("p k (b t) -> p (k b) t", t=TOK),
                                  AX_X, ALU.add).then_inc(pool_step.sem, 1)
                dve.wait_ge(pool_step.sem, pool_step.at(run, 1))
                dve.wait_ge(sum_step.sem, sum_step.at(run))
                dve.tensor_tensor(pooled_n[:], pooled[:], s_inv[:].unsqueeze(1).broadcast_to([EC, 2, RB]),
                                  ALU.mult).then_inc(pool_step.sem, 1)

            def copy_v(run, j):
                g, part = j // 2, j % 2
                dve.wait_ge(v_done.sem, v_done.at(run, j + 1))
                dve.tensor_copy(v[:, g, part * QUAD:(part + 1) * QUAD, 0:D1],
                                bank_proj[j % 2][0:GT, 0:QUAD * D1].rearrange("p (h d) -> p h d", h=QUAD)).then_inc(v_copied.sem, 1)

            def copy_sel(run):
                gain_src = bank_back[0]
                dve.wait_ge(gather_done.sem, gather_done.at(run))
                for k in range(2):
                    dve.tensor_scalar(nsel_t[:, k], gain_src[0:EC, k * RS:(k + 1) * RS], g1[:, k:k + 1], b1[:, k:k + 1],
                                      ALU.mult, ALU.add).then_inc(nsel_ready.sem, 1)
                dve.tensor_copy(sel_t[:].rearrange("p g t -> p (g t)"), gain_src[0:RS, 128:128 + RT]).then_inc(selt_copied.sem, 1)

            def q2_by_head(run):
                dve.wait_ge(q2_copied.sem, q2_copied.at(run))
                for k in range(2):
                    dve.tensor_tensor(q2_heads[:, k],
                                      q2_t[:, k].rearrange("p (g q) -> p g q", g=G).unsqueeze(2).broadcast_to([EC, G, HC, GS]),
                                      cst("headmask", EC).unsqueeze(1).unsqueeze(3).broadcast_to([EC, G, HC, GS]),
                                      ALU.mult).then_inc(q2h_ready.sem, 1)

            def logits_2(run):
                dve.wait_ge(s2_done.sem, s2_done.at(run))
                dve.scalar_tensor_tensor(out=logits2[:], in0=bank_back[0][0:HC * GS, 0:4 * GT].rearrange("p (j t) -> p j t", j=4),
                                         scalar=float(D2) ** -0.5,
                                         in1=cst("apart2", HC * GS).unsqueeze(1).broadcast_to([HC * GS, 4, GT]),
                                         op0=ALU.mult, op1=ALU.add).then_inc(logits2_ready.sem, 1)
                dve.wait_ge(logits2_ready.sem, logits2_ready.at(run))
                dve.tensor_reduce(negmax2[:], logits2[:], AX_X, ALU.max, negate=True).then_inc(max2_done.sem, 1)

            def den_2(run):
                dve.wait_ge(exp2_done.sem, exp2_done.at(run))
                dve.reciprocal(den2_inv[:], den2[:]).then_inc(den2_done.sem, 1)

            def own_ctx2(run):
                dve.wait_ge(pv2_done.sem, pv2_done.at(run))
                dve.tensor_tensor(own[:], bank_back[0][0:EC, 0:4 * HC * GS].rearrange("p (j h q) -> p j h q", j=4, h=HC),
                                  cst("headmask", EC).unsqueeze(1).unsqueeze(3).broadcast_to([EC, 4, HC, GS]),
                                  ALU.mult).then_inc(own_done.sem, 1)
                dve.wait_ge(own_done.sem, own_done.at(run))
                dve.tensor_reduce(ctx2[:], own[:].rearrange("p j h q -> p j q h"), AX_X, ALU.add).then_inc(ctx2_done.sem, 1)
                dve.wait_ge(ctx2_done.sem, ctx2_done.at(run))
                dve.tensor_tensor(ctx2_t[0:EC], ctx2[:].rearrange("p (k g) q -> p k (g q)", k=2),
                                  bv.unsqueeze(2).broadcast_to([EC, 2, RS]), ALU.add).then_inc(ctx2_ready.sem, 1)

            def softmax1(run, u):
                quad, g = UNIT[u]
                dve.wait_ge(score_done.sem, score_done.at(run, u + 1))
                dve.scalar_tensor_tensor(out=logits[:, u % 2].rearrange("p h t -> p (h t)"), in0=bank_score[0:GT, 0:QUAD * GT],
                                         scalar=float(D1) ** -0.5,
                                         in1=pos_bias[:, quad * QUAD:(quad + 1) * QUAD].rearrange("p h t -> p (h t)"),
                                         op0=ALU.mult, op1=ALU.add).then_inc(logits_ready.sem, 1)
                dve.wait_ge(logits_ready.sem, logits_ready.at(run, u + 1))
                dve.tensor_reduce(rowmax[:, u % 2], logits[:, u % 2], AX_X, ALU.max).then_inc(rowmax_done.sem, 1)

            def normalise1(run, u):
                quad, g = UNIT[u]
                pv = bank_pv[0:GT, 0:QUAD * (D1 + 1)].rearrange("p (h d) -> p h d", h=QUAD)
                dve.wait_ge(pv_done.sem, pv_done.at(run, u + 1))
                dve.reciprocal(den_inv[:, u], pv[:, :, D1]).then_inc(den_done.sem, 1)
                dve.wait_ge(den_done.sem, den_done.at(run, u + 1))
                dve.tensor_tensor(ctx1[:, g, quad * QUAD:(quad + 1) * QUAD], pv[:, :, 0:D1],
                                  den_inv[:, u].unsqueeze(2).broadcast_to([GT, QUAD, D1]), ALU.mult).then_inc(ctx1_ready.sem, 1)

            def residual1(run):
                dve.wait_ge(wo_done.sem, wo_done.at(run))
                dve.tensor_tensor(h2[:].rearrange("p g e -> p (g e)"), bank_front[0:GT, 0:G * E],
                                  h[:].rearrange("p g e -> p (g e)"), ALU.add).then_inc(h2_ready.sem, 1)

            def merge(run):
                dve.wait_ge(mix_done.sem, mix_done.at(run))
                for g in range(G):
                    dve.scalar_tensor_tensor(out=mixed[:, g], in0=bank_back[1][0:GT, g * E:(g + 1) * E], scalar=unrouted[:, g:g + 1],
                                             in1=n2[:, g], op0=ALU.mult, op1=ALU.add).then_inc(mixed_done.sem, 1)

            def residual2(run):
                dve.wait_ge(scat_done.sem, scat_done.at(run))
                dve.wait_ge(mixed_done.sem, mixed_done.at(run))
                dve.tensor_tensor(h3[:].rearrange("p g e -> p (g e)"), bank_back[0][0:GT, 0:G * E],
                                  mixed[:].rearrange("p g e -> p (g e)"), ALU.add).then_inc(h3_ready.sem, 1)
                dve.wait_ge(h3_ready.sem, h3_ready.at(run))
                stats(run, h3, stats3, mv3, stats3_done, mv3_done)

            def ln3_norm(run):
                dve.wait_ge(rstd3_done.sem, rstd3_done.at(run))
                standardise(n3, h3, mv3, rstd3, n3_ready)
                gain(run, n3_turned, bank_back[0], n3_t, g2, b2, n3t_ready)

            def residual3(run):
                dve.wait_ge(ff2_done.sem, ff2_done.at(run))
                dve.wait_ge(h3b_ready.sem, h3b_ready.at(run))
                dve.wait_ge(y_stored.sem, y_stored.before(run))
                dve.tensor_tensor(y[:].rearrange("p g e -> p (g e)"), bank_back[0][0:GT, 0:G * E],
                                  h3_b[:].rearrange("p g e -> p (g e)"), ALU.add).then_inc(y_ready.sem, 1)

            def body(back, front):
                b, f = back is not None, front is not None
                if b:
                    ln2_stats(back)
                    ln2_norm(back)
                if f:
                    add_pos(front)
                if b:
                    gain(back, n2_turned, bank_back[0], n2_t, g1, b1, n2t_ready)
                if f:
                    ln1_norm(front)
                if b:
                    route(back)
                if f:
                    for j in range(4):
                        copy_v(front, j)
                if b:
                    pool_scores(back)
                    copy_sel(back)
                    q2_by_head(back)
                    logits_2(back)
                if f:
                    softmax1(front, 0)
                if b:
                    den_2(back)
                if f:
                    softmax1(front, 1)
                if b:
                    merge(back)
                    own_ctx2(back)
                if f:
                    normalise1(front, 0)
                    normalise1(front, 1)
                if b:
                    residual2(back)
                if f:
                    softmax1(front, 2)
                if b:
                    ln3_norm(back)
                if f:
                    softmax1(front, 3)
                    normalise1(front, 2)
                    normalise1(front, 3)
                if b:
                    residual3(back)
                if f:
                    residual1(front)

            body(None, 0)
            with dve.Fori(0, RUNS - 1) as i:
                body(i, i + 1)
            body(RUNS - 1, None)

        @block.tensor
        def _(pe):
            def turn_x(run, j):
                hf, tri = j // 2, j % 2
                if j == 0:
                    pe.wait_ge(x_split_done.sem, x_split_done.at(run))
                    if type(run) is not int or run > 0:
                        pe.wait_ge(n1_copied.sem, n1_copied.at(run - 1))
                else:
                    pe.wait_ge(x_copied.sem, x_copied.at(run, CHANNELS * j))
                for n in range(TW):
                    mm = pe.transpose(bank_front[:, n * XP:(n + 1) * XP],
                                      x_split[:, tri * TW + n, hf * 128:(hf + 1) * 128], ident[0:XP, 0:XP])
                mm.then_inc(x_turned.sem, 1)

            def tokens(run):
                pe.wait_ge(x_copied.sem, x_copied.at(run))
                pe.wait_ge(h2_ready.sem, h2_ready.before(run))
                for g in range(G):
                    for c in range(PC):
                        mm = pe.matmul(bank_front[0:GT, g * E:(g + 1) * E], x_t[:, c, cols_of(g)], w_tok[:, c, :],
                                       start=(c == 0), stop=(c == PC - 1))
                mm.then_inc(tok_done.sem, 1)

            def turn_tokens(src, dst_bank, done):
                for k in range(2):
                    for g in range(G):
                        mm = pe.transpose(dst_bank[0:EC, k * RT + g * GT:k * RT + (g + 1) * GT], src[:, g, half(k)],
                                          ident[0:GT, 0:GT])
                mm.then_inc(done.sem, 1)

            def turn_n1(run):
                pe.wait_ge(n1_ready.sem, n1_ready.at(run))
                turn_tokens(n1, bank_front, n1_turned)

            def values(run, j):
                g, part = j // 2, j % 2
                if j == 0:
                    pe.wait_ge(n1_copied.sem, n1_copied.at(run))
                if j < 2:
                    pe.wait_ge(qk_copied.sem, qk_copied.at(run - 1, H1 - 1 + j))
                else:
                    pe.wait_ge(v_copied.sem, v_copied.at(run, j - 1))
                for k in range(2):
                    mm = pe.matmul(bank_proj[j % 2][0:GT, 0:QUAD * D1], n1_t[:, k, cols_of(g)],
                                   w_v[:, k, part * QUAD * D1:(part + 1) * QUAD * D1], start=(k == 0), stop=(k == 1))
                mm.then_inc(v_done.sem, 1)

            def queries_keys(run, hd):
                if hd < 2:
                    pe.wait_ge(v_copied.sem, v_copied.at(run, 3 + hd))
                else:
                    pe.wait_ge(qk_copied.sem, qk_copied.at(run, hd - 1))
                for n, w in enumerate((w_q, w_k)):
                    for k in range(2):
                        mm = pe.matmul(bank_proj[hd % 2][0:D1, n * RT:(n + 1) * RT], w[:, k, hd, :], n1_t[:, k, :],
                                       start=(k == 0), stop=(k == 1))
                mm.then_inc(qk_done.sem, 1)

            def scores(run, u):
                quad, g = UNIT[u]
                pe.wait_ge(qk_copied.sem, qk_copied.at(run, QUAD * (quad + 1)))
                pe.wait_ge(logits_ready.sem, logits_ready.at(run, u))
                for n in range(QUAD):
                    hd = quad * QUAD + n
                    mm = pe.matmul(bank_score[0:GT, n * GT:(n + 1) * GT], qk[:, hd, 0, cols_of(g)], qk[:, hd, 1, cols_of(g)],
                                   start=True, stop=True)
                mm.then_inc(score_done.sem, 1)

            def turn_probs(run, u, freed, value):
                pe.wait_ge(probs_ready.sem, probs_ready.at(run, u + 1))
                pe.wait_ge(freed.sem, value)
                for n in range(QUAD):
                    mm = pe.transpose(bank_turn[0:GT, n * GT:(n + 1) * GT], probs[:, u % 2, n], ident[0:GT, 0:GT])
                mm.then_inc(probs_turned.sem, 1)

            def probs_values(run, u):
                quad, g = UNIT[u]
                pe.wait_ge(probs_copied.sem, probs_copied.at(run, u + 1))
                pe.wait_ge(ctx1_ready.sem, ctx1_ready.at(run, u))
                for n in range(QUAD):
                    mm = pe.matmul(bank_pv[0:GT, n * (D1 + 1):(n + 1) * (D1 + 1)], probs_t[:, u % 2, n],
                                   v[:, g, quad * QUAD + n], start=True, stop=True)
                mm.then_inc(pv_done.sem, 1)

            def turn_ctx1(run, u, freed, value):
                quad, g = UNIT[u]
                pe.wait_ge(ctx1_ready.sem, ctx1_ready.at(run, u + 1))
                pe.wait_ge(freed.sem, value)
                rows = ctx1[:, g].rearrange("p h d -> p (h d)")
                for n in range(3):
                    c = 3 * quad + n
                    mm = pe.transpose(bank_turn[:, n * GT:(n + 1) * GT], rows[:, c * 128:(c + 1) * 128], ident[0:GT, 0:GT])
                mm.then_inc(ctx1_turned.sem, 1)

            def project1(run):
                pe.wait_ge(ctx1_copied.sem, ctx1_copied.at(run))
                pe.wait_ge(x_copied.sem, x_copied.at(run + 1))
                for g in range(G):
                    for c in range(FC):
                        mm = pe.matmul(bank_front[0:GT, g * E:(g + 1) * E], ctx1_t[:, c, cols_of(g)], w_o[:, c, :],
                                       start=(c == 0), stop=(c == FC - 1))
                mm.then_inc(wo_done.sem, 1)

            def turn_n2(run):
                pe.wait_ge(nn2_ready.sem, nn2_ready.at(run))
                pe.wait_ge(y_ready.sem, y_ready.before(run))
                turn_tokens(nn2, bank_back[0], n2_turned)

            def router(run):
                pe.wait_ge(n2t_ready.sem, n2t_ready.at(run))
                for k in range(2):
                    mm = pe.matmul(bank_back[1][0:GT, 0:RT], wr_all[:, k], n2_t[:, k], start=(k == 0), stop=(k == 1))
                mm.then_inc(z_done.sem, 1)

            def keys2(run):
                for m in range(2):
                    for k in range(2):
                        mm = pe.matmul(bank_back[0][0:EC, m * RT:(m + 1) * RT], w_k2[:, k, half(m)], n2_t[:, k],
                                       start=(k == 0), stop=(k == 1))
                mm.then_inc(k2_done.sem, 1)

            def values2(run):
                pe.wait_ge(score_exp.sem, score_exp.at(run))
                for g in range(G):
                    for k in range(2):
                        mm = pe.matmul(bank_back[1][0:GT, g * E:(g + 1) * E], n2_t[:, k, cols_of(g)], w_v2[:, k, :],
                                       start=(k == 0), stop=(k == 1))
                mm.then_inc(v2_done.sem, 1)

            def gather(run):
                pe.wait_ge(sel_ready.sem, sel_ready.at(run))
                pe.wait_ge(k2_copied.sem, k2_copied.at(run))
                for k in range(2):
                    for g in range(G):
                        pe.matmul(bank_back[0][0:EC, k * RS:(k + 1) * RS], nn2[:, g, half(k)], sel[:, g],
                                  start=(g == 0), stop=(g == G - 1))
                for g in range(G):
                    mm = pe.transpose(bank_back[0][0:RS, 128 + g * GT:128 + (g + 1) * GT], sel[:, g], ident[0:GT, 0:GT])
                mm.then_inc(gather_done.sem, 1)

            def queries2(run):
                pe.wait_ge(nsel_ready.sem, nsel_ready.at(run))
                pe.wait_ge(v2_copied.sem, v2_copied.at(run))
                for m in range(2):
                    for k in range(2):
                        mm = pe.matmul(bank_back[1][0:EC, m * RS:(m + 1) * RS], w_q2[:, k, half(m)], nsel_t[:, k],
                                       start=(k == 0), stop=(k == 1))
                mm.then_inc(q2_done.sem, 1)

            def scores2(run):
                pe.wait_ge(q2h_ready.sem, q2h_ready.at(run))
                pe.wait_ge(k2_copied.sem, k2_copied.at(run))
                pe.wait_ge(selt_copied.sem, selt_copied.at(run))
                for k in range(2):
                    for g in range(G):
                        j = k * G + g
                        mm = pe.matmul(bank_back[0][0:HC * GS, j * GT:(j + 1) * GT],
                                       q2_heads[:, k, g].rearrange("p h q -> p (h q)"), k2_t[:, k, cols_of(g)],
                                       start=True, stop=True)
                mm.then_inc(s2_done.sem, 1)

            def turn_probs2(run):
                pe.wait_ge(probs2_ready.sem, probs2_ready.at(run))
                pe.wait_ge(q2_copied.sem, q2_copied.at(run))
                n = HC * GS
                for j in range(4):
                    mm = pe.transpose(bank_back[1][0:GT, j * n:(j + 1) * n], probs2[:, j], ident[0:n, 0:n])
                mm.then_inc(p2_turned.sem, 1)

            def probs_values2(run):
                pe.wait_ge(p2_copied.sem, p2_copied.at(run))
                pe.wait_ge(logits2_ready.sem, logits2_ready.at(run))
                n = HC * GS
                for k in range(2):
                    for g in range(G):
                        j = k * G + g
                        mm = pe.matmul(bank_back[0][0:EC, j * n:(j + 1) * n], v2[:, g, half(k)], probs2_t[:, j],
                                       start=True, stop=True)
                mm.then_inc(pv2_done.sem, 1)

            def with_bias(out, lhs, w, n):
                pe.matmul(out, lhs[0:EC, 0, n], w[0:EC, 0, :], start=True, stop=False)
                return pe.matmul(out, lhs[:, 1, n], w[:, 1, :], start=False, stop=True)

            def project2(run):
                pe.wait_ge(ctx2_ready.sem, ctx2_ready.at(run))
                pe.wait_ge(mixed_done.sem, mixed_done.at(run))
                with_bias(bank_back[1][0:RS, 0:E], ctx2_t, w_o2, slice(0, RS)).then_inc(ao_done.sem, 1)

            def mix_project(run):
                pe.wait_ge(mix_step.sem, mix_step.at(run))
                pe.wait_ge(p2_copied.sem, p2_copied.at(run))
                for g in range(G):
                    mm = with_bias(bank_back[1][0:GT, g * E:(g + 1) * E], mix_t, w_m, cols_of(g))
                mm.then_inc(mix_done.sem, 1)

            def scatter(run):
                pe.wait_ge(attn2_copied.sem, attn2_copied.at(run))
                pe.wait_ge(own_done.sem, own_done.at(run))
                for g in range(G):
                    mm = pe.matmul(bank_back[0][0:GT, g * E:(g + 1) * E], sel_t[:, g], attn2[:], start=True, stop=True)
                mm.then_inc(scat_done.sem, 1)

            def turn_n3(run):
                pe.wait_ge(n3_ready.sem, n3_ready.at(run))
                turn_tokens(n3, bank_back[0], n3_turned)

            def ff1(run, j):
                if j == 0:
                    pe.wait_ge(n3t_ready.sem, n3t_ready.at(run))
                if j == 2:
                    pe.wait_ge(gelu_done.sem, gelu_done.at(run, 2))
                for n in range(2):
                    m = 2 * j + n
                    for k in range(2):
                        mm = pe.matmul(bank_back[(j + 1) % 2][:, n * RT:(n + 1) * RT], w_ff1[:, k, m * 128:(m + 1) * 128],
                                       n3_t[:, k], start=(k == 0), stop=(k == 1))
                mm.then_inc(ff1_done.sem, 1)

            def ff2(run):
                pe.wait_ge(gelu_done.sem, gelu_done.at(run, 6))
                for g in range(G):
                    for m in range(FC):
                        mm = pe.matmul(bank_back[0][0:GT, g * E:(g + 1) * E], ff_t[:, m, cols_of(g)], w_ff2[:, m, :],
                                       start=(m == 0), stop=(m == FC - 1))
                mm.then_inc(ff2_done.sem, 1)

            def body(back, front):
                b, f = back is not None, front is not None
                if f:
                    tokens(front)
                if b:
                    turn_n2(back)
                if f:
                    turn_n1(front)
                if b:
                    router(back)
                    keys2(back)
                    values2(back)
                if f:
                    for j in range(4):
                        values(front, j)
                if b:
                    gather(back)
                if f:
                    queries_keys(front, 0)
                    queries_keys(front, 1)
                if b:
                    queries2(back)
                if f:
                    queries_keys(front, 2)
                    queries_keys(front, 3)
                if b:
                    scores2(back)
                if f:
                    queries_keys(front, 4)
                    scores(front, 0)
                    queries_keys(front, 5)
                if b:
                    turn_probs2(back)
                if f:
                    scores(front, 1)
                if b:
                    mix_project(back)
                    probs_values2(back)
                if f:
                    turn_probs(front, 0, ctx1_copied, ctx1_copied.at(front, 0))
                    queries_keys(front, 6)
                    probs_values(front, 0)
                    turn_x(front + 1, 0)
                if b:
                    project2(back)
                if f:
                    turn_probs(front, 1, probs_copied, probs_copied.at(front, 1))
                    queries_keys(front, 7)
                    probs_values(front, 1)
                    turn_x(front + 1, 1)
                if b:
                    scatter(back)
                if f:
                    turn_ctx1(front, 0, probs_copied, probs_copied.at(front, 2))
                    scores(front, 2)
                    turn_x(front + 1, 2)
                    turn_ctx1(front, 1, ctx1_copied, ctx1_copied.at(front, 1))
                    scores(front, 3)
                    turn_x(front + 1, 3)
                if b:
                    turn_n3(back)
                if f:
                    turn_probs(front, 2, ctx1_copied, ctx1_copied.at(front, 2))
                    probs_values(front, 2)
                    turn_probs(front, 3, probs_copied, probs_copied.at(front, 3))
                if b:
                    ff1(back, 0)
                    ff1(back, 1)
                if f:
                    probs_values(front, 3)
                if b:
                    ff1(back, 2)
                if f:
                    turn_ctx1(front, 2, probs_copied, probs_copied.at(front, 4))
                    turn_ctx1(front, 3, ctx1_copied, ctx1_copied.at(front, 3))
                if b:
                    ff2(back)
                if f:
                    project1(front)

            pe.wait_ge(ld_tok, LD_TOK)
            for j in range(PC // 2):
                if j >= 2:
                    pe.wait_ge(wt_copied, j - 1)
                for n in range(2):
                    for k in range(2):
                        mm = pe.transpose(bank_proj[j % 2][:, n * E + k * EC:n * E + (k + 1) * EC],
                                          w_raw[:, k, (2 * j + n) * 128:(2 * j + n + 1) * 128], ident[0:EC, 0:EC])
                mm.then_inc(wt_turned, 1)
            for j in range(4):
                turn_x(0, j)
            pe.wait_ge(ld_back, LD_BACK)
            for k in range(2):
                pe.transpose(bank_turn[0:EC, k * 8:(k + 1) * 8], vec_rows[:, half(k)], ident[0:8, 0:8])
            pe.transpose(bank_turn[:, 16:16 + FC], b_ff1_rows[:], ident[0:FC, 0:FC]).then_inc(cols_turned, 1)
            pe.wait_ge(rel_summed, 1)
            pe.wait_ge(place_ready, 1)
            for k in range(TOK):
                mm = pe.matmul(bank_score[0:GT, k * H1:(k + 1) * H1], place[:, TOK - 1 - k],
                               rel_sum[:], start=True, stop=True)
            mm.then_inc(rel_placed, 1)
            pe.wait_ge(wt_copied, PC // 2)
            pe.wait_ge(bias_ready, GB)
            pe.wait_ge(pos_ready, 1)
            pe.wait_ge(wr_ready, 2)
            pe.wait_ge(ld_back, LD_BACK)
            pe.wait_ge(zeroed, 7)
            body(None, 0)
            with pe.Fori(0, RUNS - 1) as i:
                body(i, i + 1)
            body(RUNS - 1, None)


LD_TOK = 16 * (2 + 3 * GB)
LD_ATTN = 16 * (2 * 3 + 2)
LD_BACK = 16 * (7 + 8 + 5)


def constants():
    import numpy as np

    c = np.zeros((128, CONST_COLS), np.float32)

    def put(name, x):
        lo, hi = CONST[name]
        c[0:x.shape[0], lo:hi] = x

    t = np.arange(GT)
    same = t[:, None] // TOK == t[None, :] // TOK
    put("ident", np.eye(128, dtype=np.float32))
    put("same", same.astype(np.float32))
    put("lower", (same & (t[None, :] < t[:, None])).astype(np.float32))
    put("apart", np.where(t[:, None] // TOK == np.arange(GB)[None, :], 0.0, NEG).astype(np.float32))
    s = np.arange(GS)
    put("slot", np.where(t[:, None] // TOK == s[None, :] // SEL, s[None, :] % SEL, -1).astype(np.float32))
    put("headmask", (np.arange(EC)[:, None] // D2 == np.arange(HC)[None, :]).astype(np.float32))
    q = np.arange(HC * GS) % GS
    put("apart2", np.where(q[:, None] // SEL == t[None, :] // TOK, 0.0, NEG).astype(np.float32))
    r = np.arange(REL)
    put("shift", (r[:, None] + r[None, :] == REL - 1).astype(np.float32))
    return c


_INS = ["x", "cls_tok", "L0_tok_W", "L0_tok_b", "L0_tok_pos_embed", "L0_attn_w_q", "L0_attn_w_k", "L0_attn_w_v",
        "L0_attn_w_o", "L0_attn_rel_emb"] + ["L0_ffn_" + n for n in (
            "g1", "b1", "g2", "b2", "Wr", "br", "Wq", "bq", "Wk", "bk", "Wv", "bv", "Wo", "bo", "Wm", "bm", "W1", "bf1",
            "W2", "bf2")]


def kernel(**inputs):
    import numpy as _np
    import concourse.bacc as _bacc
    from concourse import mybir as _mybir
    from concourse.bass_utils import run_bass_kernel_spmd as _run

    nc = _bacc.Bacc("TRN2", target_bir_lowering=False, num_devices=1)
    arrays, aps = {}, {}
    for name in _INS + ["consts"]:
        v = constants() if name == "consts" else _np.ascontiguousarray(inputs[name])
        if v.ndim == 0:
            v = v.reshape(1)
        arrays[f"in_{name}_dram"] = v
        aps[name] = nc.dram_tensor(f"in_{name}_dram", v.shape, _mybir.dt.from_np(v.dtype), kind="ExternalInput").ap()
    aps["out"] = nc.dram_tensor("out_0_dram", (BATCH, TOK, E), F32, kind="ExternalOutput").ap()
    vit_block(nc, aps)
    r = _run(nc, [arrays], core_ids=[0])
    return r.results[0]["out_0_dram"]
```

```python
from contextlib import ExitStack

import concourse.bass as bass
from concourse import mybir

F32 = mybir.dt.float32
ALU = mybir.AluOpType
ACT = mybir.ActivationFunctionType
AX_X = mybir.AxisListType.X

BATCH, CHANNELS, SIDE, PATCH = 64, 3, 96, 16
HP = SIDE // PATCH
NP = HP * HP
TOK = NP + 1
E = 192
EC = E // 2
GB = 3
GT = GB * TOK
G = 2
RB = G * GB
RT = G * GT
RUNS = -(-BATCH // RB)
LAST_B = BATCH - (RUNS - 1) * RB
PD = CHANNELS * PATCH * PATCH
PC = PD // 128
H1, D1 = 8, 96
QUAD = 4
UNITS = (H1 // QUAD) * G
H2, D2 = 12, 16
HC = EC // D2
SEL = 6
GS = GB * SEL
RS = G * GS
FF = 768
FC = FF // 128
MAX_DIST = 100
REL = 2 * TOK - 1
EPS = 1e-5
NEG = -1e30
XP = CHANNELS * RB * HP
TW = HP // 2

CONST = {}
_at = 0
for _name, _n in (("ident", 128), ("same", GT), ("lower", GT), ("apart", GB), ("slot", GS),
                  ("headmask", HC), ("apart2", GT), ("shift", REL)):
    CONST[_name] = (_at, _at + _n)
    _at += _n
CONST_COLS = _at


class Signal:

    def __init__(self, sem, per_run, early):
        self.sem, self.per_run, self.early = sem, per_run, early

    def at(self, run, k=None):
        return (run + self.early) * self.per_run + (self.per_run if k is None else k)

    def before(self, run):
        assert self.early
        return run * self.per_run + self.per_run


def vit_block(nc, a):
    with ExitStack() as ctx:
        def sb(name, shape):
            return ctx.enter_context(nc.sbuf_tensor(name, shape, F32))

        def bank(name):
            return ctx.enter_context(nc.psum_tensor(name, [128, 512], F32))

        def sem(name):
            return ctx.enter_context(nc.semaphore(name))

        def signal(name, per_run=1, early=0):
            return Signal(sem(name), per_run, early)

        const = sb("const", [128, CONST_COLS])

        def cst(name, p=128):
            lo, hi = CONST[name]
            return const[0:p, lo:hi]

        ident = cst("ident")
        w_raw = sb("w_raw", [EC, 2, PD])
        w_tok = sb("w_tok", [128, PC, E])
        pos_tok = sb("pos_tok", [GT, E])
        b_tok = sb("b_tok", [GT, E])
        w_q = sb("w_q", [EC, 2, H1, D1])
        w_k = sb("w_k", [EC, 2, H1, D1])
        w_v = sb("w_v", [EC, 2, H1 * D1])
        w_o = sb("w_o", [128, FC, E])
        rel = sb("rel", [REL, H1, D1])
        place = sb("place", [REL, TOK, GT])
        rel_sum = sb("rel_sum", [REL, H1])
        pos_bias = sb("pos_bias", [GT, H1, GT])
        cols = sb("cols", [EC, 8, 2])
        g1, b1, g2, b2, bq, bk, bv, wr = (cols[:, n, :] for n in range(8))
        vec_rows = sb("vec_rows", [8, E])
        b_ff1_rows = sb("b_ff1_rows", [FC, 128])
        wr_all = sb("wr_all", [EC, 2, GT])
        br_neg = sb("br_neg", [GT, 1])
        b_ff1 = sb("b_ff1", [128, FC])
        b_ff2 = sb("b_ff2", [GT, E])
        w_q2 = sb("w_q2", [EC, 2, E])
        w_k2 = sb("w_k2", [EC, 2, E])
        w_v2 = sb("w_v2", [EC, 2, E])
        w_o2 = sb("w_o2", [EC + 1, 2, E])
        w_m = sb("w_m", [EC + 1, 2, E])
        w_ff1 = sb("w_ff1", [EC, 2, FF])
        w_ff2 = sb("w_ff2", [128, FC, E])
        power = sb("power", [GT, G])
        zero = sb("zero", [GT, G, E])
        power2 = sb("power2", [GT, 2, G])

        x_rows = sb("x_rows", [XP, PATCH, HP, PATCH])
        x_split = sb("x_split", [XP, HP, PATCH * PATCH])
        x_t = sb("x_t", [128, PC, RT])
        h = sb("h", [GT, G, E])
        stats1 = sb("stats1", [GT, G, 6])
        mv1 = sb("mv1", [GT, G, 2])
        ve1 = sb("ve1", [GT, G])
        rstd1 = sb("rstd1", [GT, G])
        n1 = sb("n1", [GT, G, E])
        n1_t = sb("n1_t", [EC, 2, RT])
        qk = sb("qk", [D1, H1, 2, RT])
        v = sb("v", [GT, G, H1, D1 + 1])
        logits = sb("logits", [GT, 2, QUAD, GT])
        rowmax = sb("rowmax", [GT, 2, QUAD])
        shifted = sb("shifted", [GT, 2, QUAD, GT])
        probs = sb("probs", [GT, 2, QUAD, GT])
        probs_t = sb("probs_t", [GT, 2, QUAD, GT])
        den_inv = sb("den_inv", [GT, UNITS, QUAD])
        ctx1 = sb("ctx1", [GT, G, H1, D1])
        ctx1_t = sb("ctx1_t", [128, FC, RT])
        h_keep = sb("h_keep", [GT, G, E])
        h2 = sb("h2", [GT, G, E])

        stats2 = sb("stats2", [GT, G, 6])
        mv2 = sb("mv2", [GT, G, 2])
        ve2 = sb("ve2", [GT, 2, G])
        rstd2 = sb("rstd2", [GT, 2, G])
        n2 = sb("n2", [GT, G, E])
        nn2 = sb("nn2", [GT, G, E])
        n2_t = sb("n2_t", [EC, 2, RT])
        score_e = sb("score_e", [GT, RT])
        score_d = sb("score_d", [GT, RT])
        score = sb("score", [GT, RT])
        junk = sb("junk", [GT, 4, GT])
        score_col = sb("score_col", [GT, G])
        less = sb("less", [GT, G, GT])
        tied = sb("tied", [GT, G, GT])
        rank = sb("rank", [GT, G])
        sel = sb("sel", [GT, G, RS])
        sel_t = sb("sel_t", [RS, G, GT])
        unrouted = sb("unrouted", [GT, G])
        s_sum = sb("s_sum", [EC, RB])
        s_eps = sb("s_eps", [EC, RB])
        s_inv = sb("s_inv", [EC, RB])
        weighted = sb("weighted", [EC, 2, RT])
        pooled = sb("pooled", [EC, 2, RB])
        pooled_n = sb("pooled_n", [EC, 2, RB])
        spread = sb("spread", [EC, 2, RT])
        mix_t = sb("mix_t", [EC + 1, 2, RT])
        k2_t = sb("k2_t", [EC, 2, RT])
        v2 = sb("v2", [GT, G, E])
        nsel_t = sb("nsel_t", [EC, 2, RS])
        q2_t = sb("q2_t", [EC, 2, RS])
        q2_heads = sb("q2_heads", [EC, 2, G, HC, GS])
        logits2 = sb("logits2", [HC * GS, 4, GT])
        negmax2 = sb("negmax2", [HC * GS, 4])
        exp2 = sb("exp2", [HC * GS, 4, GT])
        den2 = sb("den2", [HC * GS, 4])
        den2_inv = sb("den2_inv", [HC * GS, 4])
        probs2 = sb("probs2", [HC * GS, 4, GT])
        probs2_t = sb("probs2_t", [GT, 4, HC * GS])
        own = sb("own", [EC, 4, HC, GS])
        ctx2 = sb("ctx2", [EC, 4, GS])
        ctx2_t = sb("ctx2_t", [EC + 1, 2, RS])
        attn2 = sb("attn2", [RS, E])
        mixed = sb("mixed", [GT, G, E])
        h3 = sb("h3", [GT, G, E])
        h2_b = sb("h2_b", [GT, G, E])
        h3_b = sb("h3_b", [GT, G, E])
        stats3 = sb("stats3", [GT, G, 6])
        mv3 = sb("mv3", [GT, G, 2])
        ve3 = sb("ve3", [GT, G])
        rstd3 = sb("rstd3", [GT, G])
        n3 = sb("n3", [GT, G, E])
        n3_t = sb("n3_t", [EC, 2, RT])
        ff_t = sb("ff_t", [128, FC, RT])
        y = sb("y", [GT, G, E])

        bank_proj = [bank("bank_proj0"), bank("bank_proj1")]
        bank_score = bank("bank_score")
        bank_turn = bank("bank_turn")
        bank_pv = bank("bank_pv")
        bank_front = bank("bank_front")
        bank_back = [bank("bank_back0"), bank("bank_back1")]

        ld_tok, ld_attn, ld_back = sem("ld_tok"), sem("ld_attn"), sem("ld_back")
        zeroed = sem("zeroed")
        wt_turned, wt_copied = sem("wt_turned"), sem("wt_copied")
        pos_ready = sem("pos_ready")
        rel_summed, rel_placed, bias_ready = sem("rel_summed"), sem("rel_placed"), sem("bias_ready")
        vector_passed, pool_passed = sem("vector_passed"), sem("pool_passed")
        place_ready = sem("place_ready")
        cols_turned, cols_ready = sem("cols_turned"), sem("cols_ready")
        wr_ready, power_ready = sem("wr_ready"), sem("power_ready")

        x_loaded = sem("x_loaded")
        x_split_done = signal("x_split_done")
        x_turned = signal("x_turned", 4)
        x_copied = signal("x_copied", 4 * CHANNELS)
        tok_done = signal("tok_done")
        h_ready = signal("h_ready")
        stats1_done, mv1_done = signal("stats1_done", 2), signal("mv1_done", 2)
        ve1_done, rstd1_done = signal("ve1_done"), signal("rstd1_done")
        n1_ready = signal("n1_ready", 2)
        n1_turned, n1_copied = signal("n1_turned"), signal("n1_copied")
        v_done, v_copied = signal("v_done", 4), signal("v_copied", 4)
        qk_done, qk_copied = signal("qk_done", H1), signal("qk_copied", H1, 1)
        score_done, logits_ready = signal("score_done", UNITS), signal("logits_ready", UNITS, 1)
        rowmax_done, shifted_done = signal("rowmax_done", UNITS), signal("shifted_done", UNITS)
        probs_ready = signal("probs_ready", UNITS)
        probs_turned, probs_copied = signal("probs_turned", UNITS), signal("probs_copied", UNITS)
        pv_done = signal("pv_done", UNITS)
        den_done, ctx1_ready = signal("den_done", UNITS), signal("ctx1_ready", UNITS, 1)
        ctx1_turned, ctx1_copied = signal("ctx1_turned", UNITS), signal("ctx1_copied", UNITS, 1)
        h_kept = signal("h_kept")
        wo_done, h2_ready = signal("wo_done"), signal("h2_ready", 1, 1)

        stats2_done, mv2_done = signal("stats2_done", 2), signal("mv2_done", 2)
        ve2_done, rstd2_done = signal("ve2_done", 2), signal("rstd2_done")
        n2_ready, nn2_ready = signal("n2_ready", 2), signal("nn2_ready", 2)
        n2_turned, n2t_ready = signal("n2_turned"), signal("n2t_ready", 2)
        z_done, score_exp, score_step = signal("z_done"), signal("score_exp"), signal("score_step", 2)
        col_done, cmp_done = signal("col_done", 2), signal("cmp_done", 4)
        rank_done, sel_ready, unrouted_ready = signal("rank_done", 2), signal("sel_ready", 2), signal("unrouted_ready", 2)
        sum_step = signal("sum_step", 3)
        weighted_done, pool_step, mix_step = signal("weighted_done"), signal("pool_step", 2), signal("mix_step", 2)
        k2_done, k2_copied = signal("k2_done"), signal("k2_copied", 2)
        v2_done, v2_copied = signal("v2_done"), signal("v2_copied")
        gather_done, nsel_ready, selt_copied = signal("gather_done"), signal("nsel_ready", 2), signal("selt_copied")
        q2_done, q2_copied, q2h_ready = signal("q2_done"), signal("q2_copied", 2), signal("q2h_ready", 2)
        s2_done, logits2_ready, max2_done = signal("s2_done"), signal("logits2_ready"), signal("max2_done")
        exp2_done, den2_done, probs2_ready = signal("exp2_done", 4), signal("den2_done"), signal("probs2_ready")
        p2_turned, p2_copied = signal("p2_turned"), signal("p2_copied")
        pv2_done, own_done, ctx2_done, ctx2_ready = signal("pv2_done"), signal("own_done"), signal("ctx2_done"), signal("ctx2_ready")
        ao_done, attn2_copied = signal("ao_done"), signal("attn2_copied")
        scat_done, mix_done = signal("scat_done"), signal("mix_done")
        mixed_done, h3_ready = signal("mixed_done", 2), signal("h3_ready")
        stats3_done, mv3_done = signal("stats3_done", 2), signal("mv3_done", 2)
        h2b_ready = signal("h2b_ready")
        ve3_done, rstd3_done, h3b_ready = signal("ve3_done"), signal("rstd3_done"), signal("h3b_ready")
        n3_ready, n3_turned, n3t_ready = signal("n3_ready", 2), signal("n3_turned"), signal("n3t_ready", 2)
        ff1_done, gelu_done = signal("ff1_done", 3), signal("gelu_done", 6)
        ff2_done, y_ready = signal("ff2_done"), signal("y_ready", 1, 1)
        y_stored = signal("y_stored", 16 * G, 1)

        def cols_of(g):
            return slice(g * GT, (g + 1) * GT)

        def half(k):
            return slice(k * EC, (k + 1) * EC)

        def exists(run):
            return type(run) is not int or 0 <= run < RUNS

        UNIT = [(quad, g) for quad in range(H1 // QUAD) for g in range(G)]

        block = ctx.enter_context(nc.Block())

        @block.sync
        def _(sp):
            sp.sem_inc(y_stored.sem, y_stored.per_run)

            def load_x(first, images):
                for c in range(CHANNELS):
                    sp.dma_start(
                        x_rows[c * RB * HP:c * RB * HP + images * HP].rearrange("p a w b -> p (a w b)"),
                        a["x"][bass.ds(first, images), c].rearrange("b (r q) w -> b r (q w)", q=PATCH),
                    ).then_inc(x_loaded, 16)

            def store(run, first, images):
                sp.wait_ge(y_ready.sem, y_ready.at(run))
                out = a["out"].rearrange("b t e -> (b t) e")
                for g in range(-(-images // GB)):
                    n = min(GB, images - g * GB) * TOK
                    sp.dma_start(out[bass.ds(first * TOK + g * GT, n)], y[0:n, g]).then_inc(y_stored.sem, 16)

            load_x(0, RB)
            sp.dma_start(const[:], a["consts"]).then_inc(ld_tok, 16)
            sp.dma_start(w_raw[:], a["L0_tok_W"].rearrange("(k e) d -> e k d", e=EC)).then_inc(ld_tok, 16)
            sp.wait_ge(zeroed, 2)
            for b in range(GB):
                rows = slice(b * TOK + 1, (b + 1) * TOK)
                sp.dma_start(pos_tok[rows], a["L0_tok_pos_embed"][0]).then_inc(ld_tok, 16)
                sp.dma_start(pos_tok[b * TOK:b * TOK + 1], a["cls_tok"][0]).then_inc(ld_tok, 16)
                sp.dma_start(b_tok[rows], a["L0_tok_b"].rearrange("(o e) -> o e", o=1).broadcast_to([NP, E])).then_inc(ld_tok, 16)
            for w, name in ((w_v, "w_v"), (w_q, "w_q"), (w_k, "w_k")):
                src = a["L0_attn_" + name].rearrange("h (k e) d -> k e h d", e=EC)
                for k in range(2):
                    dst = w[:, k] if len(w.shape) == 4 else w[:, k].rearrange("p (h d) -> p h d", h=H1)
                    sp.dma_start(dst, src[k]).then_inc(ld_attn, 16)
            for w, name in ((w_q2, "Wq"), (w_k2, "Wk"), (w_v2, "Wv"), (w_o2, "Wo"), (w_m, "Wm"), (w_ff1, "W1")):
                sp.dma_start(w[0:EC], a["L0_ffn_" + name].rearrange("(k e) d -> e k d", e=EC)).then_inc(ld_back, 16)
            sp.dma_start(w_ff2[:], a["L0_ffn_W2"].rearrange("(k e) d -> e k d", e=128)).then_inc(ld_back, 16)

            def reload_x(run, images):
                sp.wait_ge(x_split_done.sem, x_split_done.at(run - 1))
                load_x(run * RB, images)

            reload_x(1, RB)
            reload_x(2, RB)
            with sp.Fori(0, RUNS - 4) as i:
                reload_x(i + 3, RB)
                store(i, i * RB, RB)
            reload_x(RUNS - 1, LAST_B)
            for run in range(RUNS - 4, RUNS):
                store(run, run * RB, RB if run < RUNS - 1 else LAST_B)
            sp.wait_ge(y_stored.sem, y_stored.at(RUNS - 1))

        @block.gpsimd
        def _(pool):
            pool.memset(power[:], -0.5).then_inc(power_ready, 1)
            pool.memset(power2[:], -0.5).then_inc(power_ready, 1)
            pool.memset(zero[:], 0.0).then_inc(power_ready, 1)
            pool.wait_ge(power_ready, 3)

            def keep_h(run):
                pool.wait_ge(h_ready.sem, h_ready.at(run))
                pool.tensor_tensor(h_keep[:], h[:], zero[:], ALU.add).then_inc(h_kept.sem, 1)

            def ln1(run):
                pool.wait_ge(ve1_done.sem, ve1_done.at(run))
                pool.tensor_tensor(rstd1[:], ve1[:], power[:], ALU.pow).then_inc(rstd1_done.sem, 1)

            def shift(run, u):
                pool.wait_ge(rowmax_done.sem, rowmax_done.at(run, u + 1))
                if u >= 2:
                    pool.wait_ge(probs_ready.sem, probs_ready.at(run, u - 1))
                pool.tensor_tensor(shifted[:, u % 2], logits[:, u % 2],
                                   rowmax[:, u % 2].unsqueeze(2).broadcast_to([GT, QUAD, GT]),
                                   ALU.subtract).then_inc(shifted_done.sem, 1)

            def ln2(run):
                pool.wait_ge(ve2_done.sem, ve2_done.at(run))
                pool.tensor_tensor(rstd2[:], ve2[:], power2[:], ALU.pow).then_inc(rstd2_done.sem, 1)

            def outer_residual(run):
                pool.tensor_tensor(h2_b[:], h2[:], b_ff2[:].unsqueeze(1).broadcast_to([GT, G, E]),
                                   ALU.add).then_inc(h2b_ready.sem, 1)

            def weigh(run):
                pool.wait_ge(n2t_ready.sem, n2t_ready.at(run))
                pool.wait_ge(score_step.sem, score_step.at(run))
                pool.tensor_tensor(weighted[:], n2_t[:],
                                   score[0:EC].unsqueeze(1).broadcast_to([EC, 2, RT]),
                                   ALU.mult).then_inc(weighted_done.sem, 1)

            def mix(run):
                pool.wait_ge(pool_step.sem, pool_step.at(run))
                pool.tensor_tensor(spread[:].rearrange("p k (b t) -> p k b t", t=TOK),
                                   pooled_n[:].unsqueeze(3).broadcast_to([EC, 2, RB, TOK]),
                                   score[0:EC].rearrange("p (b t) -> p b t", t=TOK).unsqueeze(1).broadcast_to([EC, 2, RB, TOK]),
                                   ALU.mult).then_inc(mix_step.sem, 1)
                pool.wait_ge(mix_step.sem, mix_step.at(run, 1))
                pool.tensor_tensor(mix_t[0:EC], spread[:], n2_t[:], ALU.add).then_inc(mix_step.sem, 1)

            def norm2(run):
                pool.wait_ge(den2_done.sem, den2_done.at(run))
                pool.wait_ge(exp2_done.sem, exp2_done.at(run))
                pool.tensor_tensor(probs2[:], exp2[:], den2_inv[:].unsqueeze(2).broadcast_to([HC * GS, 4, GT]),
                                   ALU.mult).then_inc(probs2_ready.sem, 1)

            def ln3(run):
                pool.wait_ge(ve3_done.sem, ve3_done.at(run))
                pool.tensor_tensor(rstd3[:], ve3[:], power[:], ALU.pow).then_inc(rstd3_done.sem, 1)

            def add_h3(run):
                pool.wait_ge(h3_ready.sem, h3_ready.at(run))
                pool.wait_ge(h2b_ready.sem, h2b_ready.at(run))
                pool.tensor_tensor(h3_b[:], h3[:], h2_b[:], ALU.add).then_inc(h3b_ready.sem, 1)

            def body(i):
                back, front, ahead = i, i + 1, i + 2
                b, f, a = exists(back), exists(front), exists(ahead)
                if b:
                    weigh(back)
                    mix(back)
                if f:
                    keep_h(front)
                if b:
                    outer_residual(back)
                if f:
                    shift(front, 0)
                if b:
                    norm2(back)
                if f:
                    shift(front, 1)
                    shift(front, 2)
                if b:
                    ln3(back)
                if f:
                    shift(front, 3)
                if b:
                    add_h3(back)
                if a:
                    ln1(ahead)
                if f:
                    ln2(front)

            body(-2)
            pool.wait_ge(ld_back, LD_BACK)
            body(-1)
            with pool.Fori(0, RUNS - 2) as i:
                body(i)
            body(RUNS - 2)
            body(RUNS - 1)

        @block.scalar
        def _(act):
            act.sem_inc(qk_copied.sem, qk_copied.per_run)
            act.sem_inc(ctx1_copied.sem, ctx1_copied.per_run)
            act.dma_start(w_o[:], a["L0_attn_w_o"].rearrange("h d e -> (h d) e").rearrange("(k p) e -> p k e", p=128)).then_inc(ld_attn, 16)
            act.dma_start(rel[:], a["L0_attn_rel_emb"][:, MAX_DIST - TOK:MAX_DIST - TOK + REL].rearrange("h r d o -> r h (d o)")).then_inc(ld_attn, 16)
            for n, name in enumerate(("g1", "b1", "g2", "b2", "bq", "bk", "bv", "Wr")):
                act.dma_start(vec_rows[n:n + 1], a["L0_ffn_" + name].rearrange("(o e) -> o e", o=1)).then_inc(ld_back, 16)
            act.dma_start(br_neg[:], a["L0_ffn_br"].rearrange("(o e) -> o e", o=1).broadcast_to([GT, 1])).then_inc(ld_back, 16)
            act.dma_start(b_ff1_rows[:], a["L0_ffn_bf1"].rearrange("(m p) -> m p", p=128)).then_inc(ld_back, 16)
            act.dma_start(b_ff2[:], a["L0_ffn_bf2"].rearrange("(o e) -> o e", o=1).broadcast_to([GT, E])).then_inc(ld_back, 16)
            act.dma_start(w_o2[EC:EC + 1, 1], a["L0_ffn_bo"].rearrange("(o e) -> o e", o=1)).then_inc(ld_back, 16)
            act.dma_start(w_m[EC:EC + 1, 1], a["L0_ffn_bm"].rearrange("(o e) -> o e", o=1)).then_inc(ld_back, 16)

            def copy_x(run, j):
                hf, tri = j // 2, j % 2
                act.wait_ge(x_turned.sem, x_turned.at(run, j + 1))
                src = bank_front[:, 0:TW * XP].rearrange("p (w q) -> p w q", w=TW)
                for c in range(CHANNELS):
                    dst = x_t[:, 2 * c + hf].rearrange("p (b t) -> p b t", t=TOK)[:, :, 1:]
                    dst = dst.rearrange("p b (r w) -> p b r w", w=HP)[:, :, :, tri * TW:(tri + 1) * TW]
                    s = src[:, :, c * RB * HP:(c + 1) * RB * HP].rearrange("p w (b r) -> p b r w", r=HP)
                    act.copy(dst, s).then_inc(x_copied.sem, 1)

            def copy_n1(run):
                act.wait_ge(n1_turned.sem, n1_turned.at(run))
                act.copy(n1_t[:].rearrange("p k t -> p (k t)"), bank_front[0:EC, 0:2 * RT]).then_inc(n1_copied.sem, 1)

            def copy_v(run, j):
                g, part = j // 2, j % 2
                act.wait_ge(v_done.sem, v_done.at(run, j + 1))
                act.copy(v[:, g, part * QUAD:(part + 1) * QUAD, 0:D1],
                         bank_proj[j % 2][0:GT, 0:QUAD * D1].rearrange("p (h d) -> p h d", h=QUAD)).then_inc(v_copied.sem, 1)

            def copy_qk(run, hd):
                act.wait_ge(qk_done.sem, qk_done.at(run, hd + 1))
                act.copy(qk[:, hd].rearrange("p a t -> p (a t)"), bank_proj[hd % 2][0:D1, 0:2 * RT]).then_inc(qk_copied.sem, 1)

            def exp1(run, u):
                act.wait_ge(shifted_done.sem, shifted_done.at(run, u + 1))
                act.activation(probs[:, u % 2], shifted[:, u % 2], ACT.Exp).then_inc(probs_ready.sem, 1)

            def copy_probs(run, u):
                act.wait_ge(probs_turned.sem, probs_turned.at(run, u + 1))
                act.copy(probs_t[:, u % 2].rearrange("p h t -> p (h t)"), bank_turn[0:GT, 0:QUAD * GT]).then_inc(probs_copied.sem, 1)

            def copy_ctx1(run, u):
                quad, g = UNIT[u]
                act.wait_ge(ctx1_turned.sem, ctx1_turned.at(run, u + 1))
                act.copy(ctx1_t[:, 3 * quad:3 * quad + 3, cols_of(g)],
                         bank_turn[:, 0:3 * GT].rearrange("p (k t) -> p k t", k=3)).then_inc(ctx1_copied.sem, 1)

            def exp_score(run):
                act.wait_ge(z_done.sem, z_done.at(run))
                act.activation(score_e[:], bank_back[0][0:GT, 0:RT], ACT.Exp, bias=br_neg[:], scale=-1.0).then_inc(score_exp.sem, 1)

            def copy_k2(run):
                act.wait_ge(k2_done.sem, k2_done.at(run))
                for k in range(2):
                    act.activation(k2_t[:, k], bank_back[1][0:EC, k * RT:(k + 1) * RT], ACT.Identity,
                                   bias=bk[:, k:k + 1]).then_inc(k2_copied.sem, 1)

            def copy_v2(run):
                act.wait_ge(v2_done.sem, v2_done.at(run))
                act.copy(v2[:].rearrange("p g e -> p (g e)"), bank_back[0][0:GT, 0:G * E]).then_inc(v2_copied.sem, 1)

            def copy_q2(run):
                act.wait_ge(q2_done.sem, q2_done.at(run))
                for k in range(2):
                    act.activation(q2_t[:, k], bank_back[0][0:EC, k * RS:(k + 1) * RS], ACT.Identity,
                                   bias=bq[:, k:k + 1]).then_inc(q2_copied.sem, 1)

            def exp_2(run):
                act.wait_ge(max2_done.sem, max2_done.at(run))
                for j in range(4):
                    act.activation(exp2[:, j], logits2[:, j], ACT.Exp, bias=negmax2[:, j:j + 1],
                                   accum_out=den2[:, j:j + 1]).then_inc(exp2_done.sem, 1)

            def copy_p2(run):
                act.wait_ge(p2_turned.sem, p2_turned.at(run))
                act.copy(probs2_t[:].rearrange("p j t -> p (j t)"), bank_back[0][0:GT, 0:4 * HC * GS]).then_inc(p2_copied.sem, 1)

            def copy_attn2(run):
                act.wait_ge(ao_done.sem, ao_done.at(run))
                act.copy(attn2[:], bank_back[0][0:RS, 0:E]).then_inc(attn2_copied.sem, 1)

            def gelu(run, first):
                for m in range(first, first + 2):
                    if m % 2 == 0:
                        act.wait_ge(ff1_done.sem, ff1_done.at(run, m // 2 + 1))
                    act.activation(ff_t[:, m], bank_back[(m // 2 + 1) % 2][:, (m % 2) * RT:(m % 2 + 1) * RT], ACT.Gelu,
                                   bias=b_ff1[:, m:m + 1]).then_inc(gelu_done.sem, 1)

            def body(i):
                back, front, ahead = i, i + 1, i + 2
                b, f, a = exists(back), exists(front), exists(ahead)
                if f:
                    copy_v(front, 0)
                if b:
                    exp_score(back)
                    copy_k2(back)
                if f:
                    copy_v(front, 1)
                if b:
                    copy_v2(back)
                if f:
                    copy_v(front, 2)
                    copy_v(front, 3)
                if a:
                    copy_x(ahead, 0)
                if f:
                    copy_qk(front, 0)
                    copy_qk(front, 1)
                if a:
                    copy_x(ahead, 1)
                if f:
                    copy_qk(front, 2)
                if b:
                    copy_q2(back)
                if f:
                    copy_qk(front, 3)
                if a:
                    copy_x(ahead, 2)
                if b:
                    exp_2(back)
                if f:
                    copy_qk(front, 4)
                    exp1(front, 0)
                if a:
                    copy_x(ahead, 3)
                if f:
                    copy_qk(front, 5)
                if b:
                    copy_p2(back)
                if f:
                    copy_probs(front, 0)
                    exp1(front, 1)
                    copy_qk(front, 6)
                    copy_probs(front, 1)
                    copy_qk(front, 7)
                if b:
                    copy_attn2(back)
                if f:
                    copy_ctx1(front, 0)
                    exp1(front, 2)
                    copy_ctx1(front, 1)
                    copy_probs(front, 2)
                    exp1(front, 3)
                if b:
                    gelu(back, 0)
                    gelu(back, 2)
                if f:
                    copy_probs(front, 3)
                    copy_ctx1(front, 2)
                if a:
                    copy_n1(ahead)
                if b:
                    gelu(back, 4)
                if f:
                    copy_ctx1(front, 3)

            act.wait_ge(zeroed, 6)
            body(-2)
            body(-1)
            with act.Fori(0, RUNS - 2) as i:
                body(i)
            body(RUNS - 2)
            body(RUNS - 1)

        @block.vector
        def _(dve):
            dve.memset(pos_tok[:], 0.0).then_inc(zeroed, 1)
            dve.memset(b_tok[:], 0.0).then_inc(zeroed, 1)
            dve.memset(x_t[:], 0.0).then_inc(zeroed, 1)
            dve.memset(sel[:], 0.0).then_inc(zeroed, 1)
            dve.memset(v[:, :, :, D1:D1 + 1], 1.0).then_inc(zeroed, 1)
            dve.memset(mix_t[EC:EC + 1], 1.0).then_inc(zeroed, 1)
            dve.memset(ctx2_t[EC:EC + 1], 1.0).then_inc(zeroed, 1)
            for s in (logits_ready, ctx1_ready, h2_ready, y_ready):
                dve.sem_inc(s.sem, s.per_run)
            for j in range(PC // 2):
                dve.wait_ge(wt_turned, j + 1)
                dve.tensor_copy(w_tok[:, 2 * j:2 * j + 2, :].rearrange("p c e -> p (c e)"),
                                bank_proj[j % 2][:, 0:2 * E]).then_inc(wt_copied, 1)
            dve.wait_ge(ld_tok, LD_TOK)
            dve.tensor_tensor(pos_tok[:], pos_tok[:], b_tok[:], ALU.add).then_inc(pos_ready, 1)
            shift_ap = cst("shift", REL)
            dve.tensor_copy(place[:].rearrange("p n (b q) -> p n b q", b=GB),
                            bass.AP(tensor=shift_ap.tensor, offset=shift_ap.offset,
                                    ap=[shift_ap.ap[0], [1, TOK], [0, GB], [1, TOK]])).then_inc(place_ready, 1)
            def stats(run, src, st, mv, s_st, s_mv):
                for g in range(G):
                    dve.bn_stats(st[:, g], src[:, g]).then_inc(s_st.sem, 1)
                for g in range(G):
                    dve.wait_ge(s_st.sem, s_st.at(run, g + 1))
                    dve.sem_inc(vector_passed, 1)
                    dve.bn_aggr(mv[:, g], st[:, g]).then_inc(s_mv.sem, 1)

            def standardise(dst, src, mv, rstd, done):
                for g in range(G):
                    dve.tensor_scalar(dst[:, g], src[:, g], mv[:, g, 0:1], rstd[:, g:g + 1],
                                      ALU.subtract, ALU.mult).then_inc(done.sem, 1)

            def with_eps(run, ve, mv, s_mv, done):
                dve.wait_ge(s_mv.sem, s_mv.at(run))
                dve.tensor_scalar(ve, mv[:, :, 1], EPS, None, ALU.add).then_inc(done.sem, 1)

            def ln2_stats(run):
                dve.wait_ge(h2_ready.sem, h2_ready.at(run))
                stats(run, h2, stats2, mv2, stats2_done, mv2_done)
                with_eps(run, ve2[:, 0], mv2, mv2_done, ve2_done)
                dve.tensor_scalar(ve2[:, 1], mv2[:, :, 1], 1.0 + EPS, EPS * EPS, ALU.mult, ALU.add).then_inc(ve2_done.sem, 1)

            def ln2_norm(run):
                dve.wait_ge(rstd2_done.sem, rstd2_done.at(run))
                standardise(nn2, h2, mv2, rstd2[:, 1], nn2_ready)

            def ln2_first(run):
                standardise(n2, h2, mv2, rstd2[:, 0], n2_ready)

            def add_pos(run):
                dve.wait_ge(tok_done.sem, tok_done.at(run))
                if type(run) is not int or run > 0:
                    dve.wait_ge(h_kept.sem, h_kept.at(run - 1))
                dve.tensor_tensor(h[:], bank_front[0:GT, 0:G * E].rearrange("p (g e) -> p g e", g=G),
                                  pos_tok[:].unsqueeze(1).broadcast_to([GT, G, E]), ALU.add).then_inc(h_ready.sem, 1)

            def ln1_stats(run):
                dve.wait_ge(h_ready.sem, h_ready.at(run))
                stats(run, h, stats1, mv1, stats1_done, mv1_done)
                with_eps(run, ve1[:], mv1, mv1_done, ve1_done)

            def ln1_norm(run):
                dve.wait_ge(rstd1_done.sem, rstd1_done.at(run))
                standardise(n1, h, mv1, rstd1, n1_ready)

            def gain(run, turned, src_bank, dst, gg, bb, done):
                dve.wait_ge(turned.sem, turned.at(run))
                for k in range(2):
                    dve.tensor_scalar(dst[:, k], src_bank[0:EC, k * RT:(k + 1) * RT], gg[:, k:k + 1], bb[:, k:k + 1],
                                      ALU.mult, ALU.add).then_inc(done.sem, 1)

            def route(run):
                dve.wait_ge(score_exp.sem, score_exp.at(run))
                dve.tensor_scalar(score_d[:], score_e[:], 1.0, None, ALU.add).then_inc(score_step.sem, 1)
                dve.wait_ge(score_step.sem, score_step.at(run, 1))
                dve.reciprocal(score[:], score_d[:]).then_inc(score_step.sem, 1)
                dve.wait_ge(score_step.sem, score_step.at(run, 2))
                for g in range(G):
                    dve.tensor_tensor_reduce(out=junk[:, g], in0=score[:, cols_of(g)], in1=ident[0:GT, 0:GT], scale=1.0,
                                             scalar=0.0, op0=ALU.mult, op1=ALU.add,
                                             accum_out=score_col[:, g:g + 1]).then_inc(col_done.sem, 1)
                dve.tensor_reduce(s_sum[:], score[0:EC].rearrange("p (b t) -> p b t", t=TOK), AX_X, ALU.add).then_inc(sum_step.sem, 1)
                for g in range(G):
                    dve.wait_ge(col_done.sem, col_done.at(run, g + 1))
                    dve.scalar_tensor_tensor(out=less[:, g], in0=score[:, cols_of(g)], scalar=score_col[:, g:g + 1],
                                             in1=cst("same", GT), op0=ALU.is_lt, op1=ALU.mult).then_inc(cmp_done.sem, 1)
                    dve.scalar_tensor_tensor(out=tied[:, g], in0=score[:, cols_of(g)], scalar=score_col[:, g:g + 1],
                                             in1=cst("lower", GT), op0=ALU.is_equal, op1=ALU.mult).then_inc(cmp_done.sem, 1)
                dve.wait_ge(sum_step.sem, sum_step.at(run, 1))
                dve.tensor_scalar(s_eps[:], s_sum[:], 1e-6, None, ALU.add).then_inc(sum_step.sem, 1)
                for g in range(G):
                    dve.wait_ge(cmp_done.sem, cmp_done.at(run, 2 * g + 2))
                    dve.sem_inc(vector_passed, 1)
                    dve.tensor_tensor_reduce(out=junk[:, 2 + g], in0=less[:, g], in1=tied[:, g], scale=1.0, scalar=0.0,
                                             op0=ALU.add, op1=ALU.add, accum_out=rank[:, g:g + 1]).then_inc(rank_done.sem, 1)
                dve.wait_ge(sum_step.sem, sum_step.at(run, 2))
                dve.reciprocal(s_inv[:], s_eps[:]).then_inc(sum_step.sem, 1)
                for g in range(G):
                    dve.wait_ge(rank_done.sem, rank_done.at(run, g + 1))
                    dve.tensor_scalar(sel[:, g, g * GS:(g + 1) * GS], cst("slot", GT), rank[:, g:g + 1], None,
                                      ALU.is_equal).then_inc(sel_ready.sem, 1)
                    dve.tensor_scalar(unrouted[:, g:g + 1], rank[:, g:g + 1], float(SEL), None,
                                      ALU.is_ge).then_inc(unrouted_ready.sem, 1)

            def pool_scores(run):
                dve.wait_ge(weighted_done.sem, weighted_done.at(run))
                dve.tensor_reduce(pooled[:].rearrange("p k b -> p (k b)"), weighted[:].rearrange("p k (b t) -> p (k b) t", t=TOK),
                                  AX_X, ALU.add).then_inc(pool_step.sem, 1)
                dve.wait_ge(pool_step.sem, pool_step.at(run, 1))
                dve.wait_ge(sum_step.sem, sum_step.at(run))
                dve.tensor_tensor(pooled_n[:], pooled[:], s_inv[:].unsqueeze(1).broadcast_to([EC, 2, RB]),
                                  ALU.mult).then_inc(pool_step.sem, 1)

            def split_x(run):
                dve.wait_ge(x_loaded, (run + 1) * 16 * CHANNELS)
                if type(run) is not int or run > 0:
                    dve.wait_ge(x_turned.sem, x_turned.at(run - 1))
                dve.tensor_copy(x_split[:].rearrange("p w (a b) -> p w a b", b=PATCH),
                                x_rows[:].rearrange("p a w b -> p w a b")).then_inc(x_split_done.sem, 1)

            def copy_sel(run):
                gain_src = bank_back[1]
                dve.wait_ge(gather_done.sem, gather_done.at(run))
                for k in range(2):
                    dve.tensor_scalar(nsel_t[:, k], gain_src[0:EC, k * RS:(k + 1) * RS], g1[:, k:k + 1], b1[:, k:k + 1],
                                      ALU.mult, ALU.add).then_inc(nsel_ready.sem, 1)
                dve.tensor_copy(sel_t[:].rearrange("p g t -> p (g t)"), gain_src[0:RS, 128:128 + RT]).then_inc(selt_copied.sem, 1)

            def q2_by_head(run):
                dve.wait_ge(q2_copied.sem, q2_copied.at(run))
                for k in range(2):
                    dve.tensor_tensor(q2_heads[:, k],
                                      q2_t[:, k].rearrange("p (g q) -> p g q", g=G).unsqueeze(2).broadcast_to([EC, G, HC, GS]),
                                      cst("headmask", EC).unsqueeze(1).unsqueeze(3).broadcast_to([EC, G, HC, GS]),
                                      ALU.mult).then_inc(q2h_ready.sem, 1)

            def logits_2(run):
                dve.wait_ge(s2_done.sem, s2_done.at(run))
                dve.scalar_tensor_tensor(out=logits2[:], in0=bank_back[1][0:HC * GS, 0:4 * GT].rearrange("p (j t) -> p j t", j=4),
                                         scalar=float(D2) ** -0.5,
                                         in1=cst("apart2", HC * GS).unsqueeze(1).broadcast_to([HC * GS, 4, GT]),
                                         op0=ALU.mult, op1=ALU.add).then_inc(logits2_ready.sem, 1)
                dve.wait_ge(logits2_ready.sem, logits2_ready.at(run))
                dve.tensor_reduce(negmax2[:], logits2[:], AX_X, ALU.max, negate=True).then_inc(max2_done.sem, 1)

            def den_2(run):
                dve.wait_ge(exp2_done.sem, exp2_done.at(run))
                dve.reciprocal(den2_inv[:], den2[:]).then_inc(den2_done.sem, 1)

            def own_ctx2(run):
                dve.wait_ge(pv2_done.sem, pv2_done.at(run))
                dve.tensor_tensor(own[:], bank_back[1][0:EC, 0:4 * HC * GS].rearrange("p (j h q) -> p j h q", j=4, h=HC),
                                  cst("headmask", EC).unsqueeze(1).unsqueeze(3).broadcast_to([EC, 4, HC, GS]),
                                  ALU.mult).then_inc(own_done.sem, 1)
                dve.wait_ge(own_done.sem, own_done.at(run))
                dve.tensor_reduce(ctx2[:], own[:].rearrange("p j h q -> p j q h"), AX_X, ALU.add).then_inc(ctx2_done.sem, 1)
                dve.wait_ge(ctx2_done.sem, ctx2_done.at(run))
                dve.tensor_tensor(ctx2_t[0:EC], ctx2[:].rearrange("p (k g) q -> p k (g q)", k=2),
                                  bv.unsqueeze(2).broadcast_to([EC, 2, RS]), ALU.add).then_inc(ctx2_ready.sem, 1)

            def softmax1(run, u):
                quad, g = UNIT[u]
                dve.wait_ge(score_done.sem, score_done.at(run, u + 1))
                dve.scalar_tensor_tensor(out=logits[:, u % 2].rearrange("p h t -> p (h t)"), in0=bank_score[0:GT, 0:QUAD * GT],
                                         scalar=float(D1) ** -0.5,
                                         in1=pos_bias[:, quad * QUAD:(quad + 1) * QUAD].rearrange("p h t -> p (h t)"),
                                         op0=ALU.mult, op1=ALU.add).then_inc(logits_ready.sem, 1)
                dve.wait_ge(logits_ready.sem, logits_ready.at(run, u + 1))
                dve.tensor_reduce(rowmax[:, u % 2], logits[:, u % 2], AX_X, ALU.max).then_inc(rowmax_done.sem, 1)

            def normalise1(run, u):
                quad, g = UNIT[u]
                pv = bank_pv[0:GT, 0:QUAD * (D1 + 1)].rearrange("p (h d) -> p h d", h=QUAD)
                dve.wait_ge(pv_done.sem, pv_done.at(run, u + 1))
                dve.reciprocal(den_inv[:, u], pv[:, :, D1]).then_inc(den_done.sem, 1)
                dve.wait_ge(den_done.sem, den_done.at(run, u + 1))
                dve.tensor_tensor(ctx1[:, g, quad * QUAD:(quad + 1) * QUAD], pv[:, :, 0:D1],
                                  den_inv[:, u].unsqueeze(2).broadcast_to([GT, QUAD, D1]), ALU.mult).then_inc(ctx1_ready.sem, 1)

            def ln2_gain(run):
                gain(run, n2_turned, bank_back[1], n2_t, g1, b1, n2t_ready)

            def residual1(run):
                dve.wait_ge(wo_done.sem, wo_done.at(run))
                dve.wait_ge(h_kept.sem, h_kept.at(run))
                dve.tensor_tensor(h2[:].rearrange("p g e -> p (g e)"), bank_front[0:GT, 0:G * E],
                                  h_keep[:].rearrange("p g e -> p (g e)"), ALU.add).then_inc(h2_ready.sem, 1)

            def merge(run):
                dve.wait_ge(n2_ready.sem, n2_ready.at(run))
                dve.wait_ge(mix_done.sem, mix_done.at(run))
                for g in range(G):
                    dve.scalar_tensor_tensor(out=mixed[:, g], in0=bank_back[0][0:GT, g * E:(g + 1) * E], scalar=unrouted[:, g:g + 1],
                                             in1=n2[:, g], op0=ALU.mult, op1=ALU.add).then_inc(mixed_done.sem, 1)

            def residual2(run):
                dve.wait_ge(scat_done.sem, scat_done.at(run))
                dve.wait_ge(mixed_done.sem, mixed_done.at(run))
                dve.tensor_tensor(h3[:].rearrange("p g e -> p (g e)"), bank_back[1][0:GT, 0:G * E],
                                  mixed[:].rearrange("p g e -> p (g e)"), ALU.add).then_inc(h3_ready.sem, 1)
                dve.wait_ge(h3_ready.sem, h3_ready.at(run))
                stats(run, h3, stats3, mv3, stats3_done, mv3_done)
                with_eps(run, ve3[:], mv3, mv3_done, ve3_done)

            def ln3_norm(run):
                dve.wait_ge(rstd3_done.sem, rstd3_done.at(run))
                standardise(n3, h3, mv3, rstd3, n3_ready)

            def ln3_gain(run):
                gain(run, n3_turned, bank_back[0], n3_t, g2, b2, n3t_ready)

            def residual3(run):
                dve.wait_ge(ff2_done.sem, ff2_done.at(run))
                dve.wait_ge(h3b_ready.sem, h3b_ready.at(run))
                dve.wait_ge(y_stored.sem, y_stored.before(run))
                dve.tensor_tensor(y[:].rearrange("p g e -> p (g e)"), bank_back[0][0:GT, 0:G * E],
                                  h3_b[:].rearrange("p g e -> p (g e)"), ALU.add).then_inc(y_ready.sem, 1)

            def body(i):
                back, front, ahead = i, i + 1, i + 2
                b, f, a = exists(back), exists(front), exists(ahead)
                if a:
                    split_x(ahead)
                if b:
                    ln2_first(back)
                    route(back)
                    pool_scores(back)
                    copy_sel(back)
                    q2_by_head(back)
                    logits_2(back)
                if f:
                    softmax1(front, 0)
                if b:
                    den_2(back)
                if f:
                    softmax1(front, 1)
                if b:
                    own_ctx2(back)
                if f:
                    normalise1(front, 0)
                if b:
                    merge(back)
                if f:
                    normalise1(front, 1)
                    softmax1(front, 2)
                if b:
                    residual2(back)
                    ln3_norm(back)
                if a:
                    add_pos(ahead)
                if b:
                    ln3_gain(back)
                if a:
                    ln1_stats(ahead)
                if f:
                    softmax1(front, 3)
                if a:
                    ln1_norm(ahead)
                if f:
                    normalise1(front, 2)
                    normalise1(front, 3)
                    residual1(front)
                    ln2_stats(front)
                    ln2_norm(front)
                if b:
                    residual3(back)
                if f:
                    ln2_gain(front)

            body(-2)
            dve.wait_ge(ld_attn, LD_ATTN)
            dve.tensor_reduce(rel_sum[:], rel[:], AX_X, ALU.add).then_inc(rel_summed, 1)
            dve.wait_ge(rel_placed, 1)
            placed = bank_score[0:GT, 0:TOK * H1].rearrange("p (k h) -> p k h", h=H1)
            for b in range(GB):
                dve.tensor_tensor(
                    pos_bias[:, :, b * TOK:(b + 1) * TOK], placed.rearrange("p k h -> p h k"),
                    cst("apart", GT)[:, b:b + 1].unsqueeze(2).broadcast_to([GT, H1, TOK]),
                    ALU.add).then_inc(bias_ready, 1)
            dve.wait_ge(bias_ready, GB)
            dve.wait_ge(cols_turned, 1)
            dve.tensor_copy(cols[:].rearrange("p n k -> p k n"),
                            bank_turn[0:EC, 0:16].rearrange("p (k n) -> p k n", k=2)).then_inc(cols_ready, 1)
            dve.tensor_copy(b_ff1[:], bank_turn[:, 16:16 + FC]).then_inc(cols_ready, 1)
            dve.wait_ge(cols_ready, 2)
            dve.wait_ge(ld_back, LD_BACK)
            dve.tensor_copy(wr_all[:], wr.unsqueeze(2).broadcast_to([EC, 2, GT])).then_inc(wr_ready, 1)
            dve.tensor_scalar(br_neg[:], br_neg[:], -1.0, None, ALU.mult).then_inc(wr_ready, 1)
            dve.wait_ge(wr_ready, 2)

            body(-1)
            with dve.Fori(0, RUNS - 2) as i:
                body(i)
            body(RUNS - 2)
            body(RUNS - 1)

        @block.tensor
        def _(pe):
            def turn_x(run, j):
                hf, tri = j // 2, j % 2
                if j == 0:
                    pe.wait_ge(x_split_done.sem, x_split_done.at(run))
                    if type(run) is not int or run > 1:
                        pe.wait_ge(h2_ready.sem, h2_ready.at(run - 2))
                    elif run == 1:
                        pe.wait_ge(n1_copied.sem, n1_copied.at(0))
                else:
                    pe.wait_ge(x_copied.sem, x_copied.at(run, CHANNELS * j))
                for n in range(TW):
                    mm = pe.transpose(bank_front[:, n * XP:(n + 1) * XP],
                                      x_split[:, tri * TW + n, hf * 128:(hf + 1) * 128], ident[0:XP, 0:XP])
                mm.then_inc(x_turned.sem, 1)

            def tokens(run):
                pe.wait_ge(x_copied.sem, x_copied.at(run))
                for g in range(G):
                    for c in range(PC):
                        mm = pe.matmul(bank_front[0:GT, g * E:(g + 1) * E], x_t[:, c, cols_of(g)], w_tok[:, c, :],
                                       start=(c == 0), stop=(c == PC - 1))
                mm.then_inc(tok_done.sem, 1)

            def turn_tokens(src, dst_bank, done):
                for k in range(2):
                    for g in range(G):
                        mm = pe.transpose(dst_bank[0:EC, k * RT + g * GT:k * RT + (g + 1) * GT], src[:, g, half(k)],
                                          ident[0:GT, 0:GT])
                mm.then_inc(done.sem, 1)

            def turn_n1(run):
                pe.wait_ge(n1_ready.sem, n1_ready.at(run))
                turn_tokens(n1, bank_front, n1_turned)

            def values(run, j):
                g, part = j // 2, j % 2
                if j == 0:
                    pe.wait_ge(n1_copied.sem, n1_copied.at(run))
                if j < 2:
                    pe.wait_ge(qk_copied.sem, qk_copied.at(run - 1, H1 - 1 + j))
                else:
                    pe.wait_ge(v_copied.sem, v_copied.at(run, j - 1))
                for k in range(2):
                    mm = pe.matmul(bank_proj[j % 2][0:GT, 0:QUAD * D1], n1_t[:, k, cols_of(g)],
                                   w_v[:, k, part * QUAD * D1:(part + 1) * QUAD * D1], start=(k == 0), stop=(k == 1))
                mm.then_inc(v_done.sem, 1)

            def queries_keys(run, hd):
                if hd < 2:
                    pe.wait_ge(v_copied.sem, v_copied.at(run, 3 + hd))
                else:
                    pe.wait_ge(qk_copied.sem, qk_copied.at(run, hd - 1))
                for n, w in enumerate((w_q, w_k)):
                    for k in range(2):
                        mm = pe.matmul(bank_proj[hd % 2][0:D1, n * RT:(n + 1) * RT], w[:, k, hd, :], n1_t[:, k, :],
                                       start=(k == 0), stop=(k == 1))
                mm.then_inc(qk_done.sem, 1)

            def scores(run, u):
                quad, g = UNIT[u]
                pe.wait_ge(qk_copied.sem, qk_copied.at(run, QUAD * (quad + 1)))
                pe.wait_ge(logits_ready.sem, logits_ready.at(run, u))
                for n in range(QUAD):
                    hd = quad * QUAD + n
                    mm = pe.matmul(bank_score[0:GT, n * GT:(n + 1) * GT], qk[:, hd, 0, cols_of(g)], qk[:, hd, 1, cols_of(g)],
                                   start=True, stop=True)
                mm.then_inc(score_done.sem, 1)

            def turn_probs(run, u):
                freed, value = [(ctx1_copied, 0), (probs_copied, 1), (ctx1_copied, 2), (probs_copied, 3)][u]
                pe.wait_ge(probs_ready.sem, probs_ready.at(run, u + 1))
                pe.wait_ge(freed.sem, freed.at(run, value))
                for n in range(QUAD):
                    mm = pe.transpose(bank_turn[0:GT, n * GT:(n + 1) * GT], probs[:, u % 2, n], ident[0:GT, 0:GT])
                mm.then_inc(probs_turned.sem, 1)

            def probs_values(run, u):
                quad, g = UNIT[u]
                pe.wait_ge(probs_copied.sem, probs_copied.at(run, u + 1))
                pe.wait_ge(ctx1_ready.sem, ctx1_ready.at(run, u))
                for n in range(QUAD):
                    mm = pe.matmul(bank_pv[0:GT, n * (D1 + 1):(n + 1) * (D1 + 1)], probs_t[:, u % 2, n],
                                   v[:, g, quad * QUAD + n], start=True, stop=True)
                mm.then_inc(pv_done.sem, 1)

            def turn_ctx1(run, u):
                freed, value = [(probs_copied, 2), (ctx1_copied, 1), (probs_copied, 4), (ctx1_copied, 3)][u]
                quad, g = UNIT[u]
                pe.wait_ge(ctx1_ready.sem, ctx1_ready.at(run, u + 1))
                pe.wait_ge(freed.sem, freed.at(run, value))
                rows = ctx1[:, g].rearrange("p h d -> p (h d)")
                for n in range(3):
                    c = 3 * quad + n
                    mm = pe.transpose(bank_turn[:, n * GT:(n + 1) * GT], rows[:, c * 128:(c + 1) * 128], ident[0:GT, 0:GT])
                mm.then_inc(ctx1_turned.sem, 1)

            def project1(run):
                pe.wait_ge(ctx1_copied.sem, ctx1_copied.at(run, UNITS - 1))
                if exists(run + 1):
                    pe.wait_ge(n1_copied.sem, n1_copied.at(run + 1))
                for g in range(G):
                    if g == G - 1:
                        pe.wait_ge(ctx1_copied.sem, ctx1_copied.at(run))
                    for c in range(FC):
                        mm = pe.matmul(bank_front[0:GT, g * E:(g + 1) * E], ctx1_t[:, c, cols_of(g)], w_o[:, c, :],
                                       start=(c == 0), stop=(c == FC - 1))
                mm.then_inc(wo_done.sem, 1)

            def turn_n2(run):
                pe.wait_ge(nn2_ready.sem, nn2_ready.at(run))
                turn_tokens(nn2, bank_back[1], n2_turned)

            def router(run):
                pe.wait_ge(n2t_ready.sem, n2t_ready.at(run))
                pe.wait_ge(y_ready.sem, y_ready.before(run))
                for k in range(2):
                    mm = pe.matmul(bank_back[0][0:GT, 0:RT], wr_all[:, k], n2_t[:, k], start=(k == 0), stop=(k == 1))
                mm.then_inc(z_done.sem, 1)

            def keys2(run):
                for m in range(2):
                    for k in range(2):
                        mm = pe.matmul(bank_back[1][0:EC, m * RT:(m + 1) * RT], w_k2[:, k, half(m)], n2_t[:, k],
                                       start=(k == 0), stop=(k == 1))
                mm.then_inc(k2_done.sem, 1)

            def values2(run):
                pe.wait_ge(score_exp.sem, score_exp.at(run))
                for g in range(G):
                    for k in range(2):
                        mm = pe.matmul(bank_back[0][0:GT, g * E:(g + 1) * E], n2_t[:, k, cols_of(g)], w_v2[:, k, :],
                                       start=(k == 0), stop=(k == 1))
                mm.then_inc(v2_done.sem, 1)

            def gather(run):
                pe.wait_ge(sel_ready.sem, sel_ready.at(run))
                pe.wait_ge(k2_copied.sem, k2_copied.at(run))
                for k in range(2):
                    for g in range(G):
                        pe.matmul(bank_back[1][0:EC, k * RS:(k + 1) * RS], nn2[:, g, half(k)], sel[:, g],
                                  start=(g == 0), stop=(g == G - 1))
                for g in range(G):
                    mm = pe.transpose(bank_back[1][0:RS, 128 + g * GT:128 + (g + 1) * GT], sel[:, g], ident[0:GT, 0:GT])
                mm.then_inc(gather_done.sem, 1)

            def queries2(run):
                pe.wait_ge(nsel_ready.sem, nsel_ready.at(run))
                pe.wait_ge(v2_copied.sem, v2_copied.at(run))
                for m in range(2):
                    for k in range(2):
                        mm = pe.matmul(bank_back[0][0:EC, m * RS:(m + 1) * RS], w_q2[:, k, half(m)], nsel_t[:, k],
                                       start=(k == 0), stop=(k == 1))
                mm.then_inc(q2_done.sem, 1)

            def scores2(run):
                pe.wait_ge(q2h_ready.sem, q2h_ready.at(run))
                pe.wait_ge(k2_copied.sem, k2_copied.at(run))
                pe.wait_ge(selt_copied.sem, selt_copied.at(run))
                for k in range(2):
                    for g in range(G):
                        j = k * G + g
                        mm = pe.matmul(bank_back[1][0:HC * GS, j * GT:(j + 1) * GT],
                                       q2_heads[:, k, g].rearrange("p h q -> p (h q)"), k2_t[:, k, cols_of(g)],
                                       start=True, stop=True)
                mm.then_inc(s2_done.sem, 1)

            def turn_probs2(run):
                pe.wait_ge(probs2_ready.sem, probs2_ready.at(run))
                pe.wait_ge(q2_copied.sem, q2_copied.at(run))
                n = HC * GS
                for j in range(4):
                    mm = pe.transpose(bank_back[0][0:GT, j * n:(j + 1) * n], probs2[:, j], ident[0:n, 0:n])
                mm.then_inc(p2_turned.sem, 1)

            def probs_values2(run):
                pe.wait_ge(p2_copied.sem, p2_copied.at(run))
                pe.wait_ge(logits2_ready.sem, logits2_ready.at(run))
                n = HC * GS
                for k in range(2):
                    for g in range(G):
                        j = k * G + g
                        mm = pe.matmul(bank_back[1][0:EC, j * n:(j + 1) * n], v2[:, g, half(k)], probs2_t[:, j],
                                       start=True, stop=True)
                mm.then_inc(pv2_done.sem, 1)

            def with_bias(out, lhs, w, n):
                pe.matmul(out, lhs[0:EC, 0, n], w[0:EC, 0, :], start=True, stop=False)
                return pe.matmul(out, lhs[:, 1, n], w[:, 1, :], start=False, stop=True)

            def project2(run):
                pe.wait_ge(ctx2_ready.sem, ctx2_ready.at(run))
                pe.wait_ge(mixed_done.sem, mixed_done.at(run))
                with_bias(bank_back[0][0:RS, 0:E], ctx2_t, w_o2, slice(0, RS)).then_inc(ao_done.sem, 1)

            def mix_project(run):
                pe.wait_ge(mix_step.sem, mix_step.at(run))
                pe.wait_ge(p2_copied.sem, p2_copied.at(run))
                for g in range(G):
                    mm = with_bias(bank_back[0][0:GT, g * E:(g + 1) * E], mix_t, w_m, cols_of(g))
                mm.then_inc(mix_done.sem, 1)

            def scatter(run):
                pe.wait_ge(attn2_copied.sem, attn2_copied.at(run))
                pe.wait_ge(own_done.sem, own_done.at(run))
                for g in range(G):
                    mm = pe.matmul(bank_back[1][0:GT, g * E:(g + 1) * E], sel_t[:, g], attn2[:], start=True, stop=True)
                mm.then_inc(scat_done.sem, 1)

            def turn_n3(run):
                pe.wait_ge(n3_ready.sem, n3_ready.at(run))
                turn_tokens(n3, bank_back[0], n3_turned)

            def ff1(run, j):
                if j == 0:
                    pe.wait_ge(n3t_ready.sem, n3t_ready.at(run))
                if j == 2:
                    pe.wait_ge(gelu_done.sem, gelu_done.at(run, 2))
                for n in range(2):
                    m = 2 * j + n
                    for k in range(2):
                        mm = pe.matmul(bank_back[(j + 1) % 2][:, n * RT:(n + 1) * RT], w_ff1[:, k, m * 128:(m + 1) * 128],
                                       n3_t[:, k], start=(k == 0), stop=(k == 1))
                mm.then_inc(ff1_done.sem, 1)

            def ff2(run):
                pe.wait_ge(gelu_done.sem, gelu_done.at(run, 6))
                for g in range(G):
                    for m in range(FC):
                        mm = pe.matmul(bank_back[0][0:GT, g * E:(g + 1) * E], ff_t[:, m, cols_of(g)], w_ff2[:, m, :],
                                       start=(m == 0), stop=(m == FC - 1))
                mm.then_inc(ff2_done.sem, 1)

            def body(i):
                back, front, ahead = i, i + 1, i + 2
                b, f, a = exists(back), exists(front), exists(ahead)
                if f:
                    values(front, 0)
                if b:
                    router(back)
                    keys2(back)
                if f:
                    values(front, 1)
                if b:
                    values2(back)
                if f:
                    values(front, 2)
                    values(front, 3)
                if a:
                    turn_x(ahead, 0)
                if f:
                    queries_keys(front, 0)
                    queries_keys(front, 1)
                if a:
                    turn_x(ahead, 1)
                if b:
                    gather(back)
                if f:
                    queries_keys(front, 2)
                if b:
                    queries2(back)
                if f:
                    queries_keys(front, 3)
                if a:
                    turn_x(ahead, 2)
                if b:
                    scores2(back)
                if f:
                    scores(front, 0)
                    queries_keys(front, 4)
                if a:
                    turn_x(ahead, 3)
                if f:
                    scores(front, 1)
                    queries_keys(front, 5)
                if b:
                    turn_probs2(back)
                if f:
                    turn_probs(front, 0)
                    queries_keys(front, 6)
                if b:
                    probs_values2(back)
                if f:
                    turn_probs(front, 1)
                    probs_values(front, 0)
                if b:
                    mix_project(back)
                if f:
                    queries_keys(front, 7)
                if b:
                    project2(back)
                if f:
                    probs_values(front, 1)
                    scores(front, 2)
                    turn_ctx1(front, 0)
                if b:
                    scatter(back)
                if f:
                    turn_ctx1(front, 1)
                if a:
                    tokens(ahead)
                if b:
                    turn_n3(back)
                if f:
                    turn_probs(front, 2)
                    scores(front, 3)
                if b:
                    ff1(back, 0)
                if f:
                    probs_values(front, 2)
                if b:
                    ff1(back, 1)
                if f:
                    turn_probs(front, 3)
                    turn_ctx1(front, 2)
                if a:
                    turn_n1(ahead)
                if f:
                    probs_values(front, 3)
                if b:
                    ff1(back, 2)
                if f:
                    turn_ctx1(front, 3)
                    project1(front)
                if b:
                    ff2(back)
                if f:
                    turn_n2(front)

            pe.wait_ge(ld_tok, LD_TOK)
            for j in range(PC // 2):
                if j >= 2:
                    pe.wait_ge(wt_copied, j - 1)
                for n in range(2):
                    for k in range(2):
                        mm = pe.transpose(bank_proj[j % 2][:, n * E + k * EC:n * E + (k + 1) * EC],
                                          w_raw[:, k, (2 * j + n) * 128:(2 * j + n + 1) * 128], ident[0:EC, 0:EC])
                mm.then_inc(wt_turned, 1)
            pe.wait_ge(wt_copied, PC // 2)
            pe.wait_ge(pos_ready, 1)
            body(-2)
            pe.wait_ge(ld_back, LD_BACK)
            for k in range(2):
                pe.transpose(bank_turn[0:EC, k * 8:(k + 1) * 8], vec_rows[:, half(k)], ident[0:8, 0:8])
            pe.transpose(bank_turn[:, 16:16 + FC], b_ff1_rows[:], ident[0:FC, 0:FC]).then_inc(cols_turned, 1)
            pe.wait_ge(rel_summed, 1)
            pe.wait_ge(place_ready, 1)
            for k in range(TOK):
                mm = pe.matmul(bank_score[0:GT, k * H1:(k + 1) * H1], place[:, TOK - 1 - k],
                               rel_sum[:], start=True, stop=True)
            mm.then_inc(rel_placed, 1)
            pe.wait_ge(bias_ready, GB)
            pe.wait_ge(wr_ready, 2)
            pe.wait_ge(zeroed, 7)
            body(-1)
            with pe.Fori(0, RUNS - 2) as i:
                body(i)
            body(RUNS - 2)
            body(RUNS - 1)


LD_TOK = 16 * (2 + 3 * GB)
LD_ATTN = 16 * (2 * 3 + 2)
LD_BACK = 16 * (7 + 8 + 5)


def constants():
    import numpy as np

    c = np.zeros((128, CONST_COLS), np.float32)

    def put(name, x):
        lo, hi = CONST[name]
        c[0:x.shape[0], lo:hi] = x

    t = np.arange(GT)
    same = t[:, None] // TOK == t[None, :] // TOK
    put("ident", np.eye(128, dtype=np.float32))
    put("same", same.astype(np.float32))
    put("lower", (same & (t[None, :] < t[:, None])).astype(np.float32))
    put("apart", np.where(t[:, None] // TOK == np.arange(GB)[None, :], 0.0, NEG).astype(np.float32))
    s = np.arange(GS)
    put("slot", np.where(t[:, None] // TOK == s[None, :] // SEL, s[None, :] % SEL, -1).astype(np.float32))
    put("headmask", (np.arange(EC)[:, None] // D2 == np.arange(HC)[None, :]).astype(np.float32))
    q = np.arange(HC * GS) % GS
    put("apart2", np.where(q[:, None] // SEL == t[None, :] // TOK, 0.0, NEG).astype(np.float32))
    r = np.arange(REL)
    put("shift", (r[:, None] + r[None, :] == REL - 1).astype(np.float32))
    return c


_INS = ["x", "cls_tok", "L0_tok_W", "L0_tok_b", "L0_tok_pos_embed", "L0_attn_w_q", "L0_attn_w_k", "L0_attn_w_v",
        "L0_attn_w_o", "L0_attn_rel_emb"] + ["L0_ffn_" + n for n in (
            "g1", "b1", "g2", "b2", "Wr", "br", "Wq", "bq", "Wk", "bk", "Wv", "bv", "Wo", "bo", "Wm", "bm", "W1", "bf1",
            "W2", "bf2")]


def kernel(**inputs):
    import numpy as _np
    import concourse.bacc as _bacc
    from concourse import mybir as _mybir
    from concourse.bass_utils import run_bass_kernel_spmd as _run

    nc = _bacc.Bacc("TRN2", target_bir_lowering=False, num_devices=1)
    arrays, aps = {}, {}
    for name in _INS + ["consts"]:
        v = constants() if name == "consts" else _np.ascontiguousarray(inputs[name])
        if v.ndim == 0:
            v = v.reshape(1)
        arrays[f"in_{name}_dram"] = v
        aps[name] = nc.dram_tensor(f"in_{name}_dram", v.shape, _mybir.dt.from_np(v.dtype), kind="ExternalInput").ap()
    aps["out"] = nc.dram_tensor("out_0_dram", (BATCH, TOK, E), F32, kind="ExternalOutput").ap()
    vit_block(nc, aps)
    r = _run(nc, [arrays], core_ids=[0])
    return r.results[0]["out_0_dram"]
```

```python
from contextlib import ExitStack

import concourse.bass as bass
from concourse import mybir

F32 = mybir.dt.float32
F32R = mybir.dt.float32r
ALU = mybir.AluOpType
ACT = mybir.ActivationFunctionType
AX_X = mybir.AxisListType.X

BATCH, CHANNELS, SIDE, PATCH = 64, 3, 96, 16
HP = SIDE // PATCH
NP = HP * HP
TOK = NP + 1
E = 192
EC = E // 2
GB = 3
GT = GB * TOK
G = 2
RB = G * GB
RT = G * GT
RUNS = -(-BATCH // RB)
LAST_B = BATCH - (RUNS - 1) * RB
PD = CHANNELS * PATCH * PATCH
PC = PD // 128
H1, D1 = 8, 96
QUAD = 4
UNITS = (H1 // QUAD) * G
QCH = QUAD * D1 // 128
CHUNKS = (H1 // QUAD) * QCH
TAIL = 128 - D1
assert TAIL * QCH == D1
H2, D2 = 12, 16
HC = EC // D2
QUARTERS = -(-GT // 32)
SEL = 6
GS = GB * SEL
RS = G * GS
FF = 768
FC = FF // 128
MAX_DIST = 100
REL = 2 * TOK - 1
EPS = 1e-5
NEG = -1e30
XP = CHANNELS * RB * HP
TW = HP // 2

CONST = {}
_at = 0
for _name, _n in (("ident", 128), ("same", GT), ("lower", GT), ("slot", GS),
                  ("headmask", HC), ("apart2", GT)):
    CONST[_name] = (_at, _at + _n)
    _at += _n
CONST_COLS = _at


class Signal:

    def __init__(self, sem, per_run, early):
        self.sem, self.per_run, self.early = sem, per_run, early

    def at(self, run, k=None):
        return (run + self.early) * self.per_run + (self.per_run if k is None else k)

    def before(self, run):
        assert self.early
        return run * self.per_run + self.per_run


def vit_block(nc, a):
    with ExitStack() as ctx:
        def sb(name, shape, dtype=F32):
            return ctx.enter_context(nc.sbuf_tensor(name, shape, dtype))

        def bank(name):
            return ctx.enter_context(nc.psum_tensor(name, [128, 512], F32))

        def sem(name):
            return ctx.enter_context(nc.semaphore(name))

        def signal(name, per_run=1, early=0):
            return Signal(sem(name), per_run, early)

        const = sb("const", [128, CONST_COLS])

        def cst(name, p=128):
            lo, hi = CONST[name]
            return const[0:p, lo:hi]

        ident = cst("ident")
        staged = [sb(f"staged{n}", [EC, 2, PD]) for n in range(2)]
        assert H1 * D1 == PD == CHUNKS * 128 == FF
        w_raw, w_v = staged
        w_ff1 = staged[0]
        w_q, w_k = (s[:].rearrange("p k (c m) -> p k c m", m=128) for s in staged)
        w_tok = sb("w_tok", [128, PC, E])
        pos_tok = sb("pos_tok", [GT, E])
        b_tok = sb("b_tok", [GT, E])
        w_qk_hi = sb("w_qk_hi", [EC, 2, 2, CHUNKS, 128], F32R)
        w_qk_lo = sb("w_qk_lo", [EC, 2, 2, CHUNKS, 128], F32R)
        w_v_hi = sb("w_v_hi", [EC, 2, H1 * D1], F32R)
        w_v_lo = sb("w_v_lo", [EC, 2, H1 * D1], F32R)
        w_o = sb("w_o", [128, FC, E])
        rel_sum = sb("rel_sum", [REL, H1])
        pos_bias = sb("pos_bias", [GT, H1, GT])
        cols = sb("cols", [EC, 8, 2])
        g1, b1, g2, b2, bq, bk, bv, wr = (cols[:, n, :] for n in range(8))
        vec_rows = sb("vec_rows", [8, E])
        b_ff1_rows = sb("b_ff1_rows", [FC, 128])
        br_neg = sb("br_neg", [128, 1])
        b_ff1 = sb("b_ff1", [128, FC])
        b_ff2 = sb("b_ff2", [GT, E])
        w_q2 = sb("w_q2", [EC, 2, E])
        w_k2 = sb("w_k2", [EC, 2, 2, 128])
        w_v2 = sb("w_v2", [EC, 2, E])
        w_o2 = sb("w_o2", [EC + 1, 2, E])
        w_m = sb("w_m", [EC + 1, 2, E])
        w_ff1_hi = sb("w_ff1_hi", [EC, 2, FF], F32R)
        w_ff1_lo = sb("w_ff1_lo", [EC, 2, FF], F32R)
        w_ff2 = sb("w_ff2", [128, FC, E])
        power = sb("power", [GT, G])
        zero = sb("zero", [GT, 1])
        power2 = sb("power2", [GT, 2, G])

        x_rows = sb("x_rows", [XP, PATCH, HP, PATCH])
        x_split = sb("x_split", [XP, HP, PATCH * PATCH])
        x_t = sb("x_t", [128, PC, RT])
        h = sb("h", [GT, G, E])
        stats1 = sb("stats1", [GT, G, 6])
        mv1 = sb("mv1", [GT, G, 2])
        ve1 = sb("ve1", [GT, G])
        rstd1 = sb("rstd1", [GT, G])
        n1 = sb("n1", [GT, G, E])
        n1_t = sb("n1_t", [EC, 2, RT])
        n1_hi = sb("n1_hi", [EC, 2, RT], F32R)
        n1_lo = sb("n1_lo", [EC, 2, RT], F32R)
        qk = sb("qk", [D1, H1, 2, RT])
        set_up = qk[:].rearrange("p h a t -> p (h a t)")
        rel_bias = set_up[0:H1, 0:TOK * TOK].rearrange("p (q k) -> p q k", k=TOK)
        rel = set_up[0:REL, TOK * TOK:TOK * TOK + H1 * D1].rearrange("p (h d) -> p h d", d=D1)
        v = sb("v", [GT, G, H1, D1 + 1])
        logits = sb("logits", [GT, 2, QUAD, GT])
        rowmax = sb("rowmax", [GT, 2, QUAD])
        shifted = logits
        probs = sb("probs", [GT, 2, QUAD, GT])
        probs_t = sb("probs_t", [GT, 2, QUAD, GT])
        den_inv = sb("den_inv", [GT, UNITS, QUAD])
        ctx1 = sb("ctx1", [GT, G, H1, D1])
        ctx1_t = sb("ctx1_t", [128, FC, RT])
        h_keep = sb("h_keep", [GT, G, E])
        h2 = sb("h2", [GT, G, E])

        stats2 = sb("stats2", [GT, G, 6])
        mv2 = sb("mv2", [GT, G, 2])
        ve2 = sb("ve2", [GT, 2, G])
        rstd2 = sb("rstd2", [GT, 2, G])
        n2 = sb("n2", [GT, G, E])
        nn2 = sb("nn2", [GT, G, E])
        n2_t = sb("n2_t", [EC, 2, RT])
        score_e = sb("score_e", [GT, RT])
        score_d = sb("score_d", [GT, RT])
        score = sb("score", [GT, RT])
        junk = sb("junk", [GT, G, GT])
        score_col = sb("score_col", [GT, G])
        less = sb("less", [GT, G, GT])
        tied = sb("tied", [GT, G, GT])
        rank = sb("rank", [GT, G])
        sel = sb("sel", [GT, G, RS])
        sel_t = sb("sel_t", [RS, G, GT])
        unrouted = sb("unrouted", [GT, G])
        s_sum = sb("s_sum", [EC, RB])
        s_eps = sb("s_eps", [EC, RB])
        s_inv = sb("s_inv", [EC, RB])
        weighted = sb("weighted", [EC, 2, RT])
        pooled = sb("pooled", [EC, 2, RB])
        pooled_n = sb("pooled_n", [EC, 2, RB])
        spread = weighted
        mix_t = sb("mix_t", [EC + 1, 2, RT])
        k2_t = sb("k2_t", [EC, 2, RT])
        v2 = sb("v2", [GT, G, E])
        nsel_t = sb("nsel_t", [EC, 2, RS])
        q2_t = sb("q2_t", [EC, 2, RS])
        q2_heads = sb("q2_heads", [EC, 2, G, HC, GS])
        logits2 = sb("logits2", [HC * GS, 4, GT])
        negmax2 = sb("negmax2", [HC * GS, 4])
        den2 = sb("den2", [HC * GS, 4])
        den2_inv = sb("den2_inv", [HC * GS, 4])
        exp2 = probs2 = logits2
        probs2_t = sb("probs2_t", [GT, 4, HC * GS])
        own = sb("own", [EC, 4, HC, GS])
        ctx2 = sb("ctx2", [EC, 4, GS])
        ctx2_t = sb("ctx2_t", [EC + 1, 2, RS])
        attn2 = sb("attn2", [RS, E])
        mixed = sb("mixed", [GT, G, E])
        h3 = sb("h3", [GT, G, E])
        h2_b = sb("h2_b", [GT, G, E])
        h3_b = sb("h3_b", [GT, G, E])
        stats3 = sb("stats3", [GT, G, 6])
        mv3 = sb("mv3", [GT, G, 2])
        ve3 = sb("ve3", [GT, G])
        rstd3 = sb("rstd3", [GT, G])
        n3 = sb("n3", [GT, G, E])
        n3_t = sb("n3_t", [EC, 2, RT])
        n3_hi = sb("n3_hi", [EC, 2, RT], F32R)
        n3_lo = sb("n3_lo", [EC, 2, RT], F32R)
        ff_t = sb("ff_t", [128, FC, RT])
        y = sb("y", [GT, G, E])

        bank_proj = [bank("bank_proj0"), bank("bank_proj1")]
        bank_score = bank("bank_score")
        bank_turn = bank("bank_turn")
        bank_pv = bank("bank_pv")
        bank_front = bank("bank_front")
        bank_back = [bank("bank_back0"), bank("bank_back1")]

        ld_const, ld_w, ld_pos = sem("ld_const"), sem("ld_w"), sem("ld_pos")
        ld_rel, ld_vecs, ld_v, ld_qk = sem("ld_rel"), sem("ld_vecs"), sem("ld_v"), sem("ld_qk")
        ld_wo, ld_back = sem("ld_wo"), sem("ld_back")
        tok_zeroed, x_zeroed, bias_masked, zeroed = sem("tok_zeroed"), sem("x_zeroed"), sem("bias_masked"), sem("zeroed")
        wt_turned, wt_copied = sem("wt_turned"), sem("wt_copied")
        pos_ready = sem("pos_ready")
        ld_ff1, wff1_split = sem("ld_ff1"), sem("wff1_split")
        wv_split, wqk_hi_ready, wqk_split = sem("wv_split"), sem("wqk_hi_ready"), sem("wqk_split")
        rel_summed, rel_turned = sem("rel_summed"), sem("rel_turned")
        rel_spread, bias_written, bias_placed = sem("rel_spread"), sem("bias_written"), sem("bias_placed")
        vector_passed = sem("vector_passed")
        cols_turned, cols_ready = sem("cols_turned"), sem("cols_ready")
        wr_ready, power_ready = sem("wr_ready"), sem("power_ready")

        x_loaded = sem("x_loaded")
        x_split_done = signal("x_split_done")
        x_turned = signal("x_turned", 4)
        x_copied = signal("x_copied", 4 * CHANNELS)
        tok_done = signal("tok_done")
        h_ready = signal("h_ready")
        stats1_done, mv1_done = signal("stats1_done", 2), signal("mv1_done", 2)
        ve1_done, rstd1_done = signal("ve1_done"), signal("rstd1_done")
        n1_ready = signal("n1_ready", 2)
        n1_turned, n1_copied = signal("n1_turned"), signal("n1_copied", 2)
        n1_split = signal("n1_split")
        v_done, v_copied = signal("v_done", 4), signal("v_copied", 4)
        qk_done, qk_copied = signal("qk_done", CHUNKS), signal("qk_copied", 2 * CHUNKS, 1)
        score_done, logits_ready = signal("score_done", UNITS), signal("logits_ready", UNITS, 1)
        rowmax_done, shifted_done = signal("rowmax_done", UNITS), signal("shifted_done", UNITS)
        probs_ready = signal("probs_ready", UNITS)
        probs_turned, probs_copied = signal("probs_turned", UNITS), signal("probs_copied", UNITS)
        pv_done = signal("pv_done", UNITS)
        den_done, ctx1_ready = signal("den_done", UNITS), signal("ctx1_ready", UNITS, 1)
        ctx1_turned, ctx1_copied = signal("ctx1_turned", UNITS), signal("ctx1_copied", UNITS, 1)
        h_kept = signal("h_kept")
        wo_done, h2_ready = signal("wo_done"), signal("h2_ready", 1, 1)

        stats2_done, mv2_done = signal("stats2_done", 2), signal("mv2_done", 2)
        ve2_done, rstd2_done = signal("ve2_done", 2), signal("rstd2_done")
        n2_ready, nn2_ready = signal("n2_ready", 2), signal("nn2_ready", 2)
        n2_turned, n2t_ready = signal("n2_turned"), signal("n2t_ready", 2)
        z_done, score_exp, score_step = signal("z_done"), signal("score_exp", QUARTERS), signal("score_step", 2)
        col_done, cmp_done = signal("col_done", 2), signal("cmp_done", 4)
        rank_done, sel_ready, unrouted_ready = signal("rank_done", 2), signal("sel_ready", 2), signal("unrouted_ready", 2)
        sum_step = signal("sum_step", 3)
        weighted_done, pool_step, mix_step = signal("weighted_done"), signal("pool_step", 2), signal("mix_step", 2)
        k2_done, k2_copied = signal("k2_done"), signal("k2_copied", 2)
        v2_done, v2_copied = signal("v2_done"), signal("v2_copied")
        gather_done, nsel_ready, selt_copied = signal("gather_done"), signal("nsel_ready", 2), signal("selt_copied")
        q2_done, q2_copied, q2h_ready = signal("q2_done"), signal("q2_copied", 2), signal("q2h_ready", 2)
        s2_done, logits2_ready, max2_done = signal("s2_done"), signal("logits2_ready"), signal("max2_done")
        exp2_done, den2_done, probs2_ready = signal("exp2_done", 4), signal("den2_done"), signal("probs2_ready")
        p2_turned, p2_copied = signal("p2_turned"), signal("p2_copied")
        pv2_done, own_done, ctx2_done, ctx2_ready = signal("pv2_done"), signal("own_done"), signal("ctx2_done"), signal("ctx2_ready")
        ao_done, attn2_copied = signal("ao_done"), signal("attn2_copied")
        scat_done, mix_done = signal("scat_done"), signal("mix_done")
        mixed_done, h3_ready = signal("mixed_done", 2), signal("h3_ready")
        stats3_done, mv3_done = signal("stats3_done", 2), signal("mv3_done", 2)
        h2b_ready = signal("h2b_ready")
        ve3_done, rstd3_done, h3b_ready = signal("ve3_done"), signal("rstd3_done"), signal("h3b_ready")
        n3_ready, n3_turned, n3t_ready = signal("n3_ready", 2), signal("n3_turned"), signal("n3t_ready", 2)
        n3_rounded, n3_split = signal("n3_rounded", 2), signal("n3_split", 2)
        ff1_done, gelu_done = signal("ff1_done", 3), signal("gelu_done", 6)
        ff2_done, y_ready = signal("ff2_done"), signal("y_ready", 1, 1)
        y_stored = signal("y_stored", 16 * G, 1)

        def cols_of(g):
            return slice(g * GT, (g + 1) * GT)

        def half(k):
            return slice(k * EC, (k + 1) * EC)

        def width(run):
            return LAST_B * TOK if type(run) is int and run == RUNS - 1 else RT

        def exists(run):
            return type(run) is not int or 0 <= run < RUNS

        UNIT = [(quad, g) for quad in range(H1 // QUAD) for g in range(G)]

        block = ctx.enter_context(nc.Block())

        @block.sync
        def _(sp):
            sp.sem_inc(y_stored.sem, y_stored.per_run)

            def load_x(first, images):
                for c in range(CHANNELS):
                    sp.dma_start(
                        x_rows[c * RB * HP:c * RB * HP + images * HP].rearrange("p a w b -> p (a w b)"),
                        a["x"][bass.ds(first, images), c].rearrange("b (r q) w -> b r (q w)", q=PATCH),
                    ).then_inc(x_loaded, 16)

            def store(run, first, images):
                sp.wait_ge(y_ready.sem, y_ready.at(run))
                out = a["out"].rearrange("b t e -> (b t) e")
                for g in range(-(-images // GB)):
                    n = min(GB, images - g * GB) * TOK
                    sp.dma_start(out[bass.ds(first * TOK + g * GT, n)], y[0:n, g]).then_inc(y_stored.sem, 16)

            sp.dma_start(const[:], a["consts"]).then_inc(ld_const, 16)
            load_x(0, RB)
            sp.dma_start(w_raw[:], a["L0_tok_W"].rearrange("(k e) d -> e k d", e=EC)).then_inc(ld_w, 16)
            sp.dma_start(rel, a["L0_attn_rel_emb"][:, MAX_DIST - TOK:MAX_DIST - TOK + REL].rearrange("h r d o -> r h (d o)")).then_inc(ld_rel, 16)
            sp.wait_ge(tok_zeroed, 2)
            for b in range(GB):
                rows = slice(b * TOK + 1, (b + 1) * TOK)
                sp.dma_start(pos_tok[rows], a["L0_tok_pos_embed"][0]).then_inc(ld_pos, 16)
                sp.dma_start(pos_tok[b * TOK:b * TOK + 1], a["cls_tok"][0]).then_inc(ld_pos, 16)
                sp.dma_start(b_tok[rows], a["L0_tok_b"].rearrange("(o e) -> o e", o=1).broadcast_to([NP, E])).then_inc(ld_pos, 16)

            def reload_x(run, images):
                sp.wait_ge(x_split_done.sem, x_split_done.at(run - 1))
                load_x(run * RB, images)

            src = a["L0_attn_w_v"].rearrange("h (k e) d -> k e h d", e=EC)
            for k in range(2):
                sp.dma_start(w_v[:, k].rearrange("p (h d) -> p h d", h=H1), src[k]).then_inc(ld_v, 16)
            reload_x(1, RB)
            for w, name, free, value in ((w_q, "w_q", wt_turned, PC // 2), (w_k, "w_k", wv_split, 2)):
                sp.wait_ge(free, value)
                for k in range(2):
                    for quad in range(H1 // QUAD):
                        dst = w[:, k, quad * QCH:(quad + 1) * QCH]
                        heads = a["L0_attn_" + name][quad * QUAD:(quad + 1) * QUAD, half(k)]
                        sp.dma_start(dst[:, :, 0:D1], heads[0:QCH].rearrange("h e d -> e h d")).then_inc(ld_qk, 16)
                        sp.dma_start(dst[:, :, D1:128], heads[QCH].rearrange("e (n t) -> e n t", t=TAIL)).then_inc(ld_qk, 16)
            sp.dma_start(w_o[:], a["L0_attn_w_o"].rearrange("h d e -> (h d) e").rearrange("(k p) e -> p k e", p=128)).then_inc(ld_wo, 16)
            sp.wait_ge(rel_spread, 1)
            sp.dma_start(a["bias_scratch"], rel_bias).then_inc(bias_written, 16)
            sp.wait_ge(bias_written, 16)
            sp.wait_ge(bias_masked, 1)
            for b in range(GB):
                own_tokens = slice(b * TOK, (b + 1) * TOK)
                sp.dma_start(pos_bias[own_tokens, :, own_tokens], a["bias_scratch"].rearrange("h q k -> q h k")).then_inc(bias_placed, 16)
            sp.wait_ge(wqk_split, 1)
            sp.dma_start(w_ff1[:], a["L0_ffn_W1"].rearrange("(k e) d -> e k d", e=EC)).then_inc(ld_ff1, 16)
            for m in range(2):
                sp.dma_start(w_k2[:, :, m, 0:EC], a["L0_ffn_Wk"][:, half(m)].rearrange("(k e) d -> e k d", e=EC)).then_inc(ld_back, 16)
            for w, name in ((w_q2, "Wq"), (w_v2, "Wv"), (w_o2, "Wo"), (w_m, "Wm")):
                sp.dma_start(w[0:EC], a["L0_ffn_" + name].rearrange("(k e) d -> e k d", e=EC)).then_inc(ld_back, 16)
            sp.dma_start(w_ff2[:], a["L0_ffn_W2"].rearrange("(k e) d -> e k d", e=128)).then_inc(ld_back, 16)
            sp.dma_start(b_ff2[:], a["L0_ffn_bf2"].rearrange("(o e) -> o e", o=1).broadcast_to([GT, E])).then_inc(ld_back, 16)
            sp.dma_start(w_o2[EC:EC + 1, 1], a["L0_ffn_bo"].rearrange("(o e) -> o e", o=1)).then_inc(ld_back, 16)
            sp.dma_start(w_m[EC:EC + 1, 1], a["L0_ffn_bm"].rearrange("(o e) -> o e", o=1)).then_inc(ld_back, 16)
            reload_x(2, RB)
            with sp.Fori(0, RUNS - 4) as i:
                reload_x(i + 3, RB)
                store(i, i * RB, RB)
            reload_x(RUNS - 1, LAST_B)
            for run in range(RUNS - 4, RUNS):
                store(run, run * RB, RB if run < RUNS - 1 else LAST_B)
            sp.wait_ge(y_stored.sem, y_stored.at(RUNS - 1))

        @block.gpsimd
        def _(pool):
            pool.memset(pos_tok[:], 0.0).then_inc(tok_zeroed, 1)
            pool.memset(b_tok[:], 0.0).then_inc(tok_zeroed, 1)
            pool.memset(x_t[:], 0.0).then_inc(x_zeroed, 1)
            pool.memset(power[:], -0.5).then_inc(power_ready, 1)
            pool.memset(power2[:], -0.5).then_inc(power_ready, 1)
            pool.memset(zero[:], 0.0).then_inc(power_ready, 1)
            pool.memset(pos_bias[:], NEG).then_inc(bias_masked, 1)
            pool.memset(sel[:], 0.0).then_inc(zeroed, 1)
            pool.memset(v[:, :, :, D1:D1 + 1], 1.0).then_inc(zeroed, 1)
            pool.wait_ge(zeroed, 2)
            pool.memset(mix_t[EC:EC + 1], 1.0).then_inc(zeroed, 1)
            pool.wait_ge(zeroed, 3)
            pool.memset(ctx2_t[EC:EC + 1], 1.0).then_inc(zeroed, 1)
            pool.wait_ge(power_ready, 3)
            pool.wait_ge(zeroed, 4)

            def keep_h(run):
                pool.wait_ge(h_ready.sem, h_ready.at(run))
                pool.tensor_tensor(h_keep[:], h[:], zero[:].unsqueeze(2).broadcast_to([GT, G, E]), ALU.add).then_inc(h_kept.sem, 1)

            def ln1(run):
                pool.wait_ge(ve1_done.sem, ve1_done.at(run))
                pool.tensor_tensor(rstd1[:], ve1[:], power[:], ALU.pow).then_inc(rstd1_done.sem, 1)

            def shift(run, u):
                pool.wait_ge(rowmax_done.sem, rowmax_done.at(run, u + 1))
                pool.tensor_tensor(shifted[:, u % 2], logits[:, u % 2],
                                   rowmax[:, u % 2].unsqueeze(2).broadcast_to([GT, QUAD, GT]),
                                   ALU.subtract).then_inc(shifted_done.sem, 1)

            def ln2(run):
                pool.wait_ge(ve2_done.sem, ve2_done.at(run))
                pool.tensor_tensor(rstd2[:], ve2[:], power2[:], ALU.pow).then_inc(rstd2_done.sem, 1)

            def outer_residual(run):
                pool.tensor_tensor(h2_b[:], h2[:], b_ff2[:].unsqueeze(1).broadcast_to([GT, G, E]),
                                   ALU.add).then_inc(h2b_ready.sem, 1)

            def weigh(run):
                pool.wait_ge(n2t_ready.sem, n2t_ready.at(run))
                pool.wait_ge(score_step.sem, score_step.at(run))
                pool.tensor_tensor(weighted[:], n2_t[:],
                                   score[0:EC].unsqueeze(1).broadcast_to([EC, 2, RT]),
                                   ALU.mult).then_inc(weighted_done.sem, 1)

            def mix(run):
                pool.wait_ge(pool_step.sem, pool_step.at(run))
                pool.tensor_tensor(spread[:].rearrange("p k (b t) -> p k b t", t=TOK),
                                   pooled_n[:].unsqueeze(3).broadcast_to([EC, 2, RB, TOK]),
                                   score[0:EC].rearrange("p (b t) -> p b t", t=TOK).unsqueeze(1).broadcast_to([EC, 2, RB, TOK]),
                                   ALU.mult).then_inc(mix_step.sem, 1)
                pool.wait_ge(mix_step.sem, mix_step.at(run, 1))
                pool.tensor_tensor(mix_t[0:EC], spread[:], n2_t[:], ALU.add).then_inc(mix_step.sem, 1)

            def ln3(run):
                pool.wait_ge(ve3_done.sem, ve3_done.at(run))
                pool.tensor_tensor(rstd3[:], ve3[:], power[:], ALU.pow).then_inc(rstd3_done.sem, 1)

            def add_h3(run):
                pool.wait_ge(h3_ready.sem, h3_ready.at(run))
                pool.wait_ge(h2b_ready.sem, h2b_ready.at(run))
                pool.tensor_tensor(h3_b[:], h3[:], h2_b[:], ALU.add).then_inc(h3b_ready.sem, 1)

            def body(i):
                back, front, ahead = i, i + 1, i + 2
                b, f, a = exists(back), exists(front), exists(ahead)
                if b:
                    weigh(back)
                    mix(back)
                if f:
                    keep_h(front)
                if b:
                    outer_residual(back)
                if f:
                    shift(front, 0)
                    shift(front, 1)
                    shift(front, 2)
                if b:
                    ln3(back)
                if f:
                    shift(front, 3)
                if a:
                    ln1(ahead)
                if b:
                    add_h3(back)
                if f:
                    ln2(front)

            body(-2)
            body(-1)
            pool.wait_ge(ld_back, LD_BACK)
            with pool.Fori(0, RUNS - 2) as i:
                body(i)
            body(RUNS - 2)
            body(RUNS - 1)

        @block.scalar
        def _(act):
            act.sem_inc(qk_copied.sem, qk_copied.per_run)
            act.sem_inc(ctx1_copied.sem, ctx1_copied.per_run)
            def copy_x(run, j):
                hf, tri = j // 2, j % 2
                act.wait_ge(x_turned.sem, x_turned.at(run, j + 1))
                src = bank_front[:, 0:TW * XP].rearrange("p (w q) -> p w q", w=TW)
                for c in range(CHANNELS):
                    dst = x_t[:, 2 * c + hf].rearrange("p (b t) -> p b t", t=TOK)[:, :, 1:]
                    dst = dst.rearrange("p b (r w) -> p b r w", w=HP)[:, :, :, tri * TW:(tri + 1) * TW]
                    s = src[:, :, c * RB * HP:(c + 1) * RB * HP].rearrange("p w (b r) -> p b r w", r=HP)
                    act.copy(dst, s).then_inc(x_copied.sem, 1)

            def copy_n1(run):
                act.wait_ge(n1_turned.sem, n1_turned.at(run))
                for dst in (n1_t, n1_hi):
                    act.copy(dst[:].rearrange("p k t -> p (k t)"), bank_proj[0][0:EC, 0:2 * RT]).then_inc(n1_copied.sem, 1)

            def copy_v(run, j):
                g, part = j // 2, j % 2
                act.wait_ge(v_done.sem, v_done.at(run, j + 1))
                act.copy(v[:, g, part * QUAD:(part + 1) * QUAD, 0:D1],
                         bank_proj[j % 2][0:GT, 0:QUAD * D1].rearrange("p (h d) -> p h d", h=QUAD)).then_inc(v_copied.sem, 1)

            def copy_qk(run, j):
                quad, n = j // QCH, j % QCH
                if type(run) is int and (run, j) == (0, 0):
                    act.wait_ge(bias_written, 16)
                act.wait_ge(qk_done.sem, qk_done.at(run, j + 1))
                src = bank_proj[j % 2][:, 0:2 * RT].rearrange("p (a t) -> p a t", a=2)
                act.copy(qk[:, quad * QUAD + n], src[0:D1]).then_inc(qk_copied.sem, 1)
                act.copy(qk[n * TAIL:(n + 1) * TAIL, quad * QUAD + QCH], src[D1:128]).then_inc(qk_copied.sem, 1)

            def exp1(run, u):
                act.wait_ge(shifted_done.sem, shifted_done.at(run, u + 1))
                act.activation(probs[:, u % 2], shifted[:, u % 2], ACT.Exp).then_inc(probs_ready.sem, 1)

            def copy_probs(run, u):
                act.wait_ge(probs_turned.sem, probs_turned.at(run, u + 1))
                act.copy(probs_t[:, u % 2].rearrange("p h t -> p (h t)"), bank_turn[0:GT, 0:QUAD * GT]).then_inc(probs_copied.sem, 1)

            def copy_ctx1(run, u):
                quad, g = UNIT[u]
                act.wait_ge(ctx1_turned.sem, ctx1_turned.at(run, u + 1))
                act.copy(ctx1_t[:, 3 * quad:3 * quad + 3, cols_of(g)],
                         bank_turn[:, 0:3 * GT].rearrange("p (k t) -> p k t", k=3)).then_inc(ctx1_copied.sem, 1)

            def exp_score(run):
                act.wait_ge(z_done.sem, z_done.at(run))
                for n in range(QUARTERS):
                    p = min(32, GT - n * 32)
                    act.activation(score_e[n * 32:n * 32 + p, 0:width(run)], bank_back[0][EC:EC + p, 0:width(run)], ACT.Exp,
                                   bias=br_neg[EC:EC + p], scale=-1.0).then_inc(score_exp.sem, 1)

            def copy_k2(run):
                act.wait_ge(k2_done.sem, k2_done.at(run))
                for k in range(2):
                    act.activation(k2_t[:, k], bank_back[k][0:EC, 0:RT], ACT.Identity,
                                   bias=bk[:, k:k + 1]).then_inc(k2_copied.sem, 1)

            def copy_v2(run):
                act.wait_ge(v2_done.sem, v2_done.at(run))
                act.copy(v2[:].rearrange("p g e -> p (g e)"), bank_back[0][0:GT, 0:G * E]).then_inc(v2_copied.sem, 1)

            def copy_q2(run):
                act.wait_ge(q2_done.sem, q2_done.at(run))
                for k in range(2):
                    act.activation(q2_t[:, k], bank_back[0][0:EC, k * RS:(k + 1) * RS], ACT.Identity,
                                   bias=bq[:, k:k + 1]).then_inc(q2_copied.sem, 1)

            def exp_2(run):
                act.wait_ge(max2_done.sem, max2_done.at(run))
                for j in range(4):
                    act.activation(exp2[:, j], logits2[:, j], ACT.Exp, bias=negmax2[:, j:j + 1],
                                   accum_out=den2[:, j:j + 1]).then_inc(exp2_done.sem, 1)

            def copy_p2(run):
                act.wait_ge(p2_turned.sem, p2_turned.at(run))
                act.copy(probs2_t[:].rearrange("p j t -> p (j t)"), bank_back[0][0:GT, 0:4 * HC * GS]).then_inc(p2_copied.sem, 1)

            def copy_attn2(run):
                act.wait_ge(ao_done.sem, ao_done.at(run))
                act.copy(attn2[:], bank_back[1][0:RS, 0:E]).then_inc(attn2_copied.sem, 1)

            def round_n3(run):
                for k in range(2):
                    act.wait_ge(n3t_ready.sem, n3t_ready.at(run, k + 1))
                    act.copy(n3_hi[:, k], n3_t[:, k]).then_inc(n3_rounded.sem, 1)

            def gelu(run, first):
                for m in range(first, first + 2):
                    if m % 2 == 0:
                        act.wait_ge(ff1_done.sem, ff1_done.at(run, m // 2 + 1))
                    act.activation(ff_t[:, m], bank_back[(m // 2 + 1) % 2][:, (m % 2) * RT:(m % 2 + 1) * RT], ACT.Gelu,
                                   bias=b_ff1[:, m:m + 1]).then_inc(gelu_done.sem, 1)

            def body(i):
                back, front, ahead = i, i + 1, i + 2
                b, f, a = exists(back), exists(front), exists(ahead)
                if f:
                    copy_v(front, 0)
                    copy_v(front, 1)
                if b:
                    exp_score(back)
                if f:
                    copy_v(front, 2)
                if b:
                    copy_k2(back)
                if f:
                    copy_v(front, 3)
                if a:
                    copy_x(ahead, 0)
                if f:
                    copy_qk(front, 0)
                if a:
                    copy_x(ahead, 1)
                if f:
                    copy_qk(front, 1)
                    copy_qk(front, 2)
                if a:
                    copy_x(ahead, 2)
                if f:
                    copy_qk(front, 3)
                if b:
                    copy_q2(back)
                if f:
                    exp1(front, 0)
                if a:
                    copy_x(ahead, 3)
                if f:
                    copy_qk(front, 4)
                    copy_probs(front, 0)
                    exp1(front, 1)
                if b:
                    exp_2(back)
                    copy_v2(back)
                if f:
                    copy_qk(front, 5)
                if b:
                    copy_p2(back)
                if f:
                    copy_probs(front, 1)
                    copy_ctx1(front, 0)
                if b:
                    copy_attn2(back)
                if f:
                    exp1(front, 2)
                    copy_ctx1(front, 1)
                    copy_probs(front, 2)
                    exp1(front, 3)
                if b:
                    round_n3(back)
                if f:
                    copy_probs(front, 3)
                if b:
                    gelu(back, 0)
                if f:
                    copy_ctx1(front, 2)
                if b:
                    gelu(back, 2)
                if f:
                    copy_ctx1(front, 3)
                if b:
                    gelu(back, 4)
                if a:
                    copy_n1(ahead)

            act.wait_ge(x_zeroed, 1)
            for j in range(4):
                copy_x(0, j)
            for n, name in enumerate(("g1", "b1", "g2", "b2", "bq", "bk", "bv", "Wr")):
                act.dma_start(vec_rows[n:n + 1], a["L0_ffn_" + name].rearrange("(o e) -> o e", o=1)).then_inc(ld_vecs, 16)
            act.dma_start(b_ff1_rows[:], a["L0_ffn_bf1"].rearrange("(m p) -> m p", p=128)).then_inc(ld_vecs, 16)
            act.dma_start(br_neg[:], a["L0_ffn_br"].rearrange("(o e) -> o e", o=1).broadcast_to([128, 1])).then_inc(ld_vecs, 16)
            copy_n1(0)
            act.wait_ge(ld_qk, LD_QK)
            for n, w in enumerate((w_q, w_k)):
                act.copy(w_qk_hi[:, n], w).then_inc(wqk_hi_ready, 1)
            act.wait_ge(zeroed, 4)
            body(-1)
            with act.Fori(0, RUNS - 2) as i:
                body(i)
            body(RUNS - 2)
            body(RUNS - 1)

        @block.vector
        def _(dve):
            for s in (logits_ready, ctx1_ready, h2_ready, y_ready):
                dve.sem_inc(s.sem, s.per_run)

            def stats(run, src, st, mv, s_st, s_mv):
                for g in range(G):
                    dve.bn_stats(st[:, g], src[:, g]).then_inc(s_st.sem, 1)
                for g in range(G):
                    dve.wait_ge(s_st.sem, s_st.at(run, g + 1))
                    dve.sem_inc(vector_passed, 1)
                    dve.bn_aggr(mv[:, g], st[:, g]).then_inc(s_mv.sem, 1)

            def standardise(dst, src, mv, rstd, done):
                for g in range(G):
                    dve.tensor_scalar(dst[:, g], src[:, g], mv[:, g, 0:1], rstd[:, g:g + 1],
                                      ALU.subtract, ALU.mult).then_inc(done.sem, 1)

            def with_eps(run, ve, mv, s_mv, done):
                dve.wait_ge(s_mv.sem, s_mv.at(run))
                dve.tensor_scalar(ve, mv[:, :, 1], EPS, None, ALU.add).then_inc(done.sem, 1)

            def ln2_stats(run):
                dve.wait_ge(h2_ready.sem, h2_ready.at(run))
                stats(run, h2, stats2, mv2, stats2_done, mv2_done)
                with_eps(run, ve2[:, 0], mv2, mv2_done, ve2_done)
                dve.tensor_scalar(ve2[:, 1], mv2[:, :, 1], 1.0 + EPS, EPS * EPS, ALU.mult, ALU.add).then_inc(ve2_done.sem, 1)

            def ln2_norm(run):
                dve.wait_ge(rstd2_done.sem, rstd2_done.at(run))
                standardise(nn2, h2, mv2, rstd2[:, 1], nn2_ready)

            def ln2_first(run):
                standardise(n2, h2, mv2, rstd2[:, 0], n2_ready)

            def add_pos(run):
                dve.wait_ge(tok_done.sem, tok_done.at(run))
                if type(run) is not int or run > 0:
                    dve.wait_ge(h_kept.sem, h_kept.at(run - 1))
                dve.tensor_tensor(h[:], bank_front[0:GT, 0:G * E].rearrange("p (g e) -> p g e", g=G),
                                  pos_tok[:].unsqueeze(1).broadcast_to([GT, G, E]), ALU.add).then_inc(h_ready.sem, 1)

            def ln1_stats(run):
                dve.wait_ge(h_ready.sem, h_ready.at(run))
                stats(run, h, stats1, mv1, stats1_done, mv1_done)
                with_eps(run, ve1[:], mv1, mv1_done, ve1_done)

            def ln1_norm(run):
                dve.wait_ge(rstd1_done.sem, rstd1_done.at(run))
                standardise(n1, h, mv1, rstd1, n1_ready)

            def split_n1(run):
                dve.wait_ge(n1_copied.sem, n1_copied.at(run))
                dve.tensor_tensor(n1_lo[:], n1_t[:], n1_hi[:].bitcast(F32), ALU.subtract).then_inc(n1_split.sem, 1)

            def gain(run, turned, src_bank, dst, gg, bb, done):
                dve.wait_ge(turned.sem, turned.at(run))
                for k in range(2):
                    dve.tensor_scalar(dst[:, k], src_bank[0:EC, k * RT:(k + 1) * RT], gg[:, k:k + 1], bb[:, k:k + 1],
                                      ALU.mult, ALU.add).then_inc(done.sem, 1)

            def route(run):
                dve.wait_ge(score_exp.sem, score_exp.at(run))
                t = width(run)
                dve.tensor_scalar(score_d[:, 0:t], score_e[:, 0:t], 1.0, None, ALU.add).then_inc(score_step.sem, 1)
                dve.wait_ge(score_step.sem, score_step.at(run, 1))
                dve.reciprocal(score[:, 0:t], score_d[:, 0:t]).then_inc(score_step.sem, 1)
                dve.wait_ge(score_step.sem, score_step.at(run, 2))
                for g in range(G):
                    dve.tensor_tensor_reduce(out=junk[:, g], in0=score[:, cols_of(g)], in1=ident[0:GT, 0:GT], scale=1.0,
                                             scalar=0.0, op0=ALU.mult, op1=ALU.add,
                                             accum_out=score_col[:, g:g + 1]).then_inc(col_done.sem, 1)
                for g in range(G):
                    dve.wait_ge(col_done.sem, col_done.at(run, g + 1))
                    dve.scalar_tensor_tensor(out=less[:, g], in0=score[:, cols_of(g)], scalar=score_col[:, g:g + 1],
                                             in1=cst("same", GT), op0=ALU.is_lt, op1=ALU.mult).then_inc(cmp_done.sem, 1)
                    dve.scalar_tensor_tensor(out=tied[:, g], in0=score[:, cols_of(g)], scalar=score_col[:, g:g + 1],
                                             in1=cst("lower", GT), op0=ALU.is_equal, op1=ALU.mult).then_inc(cmp_done.sem, 1)
                for g in range(G):
                    dve.wait_ge(cmp_done.sem, cmp_done.at(run, 2 * g + 2))
                    dve.sem_inc(vector_passed, 1)
                    dve.tensor_tensor_reduce(out=junk[:, g], in0=less[:, g], in1=tied[:, g], scale=1.0, scalar=0.0,
                                             op0=ALU.add, op1=ALU.add, accum_out=rank[:, g:g + 1]).then_inc(rank_done.sem, 1)
                for g in range(G):
                    dve.wait_ge(rank_done.sem, rank_done.at(run, g + 1))
                    dve.tensor_scalar(sel[:, g, g * GS:(g + 1) * GS], cst("slot", GT), rank[:, g:g + 1], None,
                                      ALU.is_equal).then_inc(sel_ready.sem, 1)
                    dve.tensor_scalar(unrouted[:, g:g + 1], rank[:, g:g + 1], float(SEL), None,
                                      ALU.is_ge).then_inc(unrouted_ready.sem, 1)

                dve.tensor_reduce(s_sum[:], score[0:EC].rearrange("p (b t) -> p b t", t=TOK), AX_X, ALU.add).then_inc(sum_step.sem, 1)
                dve.wait_ge(sum_step.sem, sum_step.at(run, 1))
                dve.tensor_scalar(s_eps[:], s_sum[:], 1e-6, None, ALU.add).then_inc(sum_step.sem, 1)
                dve.wait_ge(sum_step.sem, sum_step.at(run, 2))
                dve.reciprocal(s_inv[:], s_eps[:]).then_inc(sum_step.sem, 1)

            def pool_scores(run):
                dve.wait_ge(weighted_done.sem, weighted_done.at(run))
                dve.tensor_reduce(pooled[:].rearrange("p k b -> p (k b)"), weighted[:].rearrange("p k (b t) -> p (k b) t", t=TOK),
                                  AX_X, ALU.add).then_inc(pool_step.sem, 1)
                dve.wait_ge(pool_step.sem, pool_step.at(run, 1))
                dve.wait_ge(sum_step.sem, sum_step.at(run))
                dve.tensor_tensor(pooled_n[:], pooled[:], s_inv[:].unsqueeze(1).broadcast_to([EC, 2, RB]),
                                  ALU.mult).then_inc(pool_step.sem, 1)

            def split_x(run):
                dve.wait_ge(x_loaded, (run + 1) * 16 * CHANNELS)
                if type(run) is not int or run > 0:
                    dve.wait_ge(x_turned.sem, x_turned.at(run - 1))
                dve.tensor_copy(x_split[:].rearrange("p w (a b) -> p w a b", b=PATCH),
                                x_rows[:].rearrange("p a w b -> p w a b")).then_inc(x_split_done.sem, 1)

            def copy_sel(run):
                gain_src = bank_back[1]
                dve.wait_ge(gather_done.sem, gather_done.at(run))
                for k in range(2):
                    dve.tensor_scalar(nsel_t[:, k], gain_src[0:EC, k * RS:(k + 1) * RS], g1[:, k:k + 1], b1[:, k:k + 1],
                                      ALU.mult, ALU.add).then_inc(nsel_ready.sem, 1)
                dve.tensor_copy(sel_t[:].rearrange("p g t -> p (g t)"), gain_src[0:RS, 128:128 + RT]).then_inc(selt_copied.sem, 1)

            def q2_by_head(run):
                dve.wait_ge(q2_copied.sem, q2_copied.at(run))
                for k in range(2):
                    dve.tensor_tensor(q2_heads[:, k],
                                      q2_t[:, k].rearrange("p (g q) -> p g q", g=G).unsqueeze(2).broadcast_to([EC, G, HC, GS]),
                                      cst("headmask", EC).unsqueeze(1).unsqueeze(3).broadcast_to([EC, G, HC, GS]),
                                      ALU.mult).then_inc(q2h_ready.sem, 1)

            def logits_2(run):
                dve.wait_ge(s2_done.sem, s2_done.at(run))
                dve.scalar_tensor_tensor(out=logits2[:], in0=bank_back[1][0:HC * GS, 0:4 * GT].rearrange("p (j t) -> p j t", j=4),
                                         scalar=float(D2) ** -0.5,
                                         in1=cst("apart2", HC * GS).unsqueeze(1).broadcast_to([HC * GS, 4, GT]),
                                         op0=ALU.mult, op1=ALU.add).then_inc(logits2_ready.sem, 1)
                dve.wait_ge(logits2_ready.sem, logits2_ready.at(run))
                dve.tensor_reduce(negmax2[:], logits2[:], AX_X, ALU.max, negate=True).then_inc(max2_done.sem, 1)

            def softmax_2(run):
                dve.wait_ge(exp2_done.sem, exp2_done.at(run))
                dve.reciprocal(den2_inv[:], den2[:]).then_inc(den2_done.sem, 1)
                dve.wait_ge(den2_done.sem, den2_done.at(run))
                dve.tensor_tensor(probs2[:], exp2[:], den2_inv[:].unsqueeze(2).broadcast_to([HC * GS, 4, GT]),
                                  ALU.mult).then_inc(probs2_ready.sem, 1)

            def own_ctx2(run):
                dve.wait_ge(pv2_done.sem, pv2_done.at(run))
                dve.tensor_tensor(own[:], bank_back[1][0:EC, 0:4 * HC * GS].rearrange("p (j h q) -> p j h q", j=4, h=HC),
                                  cst("headmask", EC).unsqueeze(1).unsqueeze(3).broadcast_to([EC, 4, HC, GS]),
                                  ALU.mult).then_inc(own_done.sem, 1)
                dve.wait_ge(own_done.sem, own_done.at(run))
                dve.tensor_reduce(ctx2[:], own[:].rearrange("p j h q -> p j q h"), AX_X, ALU.add).then_inc(ctx2_done.sem, 1)
                dve.wait_ge(ctx2_done.sem, ctx2_done.at(run))
                dve.tensor_tensor(ctx2_t[0:EC], ctx2[:].rearrange("p (k g) q -> p k (g q)", k=2),
                                  bv.unsqueeze(2).broadcast_to([EC, 2, RS]), ALU.add).then_inc(ctx2_ready.sem, 1)

            def split_w_ff1(run):
                if type(run) is int and run == 0:
                    dve.wait_ge(ld_ff1, 16)
                    dve.tensor_copy(w_ff1_hi[:], w_ff1[:]).then_inc(wff1_split, 1)
                    dve.wait_ge(wff1_split, 1)
                    dve.tensor_tensor(w_ff1_lo[:], w_ff1[:], w_ff1_hi[:].bitcast(F32), ALU.subtract).then_inc(wff1_split, 1)

            def softmax1(run, u):
                quad, g = UNIT[u]
                if type(run) is int and (run, u) == (0, 0):
                    dve.wait_ge(bias_placed, 16 * GB)
                dve.wait_ge(score_done.sem, score_done.at(run, u + 1))
                dve.scalar_tensor_tensor(out=logits[:, u % 2].rearrange("p h t -> p (h t)"), in0=bank_score[0:GT, 0:QUAD * GT],
                                         scalar=float(D1) ** -0.5,
                                         in1=pos_bias[:, quad * QUAD:(quad + 1) * QUAD].rearrange("p h t -> p (h t)"),
                                         op0=ALU.mult, op1=ALU.add).then_inc(logits_ready.sem, 1)
                dve.wait_ge(logits_ready.sem, logits_ready.at(run, u + 1))
                dve.tensor_reduce(rowmax[:, u % 2], logits[:, u % 2], AX_X, ALU.max).then_inc(rowmax_done.sem, 1)

            def normalise1(run, u):
                quad, g = UNIT[u]
                pv = bank_pv[0:GT, 0:QUAD * (D1 + 1)].rearrange("p (h d) -> p h d", h=QUAD)
                dve.wait_ge(pv_done.sem, pv_done.at(run, u + 1))
                dve.reciprocal(den_inv[:, u], pv[:, :, D1]).then_inc(den_done.sem, 1)
                dve.wait_ge(den_done.sem, den_done.at(run, u + 1))
                dve.tensor_tensor(ctx1[:, g, quad * QUAD:(quad + 1) * QUAD], pv[:, :, 0:D1],
                                  den_inv[:, u].unsqueeze(2).broadcast_to([GT, QUAD, D1]), ALU.mult).then_inc(ctx1_ready.sem, 1)

            def ln2_gain(run):
                gain(run, n2_turned, bank_back[1], n2_t, g1, b1, n2t_ready)

            def residual1(run):
                dve.wait_ge(wo_done.sem, wo_done.at(run))
                dve.wait_ge(h_kept.sem, h_kept.at(run))
                dve.tensor_tensor(h2[:].rearrange("p g e -> p (g e)"), bank_front[0:GT, 0:G * E],
                                  h_keep[:].rearrange("p g e -> p (g e)"), ALU.add).then_inc(h2_ready.sem, 1)

            def merge(run):
                dve.wait_ge(n2_ready.sem, n2_ready.at(run))
                dve.wait_ge(mix_done.sem, mix_done.at(run))
                for g in range(G):
                    dve.scalar_tensor_tensor(out=mixed[:, g], in0=bank_back[0][0:GT, g * E:(g + 1) * E], scalar=unrouted[:, g:g + 1],
                                             in1=n2[:, g], op0=ALU.mult, op1=ALU.add).then_inc(mixed_done.sem, 1)

            def residual2(run):
                dve.wait_ge(scat_done.sem, scat_done.at(run))
                dve.wait_ge(mixed_done.sem, mixed_done.at(run))
                dve.tensor_tensor(h3[:].rearrange("p g e -> p (g e)"), bank_back[1][0:GT, 0:G * E],
                                  mixed[:].rearrange("p g e -> p (g e)"), ALU.add).then_inc(h3_ready.sem, 1)
                dve.wait_ge(h3_ready.sem, h3_ready.at(run))
                stats(run, h3, stats3, mv3, stats3_done, mv3_done)
                with_eps(run, ve3[:], mv3, mv3_done, ve3_done)

            def ln3_norm(run):
                dve.wait_ge(rstd3_done.sem, rstd3_done.at(run))
                standardise(n3, h3, mv3, rstd3, n3_ready)

            def ln3_gain(run):
                gain(run, n3_turned, bank_back[0], n3_t, g2, b2, n3t_ready)
                for k in range(2):
                    dve.wait_ge(n3_rounded.sem, n3_rounded.at(run, k + 1))
                    dve.tensor_tensor(n3_lo[:, k], n3_t[:, k], n3_hi[:, k].bitcast(F32), ALU.subtract).then_inc(n3_split.sem, 1)

            def residual3(run):
                dve.wait_ge(ff2_done.sem, ff2_done.at(run))
                dve.wait_ge(h3b_ready.sem, h3b_ready.at(run))
                dve.wait_ge(y_stored.sem, y_stored.before(run))
                dve.tensor_tensor(y[:].rearrange("p g e -> p (g e)"), bank_back[0][0:GT, 0:G * E],
                                  h3_b[:].rearrange("p g e -> p (g e)"), ALU.add).then_inc(y_ready.sem, 1)

            def body(i):
                back, front, ahead = i, i + 1, i + 2
                b, f, a = exists(back), exists(front), exists(ahead)
                if b:
                    ln2_gain(back)
                if a:
                    split_x(ahead)
                if b:
                    ln2_first(back)
                    route(back)
                    pool_scores(back)
                    copy_sel(back)
                if f:
                    split_w_ff1(front)
                    softmax1(front, 0)
                if b:
                    q2_by_head(back)
                if f:
                    softmax1(front, 1)
                if b:
                    logits_2(back)
                    softmax_2(back)
                if f:
                    normalise1(front, 0)
                if b:
                    own_ctx2(back)
                if f:
                    normalise1(front, 1)
                if b:
                    merge(back)
                if f:
                    softmax1(front, 2)
                if b:
                    residual2(back)
                if f:
                    softmax1(front, 3)
                if b:
                    ln3_norm(back)
                    ln3_gain(back)
                if f:
                    normalise1(front, 2)
                if a:
                    add_pos(ahead)
                    ln1_stats(ahead)
                    ln1_norm(ahead)
                if f:
                    normalise1(front, 3)
                    residual1(front)
                    ln2_stats(front)
                if a:
                    split_n1(ahead)
                if f:
                    ln2_norm(front)
                if b:
                    residual3(back)

            split_x(0)
            for j in range(PC // 2):
                dve.wait_ge(wt_turned, j + 1)
                dve.tensor_copy(w_tok[:, 2 * j:2 * j + 2, :].rearrange("p c e -> p (c e)"),
                                bank_proj[j % 2][:, 0:2 * E]).then_inc(wt_copied, 1)
            dve.wait_ge(ld_pos, LD_POS)
            dve.tensor_tensor(pos_tok[:], pos_tok[:], b_tok[:], ALU.add).then_inc(pos_ready, 1)
            dve.wait_ge(ld_rel, 16)
            dve.tensor_reduce(rel_sum[:], rel, AX_X, ALU.add).then_inc(rel_summed, 1)
            dve.wait_ge(ld_v, 16 * 2)
            dve.tensor_copy(w_v_hi[:], w_v[:]).then_inc(wv_split, 1)
            dve.wait_ge(wv_split, 1)
            dve.tensor_tensor(w_v_lo[:], w_v[:], w_v_hi[:].bitcast(F32), ALU.subtract).then_inc(wv_split, 1)
            dve.wait_ge(rel_turned, 1)
            turned = bank_score[0:H1, TOK - 1:TOK]
            dve.tensor_copy(rel_bias, bass.AP(tensor=turned.tensor, offset=turned.offset,
                                                 ap=[turned.ap[0], [-1, TOK], [1, TOK]])).then_inc(rel_spread, 1)
            dve.wait_ge(pos_ready, 1)
            add_pos(0)
            ln1_stats(0)
            ln1_norm(0)
            split_n1(0)
            dve.wait_ge(cols_turned, 1)
            dve.tensor_copy(cols[:].rearrange("p n k -> p k n"),
                            bank_turn[0:EC, 0:16].rearrange("p (k n) -> p k n", k=2)).then_inc(cols_ready, 1)
            dve.tensor_copy(b_ff1[:], bank_turn[:, 16:16 + FC]).then_inc(cols_ready, 1)
            dve.tensor_scalar(br_neg[:], br_neg[:], -1.0, None, ALU.mult).then_inc(wr_ready, 1)
            dve.wait_ge(cols_ready, 2)
            dve.tensor_copy(w_k2[:, :, :, EC:128], wr.unsqueeze(2).unsqueeze(3).broadcast_to([EC, 2, 2, 128 - EC])).then_inc(wr_ready, 1)
            dve.wait_ge(wr_ready, 2)
            for n, w in enumerate((w_q, w_k)):
                dve.wait_ge(wqk_hi_ready, n + 1)
                dve.tensor_tensor(w_qk_lo[:, n], w, w_qk_hi[:, n].bitcast(F32), ALU.subtract).then_inc(wqk_split, 1)
            body(-1)
            with dve.Fori(0, RUNS - 2) as i:
                body(i)
            body(RUNS - 2)
            body(RUNS - 1)

        @block.tensor
        def _(pe):
            def turn_x(run, j):
                hf, tri = j // 2, j % 2
                if j == 0:
                    pe.wait_ge(x_split_done.sem, x_split_done.at(run))
                    if type(run) is not int or run > 1:
                        pe.wait_ge(h2_ready.sem, h2_ready.at(run - 2))
                    elif run == 1:
                        pe.wait_ge(h_ready.sem, h_ready.at(0))
                else:
                    pe.wait_ge(x_copied.sem, x_copied.at(run, CHANNELS * j))
                for n in range(TW):
                    mm = pe.transpose(bank_front[:, n * XP:(n + 1) * XP],
                                      x_split[:, tri * TW + n, hf * 128:(hf + 1) * 128], ident[0:XP, 0:XP])
                mm.then_inc(x_turned.sem, 1)

            def tokens(run, first, last):
                if first == 0:
                    pe.wait_ge(x_copied.sem, x_copied.at(run))
                for n in range(first, last):
                    g, c = n // PC, n % PC
                    mm = pe.matmul(bank_front[0:GT, g * E:(g + 1) * E], x_t[:, c, cols_of(g)], w_tok[:, c, :],
                                   start=(c == 0), stop=(c == PC - 1))
                if last == G * PC:
                    mm.then_inc(tok_done.sem, 1)

            def turn_tokens(src, dst_bank, done):
                for k in range(2):
                    for g in range(G):
                        mm = pe.transpose(dst_bank[0:EC, k * RT + g * GT:k * RT + (g + 1) * GT], src[:, g, half(k)],
                                          ident[0:GT, 0:GT])
                mm.then_inc(done.sem, 1)

            def turn_n1(run):
                pe.wait_ge(n1_ready.sem, n1_ready.at(run))
                turn_tokens(n1, bank_proj[0], n1_turned)

            def values(run, j):
                g, part = j // 2, j % 2
                if j == 0:
                    pe.wait_ge(n1_copied.sem, n1_copied.at(run))
                if j < 2:
                    pe.wait_ge(qk_copied.sem, qk_copied.at(run - 1, 2 * (CHUNKS - 1 + j)))
                else:
                    pe.wait_ge(v_copied.sem, v_copied.at(run, j - 1))
                products = [(n1_hi, w_v_hi), (n1_hi, w_v_lo), (n1_lo, w_v_hi)]
                for n, (lhs, w) in enumerate(products):
                    if j == 0 and n == 2:
                        pe.wait_ge(n1_split.sem, n1_split.at(run))
                    for k in range(2):
                        mm = pe.matmul(bank_proj[j % 2][0:GT, 0:QUAD * D1], lhs[:, k, cols_of(g)],
                                       w[:, k, part * QUAD * D1:(part + 1) * QUAD * D1],
                                       start=(n == 0 and k == 0), stop=(n == 2 and k == 1))
                mm.then_inc(v_done.sem, 1)

            def queries_keys(run, j):
                if type(run) is int and (run, j) == (0, 0):
                    pe.wait_ge(wqk_split, 2)
                if j < 2:
                    pe.wait_ge(v_copied.sem, v_copied.at(run, 3 + j))
                else:
                    pe.wait_ge(qk_copied.sem, qk_copied.at(run, 2 * (j - 1)))
                t = width(run)
                for n in range(2):
                    for p, (w, x) in enumerate(((w_qk_hi, n1_hi), (w_qk_lo, n1_hi), (w_qk_hi, n1_lo))):
                        for k in range(2):
                            mm = pe.matmul(bank_proj[j % 2][:, n * RT:n * RT + t], w[:, n, k, j, :], x[:, k, 0:t],
                                           start=(p == 0 and k == 0), stop=(p == 2 and k == 1))
                mm.then_inc(qk_done.sem, 1)

            def scores(run, u):
                quad, g = UNIT[u]
                pe.wait_ge(qk_copied.sem, qk_copied.at(run, 2 * QCH * (quad + 1)))
                pe.wait_ge(logits_ready.sem, logits_ready.at(run, u))
                for n in range(QUAD):
                    hd = quad * QUAD + n
                    mm = pe.matmul(bank_score[0:GT, n * GT:(n + 1) * GT], qk[:, hd, 0, cols_of(g)], qk[:, hd, 1, cols_of(g)],
                                   start=True, stop=True)
                mm.then_inc(score_done.sem, 1)

            def turn_probs(run, u):
                freed, value = [(ctx1_copied, 0), (probs_copied, 1), (ctx1_copied, 2), (probs_copied, 3)][u]
                pe.wait_ge(probs_ready.sem, probs_ready.at(run, u + 1))
                pe.wait_ge(freed.sem, freed.at(run, value))
                for n in range(QUAD):
                    mm = pe.transpose(bank_turn[0:GT, n * GT:(n + 1) * GT], probs[:, u % 2, n], ident[0:GT, 0:GT])
                mm.then_inc(probs_turned.sem, 1)

            def probs_values(run, u):
                quad, g = UNIT[u]
                pe.wait_ge(probs_copied.sem, probs_copied.at(run, u + 1))
                pe.wait_ge(ctx1_ready.sem, ctx1_ready.at(run, u))
                for n in range(QUAD):
                    mm = pe.matmul(bank_pv[0:GT, n * (D1 + 1):(n + 1) * (D1 + 1)], probs_t[:, u % 2, n],
                                   v[:, g, quad * QUAD + n], start=True, stop=True)
                mm.then_inc(pv_done.sem, 1)

            def turn_ctx1(run, u):
                freed, value = [(probs_copied, 2), (ctx1_copied, 1), (probs_copied, 4), (ctx1_copied, 3)][u]
                quad, g = UNIT[u]
                pe.wait_ge(ctx1_ready.sem, ctx1_ready.at(run, u + 1))
                pe.wait_ge(freed.sem, freed.at(run, value))
                rows = ctx1[:, g].rearrange("p h d -> p (h d)")
                for n in range(3):
                    c = 3 * quad + n
                    mm = pe.transpose(bank_turn[:, n * GT:(n + 1) * GT], rows[:, c * 128:(c + 1) * 128], ident[0:GT, 0:GT])
                mm.then_inc(ctx1_turned.sem, 1)

            def project1(run, g):
                if type(run) is int and (run, g) == (0, 0):
                    pe.wait_ge(ld_wo, 16)
                pe.wait_ge(ctx1_copied.sem, ctx1_copied.at(run, UNITS - G + g + 1))
                if g == 0 and exists(run + 1):
                    pe.wait_ge(h_ready.sem, h_ready.at(run + 1))
                for c in range(FC):
                    mm = pe.matmul(bank_front[0:GT, g * E:(g + 1) * E], ctx1_t[:, c, cols_of(g)], w_o[:, c, :],
                                   start=(c == 0), stop=(c == FC - 1))
                if g == G - 1:
                    mm.then_inc(wo_done.sem, 1)

            def turn_n2(run):
                pe.wait_ge(nn2_ready.sem, nn2_ready.at(run))
                turn_tokens(nn2, bank_back[1], n2_turned)

            def keys2(run):
                pe.wait_ge(n2t_ready.sem, n2t_ready.at(run))
                pe.wait_ge(y_ready.sem, y_ready.before(run))
                for m, done in enumerate((z_done, k2_done)):
                    for k in range(2):
                        mm = pe.matmul(bank_back[m][:, 0:width(run)], w_k2[:, k, m], n2_t[:, k, 0:width(run)],
                                       start=(k == 0), stop=(k == 1))
                    mm.then_inc(done.sem, 1)

            def values2(run):
                pe.wait_ge(q2_copied.sem, q2_copied.at(run))
                for g in range(G):
                    for k in range(2):
                        mm = pe.matmul(bank_back[0][0:GT, g * E:(g + 1) * E], n2_t[:, k, cols_of(g)], w_v2[:, k, :],
                                       start=(k == 0), stop=(k == 1))
                mm.then_inc(v2_done.sem, 1)

            def gather(run):
                pe.wait_ge(sel_ready.sem, sel_ready.at(run))
                pe.wait_ge(k2_copied.sem, k2_copied.at(run))
                for k in range(2):
                    for g in range(G):
                        pe.matmul(bank_back[1][0:EC, k * RS:(k + 1) * RS], nn2[:, g, half(k)], sel[:, g],
                                  start=(g == 0), stop=(g == G - 1))
                for g in range(G):
                    mm = pe.transpose(bank_back[1][0:RS, 128 + g * GT:128 + (g + 1) * GT], sel[:, g], ident[0:GT, 0:GT])
                mm.then_inc(gather_done.sem, 1)

            def queries2(run):
                pe.wait_ge(nsel_ready.sem, nsel_ready.at(run))
                pe.wait_ge(k2_copied.sem, k2_copied.at(run))
                for m in range(2):
                    for k in range(2):
                        mm = pe.matmul(bank_back[0][0:EC, m * RS:(m + 1) * RS], w_q2[:, k, half(m)], nsel_t[:, k],
                                       start=(k == 0), stop=(k == 1))
                mm.then_inc(q2_done.sem, 1)

            def scores2(run):
                pe.wait_ge(q2h_ready.sem, q2h_ready.at(run))
                pe.wait_ge(k2_copied.sem, k2_copied.at(run))
                pe.wait_ge(selt_copied.sem, selt_copied.at(run))
                for k in range(2):
                    for g in range(G):
                        j = k * G + g
                        mm = pe.matmul(bank_back[1][0:HC * GS, j * GT:(j + 1) * GT],
                                       q2_heads[:, k, g].rearrange("p h q -> p (h q)"), k2_t[:, k, cols_of(g)],
                                       start=True, stop=True)
                mm.then_inc(s2_done.sem, 1)

            def turn_probs2(run):
                pe.wait_ge(probs2_ready.sem, probs2_ready.at(run))
                pe.wait_ge(v2_copied.sem, v2_copied.at(run))
                n = HC * GS
                for j in range(4):
                    mm = pe.transpose(bank_back[0][0:GT, j * n:(j + 1) * n], probs2[:, j], ident[0:n, 0:n])
                mm.then_inc(p2_turned.sem, 1)

            def probs_values2(run):
                pe.wait_ge(p2_copied.sem, p2_copied.at(run))
                pe.wait_ge(logits2_ready.sem, logits2_ready.at(run))
                n = HC * GS
                for k in range(2):
                    for g in range(G):
                        j = k * G + g
                        mm = pe.matmul(bank_back[1][0:EC, j * n:(j + 1) * n], v2[:, g, half(k)], probs2_t[:, j],
                                       start=True, stop=True)
                mm.then_inc(pv2_done.sem, 1)

            def with_bias(out, lhs, w, n):
                pe.matmul(out, lhs[0:EC, 0, n], w[0:EC, 0, :], start=True, stop=False)
                return pe.matmul(out, lhs[:, 1, n], w[:, 1, :], start=False, stop=True)

            def project2(run):
                pe.wait_ge(ctx2_ready.sem, ctx2_ready.at(run))
                pe.wait_ge(own_done.sem, own_done.at(run))
                with_bias(bank_back[1][0:RS, 0:E], ctx2_t, w_o2, slice(0, RS)).then_inc(ao_done.sem, 1)

            def mix_project(run):
                pe.wait_ge(mix_step.sem, mix_step.at(run))
                pe.wait_ge(p2_copied.sem, p2_copied.at(run))
                for g in range(G):
                    mm = with_bias(bank_back[0][0:GT, g * E:(g + 1) * E], mix_t, w_m, cols_of(g))
                mm.then_inc(mix_done.sem, 1)

            def scatter(run):
                pe.wait_ge(attn2_copied.sem, attn2_copied.at(run))
                for g in range(G):
                    mm = pe.matmul(bank_back[1][0:GT, g * E:(g + 1) * E], sel_t[:, g], attn2[:], start=True, stop=True)
                mm.then_inc(scat_done.sem, 1)

            def turn_n3(run):
                pe.wait_ge(n3_ready.sem, n3_ready.at(run))
                turn_tokens(n3, bank_back[0], n3_turned)

            def ff1(run, j):
                if j == 2:
                    pe.wait_ge(gelu_done.sem, gelu_done.at(run, 2))
                t = width(run)
                for n in range(2):
                    m = 2 * j + n
                    first = (j, n) == (0, 0)
                    for p, (w, x, k) in enumerate(((w_ff1_hi, n3_hi, 0), (w_ff1_lo, n3_hi, 0), (w_ff1_hi, n3_hi, 1),
                                                   (w_ff1_lo, n3_hi, 1), (w_ff1_hi, n3_lo, 0), (w_ff1_hi, n3_lo, 1))):
                        if first and p in (0, 2):
                            pe.wait_ge(n3_rounded.sem, n3_rounded.at(run, k + 1))
                        if first and p in (4, 5):
                            pe.wait_ge(n3_split.sem, n3_split.at(run, k + 1))
                        mm = pe.matmul(bank_back[(j + 1) % 2][:, n * RT:n * RT + t], w[:, k, m * 128:(m + 1) * 128],
                                       x[:, k, 0:t], start=(p == 0), stop=(p == 5))
                mm.then_inc(ff1_done.sem, 1)

            def ff2(run):
                pe.wait_ge(gelu_done.sem, gelu_done.at(run, 6))
                for g in range(G):
                    for m in range(FC):
                        mm = pe.matmul(bank_back[0][0:GT, g * E:(g + 1) * E], ff_t[:, m, cols_of(g)], w_ff2[:, m, :],
                                       start=(m == 0), stop=(m == FC - 1))
                mm.then_inc(ff2_done.sem, 1)

            def body(i):
                back, front, ahead = i, i + 1, i + 2
                b, f, a = exists(back), exists(front), exists(ahead)
                if f:
                    values(front, 0)
                if b:
                    turn_n2(back)
                if f:
                    values(front, 1)
                if b:
                    keys2(back)
                if f:
                    values(front, 2)
                    values(front, 3)
                if a:
                    turn_x(ahead, 0)
                if f:
                    queries_keys(front, 0)
                if a:
                    turn_x(ahead, 1)
                if f:
                    queries_keys(front, 1)
                    queries_keys(front, 2)
                if b:
                    gather(back)
                if a:
                    turn_x(ahead, 2)
                if f:
                    queries_keys(front, 3)
                    scores(front, 0)
                if b:
                    queries2(back)
                if a:
                    turn_x(ahead, 3)
                if f:
                    queries_keys(front, 4)
                    scores(front, 1)
                if b:
                    scores2(back)
                if f:
                    turn_probs(front, 0)
                if b:
                    values2(back)
                if f:
                    queries_keys(front, 5)
                    probs_values(front, 0)
                    turn_probs(front, 1)
                if a:
                    tokens(ahead, 0,1)
                if b:
                    turn_probs2(back)
                if a:
                    tokens(ahead, 1,3)
                if b:
                    probs_values2(back)
                if f:
                    probs_values(front, 1)
                if b:
                    mix_project(back)
                if f:
                    scores(front, 2)
                    turn_ctx1(front, 0)
                if b:
                    project2(back)
                if f:
                    turn_ctx1(front, 1)
                if a:
                    tokens(ahead, 3,4)
                if b:
                    scatter(back)
                if f:
                    scores(front, 3)
                if a:
                    tokens(ahead, 4,9)
                if f:
                    turn_probs(front, 2)
                if a:
                    tokens(ahead, 9,12)
                if b:
                    turn_n3(back)
                if f:
                    probs_values(front, 2)
                    turn_probs(front, 3)
                if b:
                    ff1(back, 0)
                    ff1(back, 1)
                if f:
                    turn_ctx1(front, 2)
                    probs_values(front, 3)
                    project1(front, 0)
                    turn_ctx1(front, 3)
                if b:
                    ff1(back, 2)
                if f:
                    project1(front, 1)
                if a:
                    turn_n1(ahead)
                if b:
                    ff2(back)

            def turn_w(j):
                if j >= 2:
                    pe.wait_ge(wt_copied, j - 1)
                for n in range(2):
                    for k in range(2):
                        mm = pe.transpose(bank_proj[j % 2][:, n * E + k * EC:n * E + (k + 1) * EC],
                                          w_raw[:, k, (2 * j + n) * 128:(2 * j + n + 1) * 128], ident[0:EC, 0:EC])
                mm.then_inc(wt_turned, 1)

            pe.wait_ge(ld_const, 16)
            turn_x(0, 0)
            pe.wait_ge(ld_w, 16)
            turn_w(0)
            turn_x(0, 1)
            turn_w(1)
            turn_x(0, 2)
            turn_w(2)
            turn_x(0, 3)
            pe.wait_ge(rel_summed, 1)
            pe.transpose(bank_score[0:H1, 0:REL], rel_sum[:], ident[0:REL, 0:REL]).then_inc(rel_turned, 1)
            pe.wait_ge(wt_copied, PC // 2)
            tokens(0, 0, G * PC)
            turn_n1(0)
            pe.wait_ge(ld_vecs, LD_VECS)
            for k in range(2):
                pe.transpose(bank_turn[0:EC, k * 8:(k + 1) * 8], vec_rows[:, half(k)], ident[0:8, 0:8])
            pe.transpose(bank_turn[:, 16:16 + FC], b_ff1_rows[:], ident[0:FC, 0:FC]).then_inc(cols_turned, 1)
            pe.wait_ge(wv_split, 2)
            pe.wait_ge(zeroed, 4)
            body(-1)
            pe.wait_ge(wr_ready, 2)
            pe.wait_ge(ld_back, LD_BACK)
            pe.wait_ge(wff1_split, 2)
            with pe.Fori(0, RUNS - 2) as i:
                body(i)
            body(RUNS - 2)
            body(RUNS - 1)


LD_POS = 16 * 3 * GB
LD_VECS = 16 * 10
LD_QK = 16 * 2 * 2 * (H1 // QUAD) * 2
LD_BACK = 16 * (7 + 3)


def constants():
    import numpy as np

    c = np.zeros((128, CONST_COLS), np.float32)

    def put(name, x):
        lo, hi = CONST[name]
        c[0:x.shape[0], lo:hi] = x

    t = np.arange(GT)
    same = t[:, None] // TOK == t[None, :] // TOK
    put("ident", np.eye(128, dtype=np.float32))
    put("same", same.astype(np.float32))
    put("lower", (same & (t[None, :] < t[:, None])).astype(np.float32))
    s = np.arange(GS)
    put("slot", np.where(t[:, None] // TOK == s[None, :] // SEL, s[None, :] % SEL, -1).astype(np.float32))
    put("headmask", (np.arange(EC)[:, None] // D2 == np.arange(HC)[None, :]).astype(np.float32))
    q = np.arange(HC * GS) % GS
    put("apart2", np.where(q[:, None] // SEL == t[None, :] // TOK, 0.0, NEG).astype(np.float32))
    return c


_INS = ["x", "cls_tok", "L0_tok_W", "L0_tok_b", "L0_tok_pos_embed", "L0_attn_w_q", "L0_attn_w_k", "L0_attn_w_v",
        "L0_attn_w_o", "L0_attn_rel_emb"] + ["L0_ffn_" + n for n in (
            "g1", "b1", "g2", "b2", "Wr", "br", "Wq", "bq", "Wk", "bk", "Wv", "bv", "Wo", "bo", "Wm", "bm", "W1", "bf1",
            "W2", "bf2")]


def kernel(**inputs):
    import numpy as _np
    import concourse.bacc as _bacc
    from concourse import mybir as _mybir
    from concourse.bass_utils import run_bass_kernel_spmd as _run

    nc = _bacc.Bacc("TRN2", target_bir_lowering=False, num_devices=1)
    arrays, aps = {}, {}
    for name in _INS + ["consts"]:
        v = constants() if name == "consts" else _np.ascontiguousarray(inputs[name])
        if v.ndim == 0:
            v = v.reshape(1)
        arrays[f"in_{name}_dram"] = v
        aps[name] = nc.dram_tensor(f"in_{name}_dram", v.shape, _mybir.dt.from_np(v.dtype), kind="ExternalInput").ap()
    aps["out"] = nc.dram_tensor("out_0_dram", (BATCH, TOK, E), F32, kind="ExternalOutput").ap()
    aps["bias_scratch"] = nc.dram_tensor("bias_scratch", (H1, TOK, TOK), F32, kind="Internal").ap()
    vit_block(nc, aps)
    r = _run(nc, [arrays], core_ids=[0])
    return r.results[0]["out_0_dram"]
```
